# Optimizing a Trainium2 kernel written in Bass

```python
import numpy as np
import jax
import jax.numpy as jnp

def _softmax(x, axis=-1):
    return jax.nn.softmax(x, axis=axis)

def _gelu(x):
    return jax.nn.gelu(x, approximate=True)

def _silu(x):
    return jax.nn.silu(x)

def _sigmoid(x):
    return jax.nn.sigmoid(x)

def _layernorm(x, axis=-1, eps=1e-05):
    m = jnp.mean(x, axis=axis, keepdims=True)
    v = jnp.var(x, axis=axis, keepdims=True)
    return (x - m) / jnp.sqrt(v + eps)

def _scatter_add(tgt, idx, src, axis=0):
    return tgt.at[idx].add(src)

def _segment_sum(src, seg, n):
    return jax.ops.segment_sum(src, seg, n)
kernel_name = 'mk_seq_preln_d2_jaxref_r8_292f5e'

def setup_inputs(seed: int=0):
    np.random.seed(seed)
    _w = jnp.asarray

    def _L0_attn_setup():
        import jax, jax.numpy as jnp
        import numpy as np
        NUM_HEADS = 16
        EPS = 1e-12

        def _l2norm(t):
            n = jnp.sqrt(jnp.sum(t * t, axis=-1, keepdims=True))
            return t / jnp.maximum(n, EPS)
        key = jax.random.key(seed)
        kx, kq, kk, kv = jax.random.split(key, 4)
        B, S, E = (2, 256, 128)
        head_dim = E // NUM_HEADS
        bound = 1.0 / np.sqrt(E)
        x = jax.random.normal(kx, (B, S, E), dtype=jnp.float32)
        Wq = jax.random.uniform(kq, (E, E), dtype=jnp.float32, minval=-bound, maxval=bound)
        Wk = jax.random.uniform(kk, (E, E), dtype=jnp.float32, minval=-bound, maxval=bound)
        Wv = jax.random.uniform(kv, (E, E), dtype=jnp.float32, minval=-bound, maxval=bound)
        g_scale = jnp.asarray(np.sqrt(head_dim), dtype=jnp.float32)
        return {'x': x, 'Wq': Wq, 'Wk': Wk, 'Wv': Wv, 'g_scale': g_scale}
    _L0_attn_in = _L0_attn_setup()

    def _L0_ffn_setup():
        import jax, jax.numpy as jnp
        import numpy as np
        B, T, D, E, H = (8, 256, 128, 8, 32)
        LN_EPS = 1e-05
        key = jax.random.key(seed)
        ks = jax.random.split(key, 4)
        return {'x': jax.random.normal(ks[0], (B, T, D), dtype=jnp.float32), 'Wg': jax.random.normal(ks[1], (E, D), dtype=jnp.float32) * 0.02, 'ln_scale': jnp.ones((E, D), dtype=jnp.float32), 'ln_bias': jnp.zeros((E, D), dtype=jnp.float32), 'W1': jax.random.normal(ks[2], (E, D, H), dtype=jnp.float32) * 0.02, 'b1': jnp.zeros((E, H), dtype=jnp.float32), 'W2': jax.random.normal(ks[3], (E, H, D), dtype=jnp.float32) * 0.02, 'b2': jnp.zeros((E, D), dtype=jnp.float32)}
    _L0_ffn_in = _L0_ffn_setup()

    def _L1_attn_setup():
        import jax, jax.numpy as jnp
        import numpy as np
        import math
        B, T, C = (4, 256, 128)
        H, DQK, DV = (16, 64, 64)
        key = jax.random.key(seed)
        k1, k2, k3, k4, k5 = jax.random.split(key, 5)
        x_q = jax.random.normal(k1, (B, T, C), dtype=jnp.float32)
        w_q = jax.random.normal(k2, (H, DQK, C), dtype=jnp.float32) / math.sqrt(C)
        w_k = jax.random.normal(k3, (H, DQK, C), dtype=jnp.float32) / math.sqrt(C)
        w_v = jax.random.normal(k4, (H, DV, C), dtype=jnp.float32) / math.sqrt(C)
        w_o = jax.random.normal(k5, (DV * H, C), dtype=jnp.float32) / math.sqrt(C)
        return {'x_q': x_q, 'w_q': w_q, 'w_k': w_k, 'w_v': w_v, 'w_o': w_o}
    _L1_attn_in = _L1_attn_setup()

    def _L1_ffn_setup():
        import jax, jax.numpy as jnp
        import numpy as np
        D = 128
        H = 512
        E = 8
        B = 2
        T = 256
        LN_EPS = 1e-05

        def _layer_norm(r, gamma, beta):
            mu = jnp.mean(r, axis=-1, keepdims=True)
            var = jnp.mean(jnp.square(r - mu), axis=-1, keepdims=True)
            return (r - mu) * jax.lax.rsqrt(var + LN_EPS) * gamma + beta
        key = jax.random.key(seed)
        ks = jax.random.split(key, 9)
        s_in = 1.0 / np.sqrt(D)
        s_hid = 1.0 / np.sqrt(H)
        x = jax.random.normal(ks[0], (B, T, D), dtype=jnp.float32)
        Wg = jax.random.uniform(ks[1], (D, E), jnp.float32, -s_in, s_in)
        bg = jax.random.uniform(ks[2], (E,), jnp.float32, -s_in, s_in)
        W1 = jax.random.uniform(ks[3], (E, D, H), jnp.float32, -s_in, s_in)
        b1 = jax.random.uniform(ks[4], (E, H), jnp.float32, -s_in, s_in)
        W2 = jax.random.uniform(ks[5], (E, H, D), jnp.float32, -s_hid, s_hid)
        b2 = jax.random.uniform(ks[6], (E, D), jnp.float32, -s_hid, s_hid)
        gamma = jnp.ones((D,), jnp.float32)
        beta = jnp.zeros((D,), jnp.float32)
        return {'x': x, 'Wg': Wg, 'bg': bg, 'W1': W1, 'b1': b1, 'W2': W2, 'b2': b2, 'gamma': gamma, 'beta': beta}
    _L1_ffn_in = _L1_ffn_setup()
    _d = {'L0_attn_x': _L0_attn_in['x'], 'L0_attn_Wq': _L0_attn_in['Wq'], 'L0_attn_Wk': _L0_attn_in['Wk'], 'L0_attn_Wv': _L0_attn_in['Wv'], 'L0_attn_g_scale': _L0_attn_in['g_scale'], 'L0_ffn_Wg': _L0_ffn_in['Wg'], 'L0_ffn_ln_scale': _L0_ffn_in['ln_scale'], 'L0_ffn_ln_bias': _L0_ffn_in['ln_bias'], 'L0_ffn_W1': _L0_ffn_in['W1'], 'L0_ffn_b1': _L0_ffn_in['b1'], 'L0_ffn_W2': _L0_ffn_in['W2'], 'L0_ffn_b2': _L0_ffn_in['b2'], 'L1_attn_w_q': _L1_attn_in['w_q'], 'L1_attn_w_k': _L1_attn_in['w_k'], 'L1_attn_w_v': _L1_attn_in['w_v'], 'L1_attn_w_o': _L1_attn_in['w_o'], 'L1_ffn_Wg': _L1_ffn_in['Wg'], 'L1_ffn_bg': _L1_ffn_in['bg'], 'L1_ffn_W1': _L1_ffn_in['W1'], 'L1_ffn_b1': _L1_ffn_in['b1'], 'L1_ffn_W2': _L1_ffn_in['W2'], 'L1_ffn_b2': _L1_ffn_in['b2'], 'L1_ffn_gamma': _L1_ffn_in['gamma'], 'L1_ffn_beta': _L1_ffn_in['beta']}
    _x0 = _d['L0_attn_x']
    _d['L0_attn_x'] = jax.random.normal(jax.random.fold_in(jax.random.key(seed), 1), (8, 512, 128), dtype=_x0.dtype)
    del _x0
    return _d

def reference(L0_attn_x, L0_attn_Wq, L0_attn_Wk, L0_attn_Wv, L0_attn_g_scale, L0_ffn_Wg, L0_ffn_ln_scale, L0_ffn_ln_bias, L0_ffn_W1, L0_ffn_b1, L0_ffn_W2, L0_ffn_b2, L1_attn_w_q, L1_attn_w_k, L1_attn_w_v, L1_attn_w_o, L1_ffn_Wg, L1_ffn_bg, L1_ffn_W1, L1_ffn_b1, L1_ffn_W2, L1_ffn_b2, L1_ffn_gamma, L1_ffn_beta):

    def _L0_attn_ref(x, Wq, Wk, Wv, g_scale):
        import jax, jax.numpy as jnp
        import numpy as np
        NUM_HEADS = 16
        EPS = 1e-12

        def _l2norm(t):
            n = jnp.sqrt(jnp.sum(t * t, axis=-1, keepdims=True))
            return t / jnp.maximum(n, EPS)
        B, S, E = x.shape
        H = NUM_HEADS
        D = E // H
        q = (x @ Wq.T).reshape(B, S, H, D).transpose(0, 2, 1, 3)
        k = (x @ Wk.T).reshape(B, S, H, D).transpose(0, 2, 1, 3)
        v = (x @ Wv.T).reshape(B, S, H, D).transpose(0, 2, 1, 3)
        q = _l2norm(q)
        k = _l2norm(k)
        scores = g_scale * jnp.einsum('bhqd,bhkd->bhqk', q, k)
        attn = jax.nn.softmax(scores, axis=-1)
        out = jnp.einsum('bhqk,bhkd->bhqd', attn, v)
        out = out.transpose(0, 2, 1, 3).reshape(B, S, E)
        return out

    def _L0_ffn_ref(x, Wg, ln_scale, ln_bias, W1, b1, W2, b2):
        import jax, jax.numpy as jnp
        import numpy as np
        B, T, D, E, H = (8, 256, 128, 8, 32)
        LN_EPS = 1e-05
        Bs, Ts, Ds = x.shape
        xt = x.reshape(Bs * Ts, Ds)
        logits = xt @ Wg.T
        top1 = jnp.argmax(logits, axis=-1)
        mu = jnp.mean(xt, axis=-1, keepdims=True)
        var = jnp.mean(jnp.square(xt - mu), axis=-1, keepdims=True)
        xhat = (xt - mu) * jax.lax.rsqrt(var + LN_EPS)
        n_experts = Wg.shape[0]

        def body(y, p):
            s_e, b_e, w1, bb1, w2, bb2, eid = p
            h = jax.nn.gelu((xhat * s_e + b_e) @ w1 + bb1, approximate=False)
            out = h @ w2 + bb2
            mask = (top1 == eid)[:, None].astype(out.dtype)
            return (y + mask * out, None)
        y0 = jnp.zeros_like(xt)
        y, _ = jax.lax.scan(body, y0, (ln_scale, ln_bias, W1, b1, W2, b2, jnp.arange(n_experts)))
        return y.reshape(Bs, Ts, Ds)

    def _L1_attn_ref(x_q, w_q, w_k, w_v, w_o):
        import jax, jax.numpy as jnp
        import numpy as np
        import math
        B, T, C = (4, 256, 128)
        H, DQK, DV = (16, 64, 64)
        q = jnp.einsum('ntc,hdc->nhtd', x_q, w_q)
        k = jnp.einsum('ntc,hdc->nhtd', x_q, w_k)
        v = jnp.einsum('ntc,hdc->nhtd', x_q, w_v)
        a = jnp.einsum('nhtd,nhsd->nhts', q, k) / math.sqrt(q.shape[3])
        t = a.shape[2]
        causal_forbidden = jnp.arange(t)[:, None] < jnp.arange(t)[None, :]
        a = jnp.where(causal_forbidden[None, None], -jnp.inf, a)
        a = jax.nn.softmax(a, axis=3)
        y = jnp.einsum('nhts,nhsd->nthd', a, v).reshape(a.shape[0], t, -1)
        return y @ w_o

    def _L1_ffn_ref(x, Wg, bg, W1, b1, W2, b2, gamma, beta):
        import jax, jax.numpy as jnp
        import numpy as np
        D = 128
        H = 512
        E = 8
        B = 2
        T = 256
        LN_EPS = 1e-05

        def _layer_norm(r, gamma, beta):
            mu = jnp.mean(r, axis=-1, keepdims=True)
            var = jnp.mean(jnp.square(r - mu), axis=-1, keepdims=True)
            return (r - mu) * jax.lax.rsqrt(var + LN_EPS) * gamma + beta
        logits = jnp.einsum('btd,de->bte', x, Wg) + bg
        top2_vals, top2_idx = jax.lax.top_k(logits, 2)
        scores = jax.nn.softmax(top2_vals, axis=-1)
        onehot = jax.nn.one_hot(top2_idx, E, dtype=x.dtype)
        combine = jnp.einsum('btk,btke->bte', scores, onehot)
        h = jnp.einsum('btd,edh->bteh', x, W1) + b1[None, None]
        h = jax.nn.gelu(h, approximate=False)
        y = jnp.einsum('bteh,ehd->bted', h, W2) + b2[None, None]
        out = jnp.einsum('bted,bte->btd', y, combine)
        return _layer_norm(x + out, gamma, beta)
    x = L0_attn_x
    x = x + _L0_attn_ref(_layernorm(x, axis=-1), L0_attn_Wq, L0_attn_Wk, L0_attn_Wv, L0_attn_g_scale)
    x = x + _L0_ffn_ref(_layernorm(x, axis=-1), L0_ffn_Wg, L0_ffn_ln_scale, L0_ffn_ln_bias, L0_ffn_W1, L0_ffn_b1, L0_ffn_W2, L0_ffn_b2)
    x = x + _L1_attn_ref(_layernorm(x, axis=-1), L1_attn_w_q, L1_attn_w_k, L1_attn_w_v, L1_attn_w_o)
    x = x + _L1_ffn_ref(_layernorm(x, axis=-1), L1_ffn_Wg, L1_ffn_bg, L1_ffn_W1, L1_ffn_b1, L1_ffn_W2, L1_ffn_b2, L1_ffn_gamma, L1_ffn_beta)
    return x

_drawn_inputs = setup_inputs


def setup_inputs(seed=0):
    import zlib

    import numpy as np

    out = dict(_drawn_inputs(seed))
    spreads = {'L0_ffn_ln_scale': (1.0, 0.6),
     'L0_ffn_ln_bias': (0.0, 0.8),
     'L0_ffn_b1': (0.0, 0.8),
     'L0_ffn_b2': (0.0, 0.1),
     'L1_ffn_gamma': (1.0, 0.2),
     'L1_ffn_beta': (0.0, 0.1)}
    factors = {'L0_ffn_W1': 3.319,
     'L0_ffn_W2': 2.946,
     'L1_ffn_bg': 3.52,
     'L1_ffn_b1': 8.0,
     'L1_ffn_b2': 6.509}
    for name, (base, spread) in spreads.items():
        noise = np.random.default_rng([zlib.crc32(name.encode()), seed]).standard_normal(out[name].shape)
        drawn = base * np.exp(spread * noise) if base else spread * noise
        out[name] = jnp.asarray(drawn.astype(out[name].dtype))
    for name, factor in factors.items():
        out[name] = (out[name] * factor).astype(out[name].dtype)
    return out
```

```python
import numpy as np
from contextlib import ExitStack

import concourse.bass as bass
from concourse import mybir

F32 = mybir.dt.float32
F32R = mybir.dt.float32r
BF16 = mybir.dt.bfloat16
ALU = mybir.AluOpType
ACT = mybir.ActivationFunctionType
AX = mybir.AxisListType

P = 128
BATCH, SEQ, DIM = 8, 512, 128
TILES = SEQ // P
EXPERTS = 8
LN_EPS = 1e-5
L2_EPS = 1e-12
MASKED = -1e30

H0 = 16
D0 = DIM // H0
HG = 4
GROUPS0 = H0 // HG
STRIP = 32
TERMS = 4
STEPS0 = GROUPS0 * TILES
HID0 = 32
CH0 = EXPERTS * HID0 // P
H1 = 16
D1 = 64
PAIRS = H1 // 2
SCALE1 = 1.0 / D1 ** 0.5
HID1 = 512
CH1 = HID1 // P

WORK = (["xT0"] + [f"qkv0_{t}" for t in range(TILES)]
        + [f"{n}{g}" for g in range(GROUPS0) for n in ("qT", "kT")]
        + [f"oT{g}" for g in range(GROUPS0)]
        + ["xtT", "xh2T", "lg0", "hid0_0", "hid0_1", "ohT", "mask0", "mask1", "y0"]
        + ["x2T"] + [f"v{t}_{n}" for t in range(TILES) for n in range(2)]
        + ["q0", "k0", "q1", "k1"] + [f"mx0_{i}" for i in range(5)] + ["mT0"]
        + [n for p in range(PAIRS) for n in
           ([f"q{p + 2}", f"k{p + 2}"] if p + 2 < PAIRS else [])
           + ([f"mx{p + 1}_{i}" for i in range(5)] + [f"mT{p + 1}"] if p + 1 < PAIRS else [])]
        + ["proj", "xnT", "lg1", "cT", "b2"])
if len(WORK) % 2:
    WORK.append("pad")
WORK_NO = {name: n for n, name in enumerate(WORK)}
WORK_PER = len(WORK) // 2

UNITS_A0 = 2 * STEPS0
UNITS_A1 = 3 * PAIRS
UNITS_F1 = EXPERTS * CH1 // 2
UNIT_A1 = UNITS_A0
UNIT_F1 = UNITS_A0 + UNITS_A1
UNITS = UNIT_F1 + UNITS_F1

OUT_A1 = GROUPS0 // 2
OUT_F1 = OUT_A1 + PAIRS
OUT_PER = OUT_F1 + EXPERTS // 2

PROB0 = 0
PROB0_SLOTS = 3
HIDT = PROB0_SLOTS * HG * SEQ
V1 = 0
PROB1 = V1 + TILES * H1 * D1
PROB1_PAIR = 2 * 1024 + 512
TSUM = PROB1 + 2 * PROB1_PAIR
BIG = TSUM + 2 * 2 * 384

LAYERNORMS = 6
DVE_LINKS = 66


def layers_kernel(nc, x, wqkv0, g_scale, wg0, s0, bias_ln0, w1_0, b1_0, w2_0, b2_0,
                  wq1, wk1, wv1, wo1, wg1, bg1, w1_1, b1_1, w2_1, b2_1, gamma, beta, out):
    ctx = ExitStack()
    with ctx:
        def sb(name, shape, dt=F32):
            return ctx.enter_context(nc.sbuf_tensor(name, shape, dt))

        def sem(name):
            return ctx.enter_context(nc.semaphore(name))

        ident = sb("ident", [P, P])
        ident_r = sb("ident_r", [P, P], F32R)
        ident_b = sb("ident_b", [P, P], BF16)
        mask_qk = sb("mask_qk", [P, P], BF16)
        mask_kq = sb("mask_kq", [P, P], BF16)
        ones = sb("ones", [P, D1])
        rank = sb("rank", [P, EXPERTS])
        head_sel = sb("head_sel", [P, 2, 1])
        wqkv0_sb = sb("wqkv0_sb", [P, 3 * DIM])
        g_sb = sb("g_sb", [P, 1])
        wg0_sb = sb("wg0_sb", [P, EXPERTS])
        s0_sb = sb("s0_sb", [P, EXPERTS])
        bias_ln0_sb = sb("bias_ln0_sb", [P, EXPERTS])
        w1s0 = sb("w1s0", [P, EXPERTS * HID0])
        b1_0_sb = sb("b1_0_sb", [P, CH0])
        bias0 = sb("bias0", [P, CH0])
        w2_0_sb = sb("w2_0_sb", [P, CH0, DIM])
        b2_0_sb = sb("b2_0_sb", [EXPERTS, DIM])
        wqkv1_hi = sb("wqkv1_hi", [P, 3, H1 * D1], F32R)
        wqkv1_lo = sb("wqkv1_lo", [P, 3, H1 * D1], F32R)
        wo_sb = sb("wo_sb", [P, PAIRS, DIM])
        wg1_sb = sb("wg1_sb", [P, EXPERTS])
        bg1_sb = sb("bg1_sb", [P, EXPERTS])
        w1_hi = sb("w1_hi", [P, EXPERTS * HID1], F32R)
        w1_lo = sb("w1_lo", [P, EXPERTS * HID1], F32R)
        b1_1_sb = sb("b1_1_sb", [P, EXPERTS * CH1])
        w2_1_sb = sb("w2_1_sb", [P, EXPERTS * CH1, DIM])
        b2_1_sb = sb("b2_1_sb", [EXPERTS, DIM])
        gamma_sb = sb("gamma_sb", [P, DIM])
        beta_sb = sb("beta_sb", [P, DIM])

        x_in = sb("x_in", [P, TILES, DIM])
        res = sb("res", [P, TILES, DIM])
        norm_a = sb("norm_a", [P, TILES, DIM])
        norm_b = sb("norm_b", [P, TILES, DIM])
        acc = sb("acc", [P, TILES, DIM])
        xT = sb("xT", [P, SEQ])
        xT2 = sb("xT2", [P, SEQ])
        xT_hi = sb("xT_hi", [P, SEQ], F32R)
        xT_lo = sb("xT_lo", [P, SEQ], F32R)
        stats = sb("stats", [P, TILES, 6])
        mean = sb("mean", [P, TILES])
        halves = sb("halves", [P, TILES])
        var_eps = sb("var_eps", [P, TILES])
        minus_half = sb("minus_half", [P, TILES])
        rstd = sb("rstd", [P, TILES])
        inv_norm = sb("inv_norm", [P, 2 * TILES * H0])
        sum_sq = sb("sum_sq", [P, 2 * TILES * H0])
        newton = sb("newton", [P, 2 * TILES * H0])
        vstat = sb("vstat", [P, TILES, H0, STRIP])
        oT_sb = sb("oT_sb", [P, SEQ])
        rsum0 = sb("rsum0", [P, TILES * HG])
        lg = sb("lg", [P, TILES, EXPERTS])
        lg2 = sb("lg2", [P, TILES, EXPERTS])
        eq = sb("eq", [P, TILES, EXPERTS])
        oh1 = sb("oh1", [P, TILES, EXPERTS])
        oh2 = sb("oh2", [P, TILES, EXPERTS])
        comb = sb("comb", [P, TILES, EXPERTS])
        top1 = sb("top1", [P, TILES])
        top2 = sb("top2", [P, TILES])
        best = sb("best", [P, TILES])
        gap = sb("gap", [P, TILES])
        eg = sb("eg", [P, TILES])
        sc1 = sb("sc1", [P, TILES])
        sc2 = sb("sc2", [P, TILES])
        neg_max = sb("neg_max", [P, TILES, 2])
        neg_max_hl = sb("neg_max_hl", [P, TILES, 4], BF16)
        ra = sb("ra", [P, 8 * SEQ], F32R)
        rb = sb("rb", [P, 8 * SEQ], F32R)
        big = sb("big", [P, BIG])
        g_buf = sb("g_buf", [P, PAIRS, SEQ])
        gf = g_buf[:, :, :].rearrange("p a b -> p (a b)")
        QK = 2 * TILES * DIM
        qk_sb = gf[:, 0:QK]
        qk_sq = gf[:, QK:2 * QK]
        qk_n = gf[:, 2 * QK:3 * QK]
        hid0T = gf[:, 3 * QK:3 * QK + CH0 * SEQ].rearrange("p (c n) -> p c n", c=CH0)
        hid0m = gf[:, QK:QK + CH0 * SEQ].rearrange("p (c n) -> p c n", c=CH0)
        yT = g_buf
        mask_f = acc[:, 0:2, :]
        ohx = acc[:, :, :].bitcast(BF16).rearrange("p t (e h) -> p t e h", e=EXPERTS)
        w1raw0 = xT2[:, 0:EXPERTS * HID0]
        lnsum = xT2
        rsum1 = oT_sb
        selT = oT_sb[0:EXPERTS, :]
        parts = ra[:, :].rearrange("p (w t h r d) -> p w t h r d", w=2, t=TILES, h=H0, r=TERMS)
        qkT0 = rb[:, :].rearrange("p (w g n) -> p w g n", w=2, g=GROUPS0)
        qa1 = ra[:, 0:4 * SEQ].rearrange("p (s n) -> p s n", s=4)
        ka1 = ra[:, 4 * SEQ:8 * SEQ].rearrange("p (s n) -> p s n", s=4)
        qb1 = rb[:, 0:4 * SEQ].rearrange("p (s n) -> p s n", s=4)
        kb1 = rb[:, 4 * SEQ:8 * SEQ].rearrange("p (s n) -> p s n", s=4)
        v1 = big[:, V1:PROB1].rearrange("p (t n) -> p t n", t=TILES)
        stage_qkv1 = big[:, 0:3 * H1 * D1]
        stage_w1 = big[:, 3 * H1 * D1:3 * H1 * D1 + EXPERTS * HID1]

        def prob0(n):
            at = PROB0 + (n % PROB0_SLOTS) * HG * SEQ
            return big[:, at:at + HG * SEQ]

        def prob1_main(p, j):
            at = PROB1 + (p % 2) * PROB1_PAIR + j * 1024
            return big[:, at:at + 1024]

        def prob1_rest(p):
            at = PROB1 + (p % 2) * PROB1_PAIR + 2048
            return big[:, at:at + 512]

        def tsum(p, j):
            at = TSUM + ((p % 2) * 2 + j) * 384
            return big[:, at:at + 384]

        def hid1T(e, c):
            at = HIDT + ((e % 2) * CH1 + c) * SEQ
            return big[:, at:at + SEQ]

        scores = ctx.enter_context(nc.psum_tensor("scores", [P, 2, 1024], F32))
        outs = ctx.enter_context(nc.psum_tensor("outs", [P, 2, SEQ], F32))
        work = ctx.enter_context(nc.psum_tensor("work", [P, 2, SEQ], F32))

        weights_in = sem("weights_in")
        consts = sem("consts")
        const_step = sem("const_step")
        weights_hi = sem("weights_hi")
        weights_ready = sem("weights_ready")
        fold_ready = sem("fold_ready")
        x_loaded = sem("x_loaded")
        x_taken = sem("x_taken")
        out_sent = sem("out_sent")
        out_ready = sem("out_ready")
        var_ready = sem("var_ready")
        rstd_ready = sem("rstd_ready")
        rows_ready = sem("rows_ready")
        sumsq_ready = sem("sumsq_ready")
        invn_ready = sem("invn_ready")
        ln_done = sem("ln_done")
        qkn_ready = sem("qkn_ready")
        parts_hi = sem("parts_hi")
        parts_ready = sem("parts_ready")
        pv0_done = sem("pv0_done")
        onehot_ready = sem("onehot_ready")
        x_hi = sem("x_hi")
        qk1_hi = sem("qk1_hi")
        negmax_ready = sem("negmax_ready")
        tsum_ready = sem("tsum_ready")
        tsum_step = sem("tsum_step")
        rsum1_ready = sem("rsum1_ready")
        gap_ready = sem("gap_ready")
        eg_ready = sem("eg_ready")
        comb_ready = sem("comb_ready")
        dve_step = sem("dve_step")
        score_full = sem("score_full")
        score_done = sem("score_done")
        out_full = [sem(f"out_full{i}") for i in range(2)]
        out_free = [sem(f"out_free{i}") for i in range(2)]
        work_full = [sem(f"work_full{i}") for i in range(2)]
        work_free = [sem(f"work_free{i}") for i in range(2)]

        block = ctx.enter_context(nc.Block())

        def work_bank(name):
            return work[:, WORK_NO[name] % 2, :]

        def work_fills(name, b):
            return b * WORK_PER + WORK_NO[name] // 2 + 1

        def work_open(pe, name, b):
            pe.wait_ge(work_free[WORK_NO[name] % 2], work_fills(name, b))
            return work_bank(name)

        def work_wait(eng, name, b):
            eng.wait_ge(work_full[WORK_NO[name] % 2], work_fills(name, b))
            return work_bank(name)

        def work_moved(eng, name, b):
            eng.wait_ge(work_free[WORK_NO[name] % 2], work_fills(name, b) + 1)

        def full_of(name):
            return work_full[WORK_NO[name] % 2]

        def free_of(name):
            return work_free[WORK_NO[name] % 2]

        def unit_slot(u):
            return scores[:, u % 2, :]

        N_WEIGHTS = 20

        @block.sync
        def _(sp):
            for dst, src in ((wqkv0_sb[:], wqkv0), (g_sb[:], g_scale.to_broadcast([P, 1])),
                             (wg0_sb[:], wg0), (s0_sb[:], s0), (bias_ln0_sb[:], bias_ln0),
                             (w1raw0[:], w1_0), (b1_0_sb[:], b1_0),
                             (stage_qkv1[:, 0:H1 * D1], wq1),
                             (stage_qkv1[:, H1 * D1:2 * H1 * D1], wk1),
                             (stage_qkv1[:, 2 * H1 * D1:], wv1), (stage_w1, w1_1),
                             (w2_0_sb[:], w2_0), (b2_0_sb[:], b2_0), (wo_sb[:], wo1),
                             (wg1_sb[:], wg1), (bg1_sb[:], bg1.to_broadcast([P, EXPERTS])),
                             (b1_1_sb[:], b1_1), (w2_1_sb[:], w2_1), (b2_1_sb[:], b2_1),
                             (gamma_sb[:], gamma.to_broadcast([P, DIM]))):
                sp.dma_start(dst, src).then_inc(weights_in, 16)
            sp.dma_start(x_in[:], x[0]).then_inc(x_loaded, 16)
            sp.dma_start(beta_sb[:], beta.to_broadcast([P, DIM])).then_inc(out_sent, 16)
            with sp.Fori(0, BATCH - 1) as b:
                sp.wait_ge(x_taken, b + 1)
                sp.dma_start(x_in[:], x[bass.ds(b + 1, 1)]).then_inc(x_loaded, 16)
                sp.wait_ge(out_ready, b + 1)
                sp.dma_start(out[bass.ds(b, 1)], norm_b[:]).then_inc(out_sent, 16)
            sp.wait_ge(out_ready, BATCH)
            sp.dma_start(out[BATCH - 1], norm_b[:]).then_inc(out_sent, 16)
            sp.wait_ge(out_sent, 16 * (BATCH + 1))

        @block.gpsimd
        def _(pool):
            nc.gpsimd.memset(ident[:], 0.0).then_inc(const_step, 1)
            nc.gpsimd.memset(mask_f[:], 0.0).then_inc(const_step, 1)
            nc.gpsimd.memset(head_sel[:], 0.0).then_inc(const_step, 1)
            nc.gpsimd.memset(ones[:], 1.0)
            nc.gpsimd.memset(minus_half[:], -0.5)
            nc.gpsimd.iota(rank[:], pattern=[[-1, EXPERTS]], base=EXPERTS, channel_multiplier=0,
                           allow_small_or_imprecise_dtypes=True)
            pool.wait_ge(const_step, 3)
            nc.gpsimd.affine_select(out=ident[:], in_=ident[:], compare_op=ALU.not_equal, fill=1.0,
                                    base=0, pattern=[[-1, P]], channel_multiplier=1)
            nc.gpsimd.affine_select(out=mask_f[:, 0, :], in_=mask_f[:, 0, :], compare_op=ALU.is_ge,
                                    fill=MASKED, base=0, pattern=[[-1, P]], channel_multiplier=1)
            nc.gpsimd.affine_select(out=mask_f[:, 1, :], in_=mask_f[:, 1, :], compare_op=ALU.is_ge,
                                    fill=MASKED, base=0, pattern=[[1, P]],
                                    channel_multiplier=-1).then_inc(const_step, 1)
            pool.wait_ge(const_step, 4)
            sel = head_sel[D1:D1 + 4, :, 0]
            nc.gpsimd.affine_select(out=sel, in_=sel, compare_op=ALU.not_equal, fill=1.0, base=0,
                                    pattern=[[-1, 2]], channel_multiplier=1).then_inc(const_step, 1)
            pool.wait_ge(const_step, 5)
            nc.gpsimd.affine_select(out=sel, in_=sel, compare_op=ALU.not_equal, fill=1.0, base=-2,
                                    pattern=[[-1, 2]], channel_multiplier=1).then_inc(consts, 1)

            with pool.Fori(0, BATCH) as b:
                def inverse_deviations(n):
                    pool.wait_ge(var_ready, b * LAYERNORMS + n + 1)
                    nc.gpsimd.tensor_tensor(rstd[:], var_eps[:], minus_half[:],
                                            ALU.pow).then_inc(rstd_ready, 1)

                for n in range(4):
                    inverse_deviations(n)
                for p in range(PAIRS):
                    pool.wait_ge(score_done, b * UNITS + UNIT_A1 + 3 * p + 3 + 2)
                    for j in range(2):
                        m, r = prob1_main(p, j), prob1_rest(p)
                        t = tsum(p, j)
                        nc.gpsimd.tensor_tensor(t, m[:, P:SEQ], m[:, SEQ:SEQ + 3 * P],
                                                ALU.add).then_inc(tsum_step, 1)
                        pool.wait_ge(tsum_step, b * (4 * PAIRS) + 4 * p + 2 * j + 1)
                        nc.gpsimd.tensor_tensor(t[:, P:3 * P], t[:, P:3 * P],
                                                r[:, 2 * P * j:2 * P * (j + 1)],
                                                ALU.add).then_inc(tsum_step, 1)
                        pool.wait_ge(tsum_step, b * (4 * PAIRS) + 4 * p + 2 * j + 2)
                        nc.gpsimd.tensor_tensor(t[:, 2 * P:3 * P], t[:, 2 * P:3 * P],
                                                m[:, 7 * P:8 * P], ALU.add).then_inc(tsum_ready, 1)
                for n in range(4, LAYERNORMS):
                    inverse_deviations(n)

        @block.scalar
        def _(act):
            copy, activation = nc.scalar.copy, nc.scalar.activation
            act.wait_ge(consts, 1)
            copy(eg[:], minus_half[:]).then_inc(score_done, 2)
            act.wait_ge(weights_in, 16 * N_WEIGHTS)
            copy(wqkv1_hi[:].rearrange("p a n -> p (a n)"), stage_qkv1).then_inc(weights_hi, 1)
            copy(w1_hi[:], stage_w1).then_inc(weights_hi, 1)

            with act.Fori(0, BATCH) as b:
                nc.scalar.preload_act_table_set("natural_log_exp_and_others")
                w = work_wait(act, "xT0", b)
                copy(xT[:], w).then_inc(free_of("xT0"), 1)
                for t in range(TILES):
                    w = work_wait(act, f"qkv0_{t}", b)
                    copy(qk_sb.rearrange("p (w t n) -> p w t n", w=2, t=TILES)[:, :, t, :],
                         w[:, 0:2 * DIM].rearrange("p (w n) -> p w n", w=2))
                    if t == 0:
                        act.wait_ge(weights_ready, 1)
                    copy(vstat[:, t, :, 0:D0],
                         w[:, 2 * DIM:3 * DIM].rearrange("p (h d) -> p h d", d=D0)
                         ).then_inc(free_of(f"qkv0_{t}"), 1)
                act.wait_ge(sumsq_ready, b + 1)
                activation(newton[:], sum_sq[:], ACT.Ln).then_inc(ln_done, 1)
                act.wait_ge(ln_done, b + 1)
                activation(inv_norm[:], newton[:], ACT.Exp, scale=-0.5).then_inc(invn_ready, 1)
                act.wait_ge(qkn_ready, b + 1)
                n4 = qk_n.rearrange("p (w n d) -> p w n d", w=2, d=D0)
                for w_, sl in ((0, slice(0, 2)), (1, slice(0, 3, 2))):
                    dst = parts[:, w_].rearrange("p t h r d -> p (t h) r d")[:, :, sl, :]
                    last = copy(dst, n4[:, w_].unsqueeze(2).broadcast_to([P, TILES * H0, 2, D0]))
                last.then_inc(parts_hi, 1)
                for g in range(GROUPS0):
                    w = work_wait(act, f"qT{g}", b)
                    copy(qkT0[:, 0, g, :], w).then_inc(free_of(f"qT{g}"), 1)

                for u in range(UNITS_A0):
                    n = u // 2
                    act.wait_ge(score_full, b * UNITS + u + 1)
                    if n >= PROB0_SLOTS:
                        g, kb = (n - PROB0_SLOTS) // TILES, (n - PROB0_SLOTS) % TILES
                        if kb == TILES - 1:
                            act.wait_ge(out_full[g % 2], b * OUT_PER + g // 2 + 1)
                        else:
                            act.wait_ge(pv0_done, (b * GROUPS0 + g) * (TILES - 1) + kb + 1)
                    activation(prob0(n)[:, (u % 2) * 1024:(u % 2 + 1) * 1024], unit_slot(u),
                               ACT.Exp).then_inc(score_done, 1)

                w = work_wait(act, "xtT", b)
                copy(xT[:], w).then_inc(free_of("xtT"), 1)
                for c in range(CH0):
                    w = work_wait(act, f"hid0_{c}", b)
                    activation(hid0T[:, c, :], w, ACT.Gelu,
                               bias=bias0[:, c:c + 1]).then_inc(free_of(f"hid0_{c}"), 1)
                w = work_wait(act, "ohT", b)
                copy(selT[:], w[0:EXPERTS, :]).then_inc(free_of("ohT"), 1)

                nc.scalar.preload_act_table_set("natural_log_exp_and_others")
                w = work_wait(act, "x2T", b)
                copy(xT_hi[:], w).then_inc(x_hi, 1)
                for t in range(TILES):
                    w = work_wait(act, f"v{t}_0", b)
                    copy(v1[:, t, 0:SEQ], w).then_inc(free_of(f"v{t}_0"), 1)

                def hi_q(p):
                    w = work_wait(act, f"q{p}", b)
                    for j in range(2):
                        s = 2 * (p % 2) + j
                        copy(qb1[0:D1, s, :], w[j * D1:(j + 1) * D1, :])
                        last = copy(qa1[0:D1, s, :], w[j * D1:(j + 1) * D1, :])
                    last.then_inc(qk1_hi, 1)

                def hi_k(p):
                    w = work_wait(act, f"k{p}", b)
                    for j in range(2):
                        s = 2 * (p % 2) + j
                        last = copy(ka1[0:D1, s, :], w[j * D1:(j + 1) * D1, :])
                    last.then_inc(qk1_hi, 1)

                def max_rows(p):
                    w = work_wait(act, f"mT{p}", b)
                    for j in range(2):
                        last = copy(qb1[D1:D1 + 4, 2 * (p % 2) + j, :], w[D1:D1 + 4, :])
                    last.then_inc(free_of(f"mT{p}"), 1)

                def inverse_sums(p):
                    act.wait_ge(out_full[1], b * OUT_PER + OUT_A1 + p + 1)
                    activation(lnsum[:], outs[:, 1, :], ACT.Ln).then_inc(out_free[1], 1)
                    act.wait_ge(out_free[1], b * OUT_PER + OUT_A1 + p + 2)
                    act.wait_ge(out_free[0], b * OUT_PER + OUT_A1 + p + 1)
                    activation(rsum1[:], lnsum[:], ACT.Exp, scale=-1.0).then_inc(rsum1_ready, 1)

                for p in range(2):
                    hi_q(p)
                    hi_k(p)
                max_rows(0)
                for p in range(PAIRS):
                    u = UNIT_A1 + 3 * p
                    for j in range(2):
                        act.wait_ge(score_full, b * UNITS + u + j + 1)
                        activation(prob1_main(p, j), unit_slot(u + j), ACT.Exp,
                                   scale=SCALE1).then_inc(score_done, 1)
                    if p + 2 < PAIRS:
                        hi_q(p + 2)
                    act.wait_ge(score_full, b * UNITS + u + 3)
                    activation(prob1_rest(p), unit_slot(u + 2)[:, 0:512], ACT.Exp,
                               scale=SCALE1).then_inc(score_done, 1)
                    if p + 2 < PAIRS:
                        hi_k(p + 2)
                    if p >= 1:
                        inverse_sums(p - 1)
                    if p + 1 < PAIRS:
                        max_rows(p + 1)
                inverse_sums(PAIRS - 1)

                w = work_wait(act, "xnT", b)
                copy(xT[:], w)
                copy(xT_hi[:], w).then_inc(x_hi, 1)
                act.wait_ge(gap_ready, b + 1)
                activation(eg[:], gap[:], ACT.Exp).then_inc(eg_ready, 1)
                w = work_wait(act, "cT", b)
                copy(selT[:], w[0:EXPERTS, :]).then_inc(free_of("cT"), 1)
                for e in range(EXPERTS):
                    if e >= 2:
                        act.wait_ge(out_full[e % 2], b * OUT_PER + OUT_F1 + (e - 2) // 2 + 1)
                    for h in range(CH1 // 2):
                        u = UNIT_F1 + e * (CH1 // 2) + h
                        act.wait_ge(score_full, b * UNITS + u + 1)
                        for c in range(2):
                            ch = 2 * h + c
                            last = activation(hid1T(e, ch), unit_slot(u)[:, c * SEQ:(c + 1) * SEQ],
                                              ACT.Gelu, bias=b1_1_sb[:, e * CH1 + ch:e * CH1 + ch + 1])
                        last.then_inc(score_done, 1)

        @block.vector
        def _(dve):
            v = nc.vector
            dve.wait_ge(weights_in, 16 * N_WEIGHTS)
            dve.wait_ge(consts, 1)
            v.memset(vstat[:], 0.0).then_inc(dve_step, 1)
            v.tensor_copy(ident_b[:], ident[:]).then_inc(work_free[0], 1)
            v.tensor_copy(ident_r[:], ident[:]).then_inc(work_free[1], 1)
            v.tensor_copy(mask_qk[:], mask_f[:, 0, :]).then_inc(out_free[0], 1)
            v.tensor_copy(mask_kq[:], mask_f[:, 1, :]).then_inc(out_free[1], 1)
            v.tensor_tensor(w1s0[:].rearrange("p (e h) -> p e h", h=HID0),
                            w1raw0[:].rearrange("p (e h) -> p e h", h=HID0),
                            s0_sb[:].unsqueeze(2).broadcast_to([P, EXPERTS, HID0]), ALU.mult)
            dve.wait_ge(dve_step, 1)
            v.memset(vstat[:, :, :, D0:D0 + 1], 1.0)
            dve.wait_ge(fold_ready, 1)
            for c in range(CH0):
                for j in range(P // HID0):
                    e = c * (P // HID0) + j
                    rows = slice(j * HID0, (j + 1) * HID0)
                    v.tensor_tensor(bias0[rows, c:c + 1], outs[rows, 0, c * 8 + e:c * 8 + e + 1],
                                    b1_0_sb[rows, c:c + 1], ALU.add)
            dve.wait_ge(weights_hi, 2)
            v.tensor_tensor(wqkv1_lo[:].rearrange("p a n -> p (a n)"), stage_qkv1,
                            wqkv1_hi[:].bitcast(F32).rearrange("p a n -> p (a n)"), ALU.subtract)
            v.tensor_tensor(w1_lo[:], stage_w1, w1_hi[:].bitcast(F32),
                            ALU.subtract).then_inc(weights_ready, 1)
            dve.wait_ge(weights_ready, 1)

            with dve.Fori(0, BATCH) as b:
                links = [0]

                def link(ins):
                    links[0] += 1
                    ins.then_inc(dve_step, 1)
                    dve.wait_ge(dve_step, b * DVE_LINKS + links[0] + 1)

                def layernorm(n, src, dst):
                    for t in range(TILES):
                        last = v.bn_stats(stats[:, t, :], src[:, t, :])
                    link(last)
                    v.tensor_tensor(mean[:], stats[:, :, 1], stats[:, :, 4], ALU.add)
                    v.tensor_tensor(var_eps[:], stats[:, :, 2], stats[:, :, 5], ALU.add)
                    link(v.tensor_tensor(halves[:], stats[:, :, 1], stats[:, :, 4], ALU.subtract))
                    v.tensor_scalar(mean[:], mean[:], 0.5, None, ALU.mult)
                    link(v.tensor_tensor(halves[:], halves[:], halves[:], ALU.mult))
                    link(v.scalar_tensor_tensor(var_eps[:], halves[:], DIM / 4.0, var_eps[:],
                                                ALU.mult, ALU.add))
                    v.tensor_scalar(var_eps[:], var_eps[:], 1.0 / DIM, LN_EPS, ALU.mult,
                                    ALU.add).then_inc(var_ready, 1)
                    dve.wait_ge(rstd_ready, b * LAYERNORMS + n + 1)
                    for t in range(TILES):
                        last = v.tensor_scalar(dst[:, t, :], src[:, t, :], mean[:, t:t + 1],
                                               rstd[:, t:t + 1], ALU.subtract, ALU.mult)
                    return last

                def first_best(logits, onehot, value):
                    wide = [P, TILES, EXPERTS]
                    link(v.tensor_reduce(value[:], logits[:], AX.X, ALU.max))
                    link(v.tensor_tensor(eq[:], logits[:], value[:].unsqueeze(2).broadcast_to(wide),
                                         ALU.is_equal))
                    link(v.tensor_tensor(eq[:], eq[:], rank[:].unsqueeze(1).broadcast_to(wide),
                                         ALU.mult))
                    link(v.tensor_reduce(best[:], eq[:], AX.X, ALU.max))
                    return v.tensor_tensor(onehot[:], rank[:].unsqueeze(1).broadcast_to(wide),
                                           best[:].unsqueeze(2).broadcast_to(wide), ALU.is_equal)

                dve.wait_ge(x_loaded, b * 16 + 16)
                layernorm(0, x_in, norm_a).then_inc(rows_ready, 1)
                for t in range(TILES):
                    work_moved(dve, f"qkv0_{t}", b)
                link(v.tensor_tensor(qk_sq, qk_sb, qk_sb, ALU.mult))
                link(v.tensor_reduce(sum_sq[:], qk_sq.rearrange("p (n d) -> p n d", d=D0), AX.X,
                                     ALU.add))
                v.tensor_scalar(sum_sq[:], sum_sq[:], L2_EPS ** 2, None,
                                ALU.max).then_inc(sumsq_ready, 1)
                dve.wait_ge(invn_ready, b + 1)
                link(v.tensor_tensor(newton[:], inv_norm[:], inv_norm[:], ALU.mult))
                link(v.tensor_tensor(newton[:], newton[:], sum_sq[:], ALU.mult))
                link(v.tensor_scalar(newton[:], newton[:], -0.5, 1.5, ALU.mult, ALU.add))
                link(v.tensor_tensor(inv_norm[:], inv_norm[:], newton[:], ALU.mult))
                link(v.tensor_scalar(inv_norm[:, 0:TILES * H0], inv_norm[:, 0:TILES * H0],
                                     g_sb[:, 0:1], None, ALU.mult))
                v.tensor_tensor(qk_n.rearrange("p (n d) -> p n d", d=D0),
                                qk_sb.rearrange("p (n d) -> p n d", d=D0),
                                inv_norm[:].unsqueeze(2).broadcast_to([P, 2 * TILES * H0, D0]),
                                ALU.mult).then_inc(qkn_ready, 1)
                dve.wait_ge(qkn_ready, b + 1)
                dve.wait_ge(parts_hi, b + 1)
                n4 = qk_n.rearrange("p (w n d) -> p w n d", w=2, d=D0)
                for w_, sl in ((0, slice(2, 4)), (1, slice(1, 4, 2))):
                    hl = parts[:, w_].rearrange("p t h r d -> p (t h) r d")
                    wide = [P, TILES * H0, 2, D0]
                    last = v.tensor_tensor(
                        hl[:, :, sl, :], n4[:, w_].unsqueeze(2).broadcast_to(wide),
                        hl[:, :, 0, :].bitcast(F32).unsqueeze(2).broadcast_to(wide), ALU.subtract)
                last.then_inc(parts_ready, 1)
                for g in range(GROUPS0):
                    w = work_wait(dve, f"kT{g}", b)
                    v.tensor_copy(qkT0[:, 1, g, :], w).then_inc(free_of(f"kT{g}"), 1)
                dve.wait_ge(out_sent, b * 16 + 16)
                for g in range(GROUPS0):
                    dve.wait_ge(out_full[g % 2], b * OUT_PER + g // 2 + 1)
                    v.tensor_copy(oT_sb[:], outs[:, g % 2, :]).then_inc(out_free[g % 2], 1)
                    w = work_wait(dve, f"oT{g}", b).rearrange("p (n s) -> p n s", s=STRIP)
                    link(v.reciprocal(rsum0[:], w[:, :, D0]))
                    last = v.tensor_tensor(
                        norm_b[:, :, g * HG * D0:(g + 1) * HG * D0].rearrange(
                            "p t (h d) -> p t h d", d=D0),
                        w[:, :, 0:D0].rearrange("p (t h) d -> p t h d", h=HG),
                        rsum0[:].rearrange("p (t h) -> p t h", h=HG).unsqueeze(3).broadcast_to(
                            [P, TILES, HG, D0]), ALU.mult)
                    last.then_inc(free_of(f"oT{g}"), 1)
                for g in range(GROUPS0 - 2, GROUPS0):
                    work_moved(dve, f"oT{g}", b)
                v.tensor_tensor(res[:], x_in[:], norm_b[:], ALU.add).then_inc(x_taken, 1)
                dve.wait_ge(x_taken, b + 1)

                layernorm(1, res, norm_a).then_inc(rows_ready, 1)
                dve.wait_ge(rows_ready, b * 5 + 2)
                layernorm(2, norm_a, norm_b).then_inc(rows_ready, 1)
                w = work_wait(dve, "xh2T", b)
                v.tensor_copy(xT2[:], w).then_inc(free_of("xh2T"), 1)
                w = work_wait(dve, "lg0", b)
                v.tensor_copy(lg[:], w[:, 0:TILES * EXPERTS].rearrange(
                    "p (t e) -> p t e", e=EXPERTS)).then_inc(free_of("lg0"), 1)
                work_moved(dve, "lg0", b)
                link(first_best(lg, oh1, top1))
                v.tensor_copy(ohx[:], oh1[:].unsqueeze(3).broadcast_to(
                    [P, TILES, EXPERTS, HID0])).then_inc(onehot_ready, 1)
                for c in range(CH0):
                    work_moved(dve, f"hid0_{c}", b)
                    w = work_wait(dve, f"mask{c}", b)
                    v.tensor_tensor(hid0m[:, c, :], hid0T[:, c, :], w,
                                    ALU.mult).then_inc(free_of(f"mask{c}"), 1)
                w = work_wait(dve, "y0", b)
                v.tensor_tensor(res[:].rearrange("p t d -> p (t d)"),
                                res[:].rearrange("p t d -> p (t d)"), w,
                                ALU.add).then_inc(free_of("y0"), 1)
                work_moved(dve, "y0", b)

                layernorm(3, res, norm_a).then_inc(rows_ready, 1)
                w = work_wait(dve, "x2T", b)
                v.tensor_copy(kb1[D1:D1 + 4, :, :].rearrange("p (a j) n -> p a j n", j=2),
                              head_sel[D1:D1 + 4].unsqueeze(1).broadcast_to([4, 2, 2, SEQ]))
                dve.wait_ge(x_hi, b * 2 + 1)
                v.tensor_tensor(xT_lo[:], w, xT_hi[:].bitcast(F32),
                                ALU.subtract).then_inc(free_of("x2T"), 1)
                for t in range(TILES):
                    w = work_wait(dve, f"v{t}_1", b)
                    v.tensor_copy(v1[:, t, SEQ:2 * SEQ], w).then_inc(free_of(f"v{t}_1"), 1)

                def lo_q(p):
                    w = work_bank(f"q{p}")
                    dve.wait_ge(qk1_hi, b * 2 * PAIRS + 2 * p + 1)
                    for j in range(2):
                        s = 2 * (p % 2) + j
                        last = v.tensor_tensor(qa1[D1:2 * D1, s, :], w[j * D1:(j + 1) * D1, :],
                                               qa1[0:D1, s, :].bitcast(F32), ALU.subtract)
                    last.then_inc(free_of(f"q{p}"), 1)

                def lo_k(p):
                    w = work_bank(f"k{p}")
                    dve.wait_ge(qk1_hi, b * 2 * PAIRS + 2 * p + 2)
                    for j in range(2):
                        s = 2 * (p % 2) + j
                        v.tensor_tensor(kb1[0:D1, s, :], w[j * D1:(j + 1) * D1, :],
                                        ka1[0:D1, s, :].bitcast(F32), ALU.subtract)
                        last = v.tensor_copy(ka1[D1:2 * D1, s, :], ka1[0:D1, s, :])
                    last.then_inc(free_of(f"k{p}"), 1)

                def maxima(p):
                    for j in range(2):
                        w = work_wait(dve, f"mx{p}_{2 * j}", b)
                        v.tensor_reduce(neg_max[:, 0, j:j + 1], w[:, 0:P], AX.X, ALU.max,
                                        negate=True)
                        v.tensor_reduce(neg_max[:, 2, j:j + 1], w[:, P:4 * P], AX.X, ALU.max,
                                        negate=True).then_inc(free_of(f"mx{p}_{2 * j}"), 1)
                        w = work_wait(dve, f"mx{p}_{2 * j + 1}", b)
                        v.tensor_reduce(neg_max[:, 3, j:j + 1], w, AX.X, ALU.max,
                                        negate=True).then_inc(free_of(f"mx{p}_{2 * j + 1}"), 1)
                    w = work_wait(dve, f"mx{p}_4", b)
                    v.tensor_reduce(neg_max[:, 1, :], w.rearrange("p (j n) -> p j n", j=2), AX.X,
                                    ALU.max, negate=True).then_inc(free_of(f"mx{p}_4"), 1)
                    for i in range(5):
                        work_moved(dve, f"mx{p}_{i}", b)
                    link(v.tensor_copy(neg_max_hl[:, :, 0:2], neg_max[:]))
                    v.tensor_tensor(neg_max_hl[:, :, 2:4], neg_max[:], neg_max_hl[:, :, 0:2],
                                    ALU.subtract).then_inc(negmax_ready, 1)
                    dve.wait_ge(negmax_ready, b * PAIRS + p + 1)

                def normalize(p):
                    dve.wait_ge(out_full[0], b * OUT_PER + OUT_A1 + p + 1)
                    dve.wait_ge(rsum1_ready, b * PAIRS + p + 1)
                    v.tensor_tensor(yT[:, p, :], outs[:, 0, :], rsum1[:],
                                    ALU.mult).then_inc(out_free[0], 1)

                for p in range(2):
                    lo_q(p)
                    lo_k(p)
                maxima(0)
                for p in range(PAIRS):
                    if p + 2 < PAIRS:
                        lo_q(p + 2)
                        lo_k(p + 2)
                    if p + 1 < PAIRS:
                        maxima(p + 1)
                    if p >= 1:
                        normalize(p - 1)
                normalize(PAIRS - 1)
                w = work_wait(dve, "proj", b)
                v.tensor_tensor(res[:].rearrange("p t d -> p (t d)"),
                                res[:].rearrange("p t d -> p (t d)"), w,
                                ALU.add).then_inc(free_of("proj"), 1)
                work_moved(dve, "proj", b)

                layernorm(4, res, norm_a).then_inc(rows_ready, 1)
                w = work_wait(dve, "xnT", b)
                dve.wait_ge(x_hi, b * 2 + 2)
                v.tensor_tensor(xT_lo[:], w, xT_hi[:].bitcast(F32),
                                ALU.subtract).then_inc(free_of("xnT"), 1)
                w = work_wait(dve, "lg1", b)
                v.tensor_tensor(lg[:], w[:, 0:TILES * EXPERTS].rearrange("p (t e) -> p t e",
                                                                        e=EXPERTS),
                                bg1_sb[:].unsqueeze(1).broadcast_to([P, TILES, EXPERTS]),
                                ALU.add).then_inc(free_of("lg1"), 1)
                work_moved(dve, "lg1", b)
                link(first_best(lg, oh1, top1))
                link(v.scalar_tensor_tensor(lg2[:], oh1[:], -3e38, lg[:], ALU.mult, ALU.add))
                link(first_best(lg2, oh2, top2))
                v.tensor_tensor(gap[:], top2[:], top1[:], ALU.subtract).then_inc(gap_ready, 1)
                dve.wait_ge(eg_ready, b + 1)
                link(v.tensor_scalar(sc2[:], eg[:], 1.0, None, ALU.add))
                link(v.reciprocal(sc1[:], sc2[:]))
                link(v.tensor_tensor(sc2[:], eg[:], sc1[:], ALU.mult))
                wide = [P, TILES, EXPERTS]
                v.tensor_tensor(oh1[:], oh1[:], sc1[:].unsqueeze(2).broadcast_to(wide), ALU.mult)
                link(v.tensor_tensor(oh2[:], oh2[:], sc2[:].unsqueeze(2).broadcast_to(wide),
                                     ALU.mult))
                v.tensor_tensor(comb[:], oh1[:], oh2[:], ALU.add).then_inc(comb_ready, 1)
                dve.wait_ge(comb_ready, b + 1)
                w = work_wait(dve, "b2", b)
                v.tensor_tensor(acc[:].rearrange("p t d -> p (t d)"),
                                norm_a[:].rearrange("p t d -> p (t d)"), w,
                                ALU.add).then_inc(free_of("b2"), 1)
                work_moved(dve, "b2", b)
                for e in range(EXPERTS):
                    dve.wait_ge(out_full[e % 2], b * OUT_PER + OUT_F1 + e // 2 + 1)
                    for t in range(TILES):
                        last = v.scalar_tensor_tensor(
                            acc[:, t, :], outs[:, e % 2, t * DIM:(t + 1) * DIM],
                            comb[:, t, e:e + 1], acc[:, t, :], ALU.mult, ALU.add)
                    last.then_inc(out_free[e % 2], 1)
                    dve.wait_ge(out_free[e % 2], b * OUT_PER + OUT_F1 + e // 2 + 2)
                link(layernorm(5, acc, norm_b))
                link(v.tensor_tensor(norm_b[:], norm_b[:], gamma_sb[:].unsqueeze(1).broadcast_to(
                    [P, TILES, DIM]), ALU.mult))
                link(v.tensor_tensor(norm_b[:], norm_b[:], beta_sb[:].unsqueeze(1).broadcast_to(
                    [P, TILES, DIM]), ALU.add))
                v.tensor_tensor(norm_b[:], res[:], norm_b[:], ALU.add).then_inc(out_ready, 1)
                dve.wait_ge(out_ready, b + 1)
                if WORK[-1] == "pad":
                    work_wait(dve, "pad", b)
                    v.tensor_copy(best[:], top1[:]).then_inc(free_of("pad"), 1)
                assert links[0] == DVE_LINKS, links[0]

        @block.tensor
        def _(pe):
            mm = nc.tensor.matmul
            pe.wait_ge(weights_in, 16 * N_WEIGHTS)
            for c in range(CH0):
                last = mm(outs[:, 0, c * 8:(c + 1) * 8], w1raw0[:, c * P:(c + 1) * P],
                          bias_ln0_sb[:], start=True, stop=True)
            last.then_inc(fold_ready, 1)
            pe.wait_ge(weights_ready, 1)

            def mm3(dst, w_hi, w_lo, x_hi_, x_lo_, swap=False):
                for n, (a, c) in enumerate(((w_hi, x_hi_), (w_hi, x_lo_), (w_lo, x_hi_))):
                    last = mm(dst, a, c, start=(n == 0), stop=(n == 2))
                return last

            with pe.Fori(0, BATCH) as b:
                def transposes(name, rows):
                    w = work_open(pe, name, b)
                    for t in range(TILES):
                        last = nc.tensor.transpose(w[:, t * P:(t + 1) * P], rows[:, t, :], ident[:])
                    last.then_inc(full_of(name), 1)

                pe.wait_ge(rows_ready, b * 5 + 1)
                transposes("xT0", norm_a)
                work_moved(pe, "xT0", b)
                for t in range(TILES):
                    w = work_open(pe, f"qkv0_{t}", b)
                    mm(w[:, 0:3 * DIM], xT[:, t * P:(t + 1) * P], wqkv0_sb[:],
                       start=True, stop=True).then_inc(full_of(f"qkv0_{t}"), 1)
                pe.wait_ge(parts_ready, b + 1)
                for g in range(GROUPS0):
                    for w_, name in enumerate((f"qT{g}", f"kT{g}")):
                        w = work_open(pe, name, b).bitcast(F32R)
                        for t in range(TILES):
                            rows = parts[:, w_, t, g * HG:(g + 1) * HG].rearrange(
                                "p h r d -> p (h r d)")
                            last = nc.tensor.transpose(w[:, t * P:(t + 1) * P], rows, ident_r[:])
                        last.then_inc(full_of(name), 1)

                def scores0(u):
                    n, pair = u // 2, u % 2
                    g, kb = n // TILES, n % TILES
                    if kb == 0 and pair == 0:
                        work_moved(pe, f"qT{g}", b)
                        work_moved(pe, f"kT{g}", b)
                    pe.wait_ge(score_done, b * UNITS + u + 1)
                    for i in range(2):
                        j = 2 * pair + i
                        rows = slice(STRIP * j, STRIP * (j + 1))
                        last = mm(unit_slot(u)[:, i * SEQ:(i + 1) * SEQ],
                                  qkT0[rows, 1, g, kb * P:(kb + 1) * P], qkT0[rows, 0, g, :],
                                  start=True, stop=True)
                    last.then_inc(score_full, 1)

                def values0(n):
                    g, kb = n // TILES, n % TILES
                    if kb == 0:
                        pe.wait_ge(out_free[g % 2], b * OUT_PER + g // 2 + 1)
                    pe.wait_ge(score_done, b * UNITS + 2 * n + 2 + 2)
                    for j in range(HG):
                        last = mm(outs[STRIP * j:STRIP * (j + 1), g % 2, :],
                                  vstat[:, kb, g * HG + j, :], prob0(n)[:, j * SEQ:(j + 1) * SEQ],
                                  start=(kb == 0), stop=(kb == TILES - 1))
                    last.then_inc(out_full[g % 2] if kb == TILES - 1 else pv0_done, 1)

                def rows0(g):
                    pe.wait_ge(out_free[g % 2], b * OUT_PER + g // 2 + 2)
                    w = work_open(pe, f"oT{g}", b)
                    for t in range(TILES):
                        last = nc.tensor.transpose(w[:, t * P:(t + 1) * P],
                                                   oT_sb[:, t * P:(t + 1) * P], ident[:])
                    last.then_inc(full_of(f"oT{g}"), 1)

                scores0(0)
                scores0(1)
                for n in range(STEPS0):
                    if n + 1 < STEPS0:
                        scores0(2 * n + 2)
                        scores0(2 * n + 3)
                    values0(n)
                    if n % TILES == 1 and n > TILES:
                        rows0(n // TILES - 1)
                rows0(GROUPS0 - 1)

                pe.wait_ge(rows_ready, b * 5 + 2)
                transposes("xtT", norm_a)
                pe.wait_ge(rows_ready, b * 5 + 3)
                transposes("xh2T", norm_b)
                work_moved(pe, "xtT", b)
                w = work_open(pe, "lg0", b)
                for t in range(TILES):
                    last = mm(w[:, t * EXPERTS:(t + 1) * EXPERTS], xT[:, t * P:(t + 1) * P],
                              wg0_sb[:], start=True, stop=True)
                last.then_inc(full_of("lg0"), 1)
                work_moved(pe, "xh2T", b)
                for c in range(CH0):
                    w = work_open(pe, f"hid0_{c}", b)
                    mm(w, w1s0[:, c * P:(c + 1) * P], xT2[:], start=True,
                       stop=True).then_inc(full_of(f"hid0_{c}"), 1)
                pe.wait_ge(onehot_ready, b + 1)
                w = work_open(pe, "ohT", b)
                for t in range(TILES):
                    last = mm(w[0:EXPERTS, t * P:(t + 1) * P], oh1[:, t, :], ident[:], start=True,
                              stop=True)
                last.then_inc(full_of("ohT"), 1)
                for c in range(CH0):
                    w = work_open(pe, f"mask{c}", b)
                    for t in range(TILES):
                        rows = ohx[:, t].rearrange("p e h -> p (e h)")[:, c * P:(c + 1) * P]
                        last = mm(w[:, t * P:(t + 1) * P], rows, ident_b[:], start=True, stop=True)
                    last.then_inc(full_of(f"mask{c}"), 1)
                work_moved(pe, "ohT", b)
                for c in range(CH0):
                    work_moved(pe, f"mask{c}", b)
                w = work_open(pe, "y0", b)
                for t in range(TILES):
                    cols = slice(t * P, (t + 1) * P)
                    for c in range(CH0):
                        mm(w[:, cols], hid0m[:, c, cols], w2_0_sb[:, c, :], start=(c == 0),
                           stop=False)
                    last = mm(w[:, cols], selT[:, cols], b2_0_sb[:], start=False, stop=True)
                last.then_inc(full_of("y0"), 1)

                pe.wait_ge(rows_ready, b * 5 + 4)
                transposes("x2T", norm_a)
                work_moved(pe, "x2T", b)
                for t in range(TILES):
                    cols = slice(t * P, (t + 1) * P)
                    for n in range(2):
                        w = work_open(pe, f"v{t}_{n}", b)
                        half = slice(n * SEQ, (n + 1) * SEQ)
                        mm3(w, xT_hi[:, cols], xT_lo[:, cols], wqkv1_hi[:, 2, half],
                            wqkv1_lo[:, 2, half]).then_inc(full_of(f"v{t}_{n}"), 1)

                def project(name, which, p):
                    w = work_open(pe, name, b)
                    cols = slice(p * P, (p + 1) * P)
                    mm3(w, wqkv1_hi[:, which, cols], wqkv1_lo[:, which, cols], xT_hi[:],
                        xT_lo[:]).then_inc(full_of(name), 1)

                def max_scores(p):
                    work_moved(pe, f"q{p}", b)
                    work_moved(pe, f"k{p}", b)

                    def tile(w, at, j, qt):
                        s = 2 * (p % 2) + j
                        width = (qt + 1) * P
                        mm(w[:, at:at + width], qa1[:, s, qt * P:(qt + 1) * P],
                           ka1[:, s, 0:width], start=True, stop=False)
                        return mm(w[:, at + width - P:at + width], ident_b[:], mask_qk[:],
                                  start=False, stop=True)

                    for j in range(2):
                        w = work_open(pe, f"mx{p}_{2 * j}", b)
                        tile(w, 0, j, 0)
                        tile(w, P, j, 2).then_inc(full_of(f"mx{p}_{2 * j}"), 1)
                        w = work_open(pe, f"mx{p}_{2 * j + 1}", b)
                        tile(w, 0, j, 3).then_inc(full_of(f"mx{p}_{2 * j + 1}"), 1)
                    w = work_open(pe, f"mx{p}_4", b)
                    tile(w, 0, 0, 1)
                    tile(w, 2 * P, 1, 1).then_inc(full_of(f"mx{p}_4"), 1)

                def max_transposed(p):
                    pe.wait_ge(negmax_ready, b * PAIRS + p + 1)
                    w = work_open(pe, f"mT{p}", b)
                    for qt in range(TILES):
                        last = mm(w[D1:D1 + 4, qt * P:(qt + 1) * P], neg_max_hl[:, qt, :],
                                  ident_b[:], start=True, stop=True)
                    last.then_inc(full_of(f"mT{p}"), 1)

                def key_block(dst, p, j, kb):
                    s = 2 * (p % 2) + j
                    keys, queries = slice(kb * P, (kb + 1) * P), slice(kb * P, SEQ)
                    mm(dst, ka1[:, s, keys], qa1[:, s, queries], start=True, stop=False)
                    mm(dst, kb1[0:D1 + 4, s, keys], qb1[0:D1 + 4, s, queries], start=False,
                       stop=False)
                    return mm(dst[:, 0:P], ident_b[:], mask_kq[:], start=False, stop=True)

                def main_unit(p, j):
                    u = UNIT_A1 + 3 * p + j
                    pe.wait_ge(score_done, b * UNITS + u + 1)
                    d = unit_slot(u)
                    key_block(d[:, 0:4 * P], p, j, 0)
                    key_block(d[:, 4 * P:7 * P], p, j, 1)
                    key_block(d[:, 7 * P:8 * P], p, j, 3).then_inc(score_full, 1)

                def rest_unit(p):
                    u = UNIT_A1 + 3 * p + 2
                    pe.wait_ge(score_done, b * UNITS + u + 1)
                    d = unit_slot(u)
                    key_block(d[:, 0:2 * P], p, 0, 2)
                    key_block(d[:, 2 * P:4 * P], p, 1, 2).then_inc(score_full, 1)

                def values1(p):
                    pe.wait_ge(out_free[0], b * OUT_PER + OUT_A1 + p + 1)
                    pe.wait_ge(score_done, b * UNITS + UNIT_A1 + 3 * p + 3 + 2)
                    blocks = [(0, lambda j: prob1_main(p, j)[:, 0:4 * P]),
                              (1, lambda j: prob1_main(p, j)[:, 4 * P:7 * P]),
                              (3, lambda j: prob1_main(p, j)[:, 7 * P:8 * P]),
                              (2, lambda j: prob1_rest(p)[:, 2 * P * j:2 * P * (j + 1)])]
                    for n, (kb, probs) in enumerate(blocks):
                        for j in range(2):
                            h = 2 * p + j
                            last = mm(outs[D1 * j:D1 * (j + 1), 0, kb * P:],
                                      v1[:, kb, h * D1:(h + 1) * D1], probs(j), start=(n == 0),
                                      stop=(n == TILES - 1))
                    last.then_inc(out_full[0], 1)
                    pe.wait_ge(out_free[1], b * OUT_PER + OUT_A1 + p + 1)
                    pe.wait_ge(tsum_ready, (b * PAIRS + p + 1) * 2)
                    for j in range(2):
                        mm(outs[D1 * j:D1 * (j + 1), 1, 0:P], ones[:], prob1_main(p, j)[:, 0:P],
                           start=True, stop=True)
                    for j in range(2):
                        last = mm(outs[D1 * j:D1 * (j + 1), 1, P:], ones[:], tsum(p, j),
                                  start=True, stop=True)
                    last.then_inc(out_full[1], 1)

                for p in range(2):
                    project(f"q{p}", 0, p)
                    project(f"k{p}", 1, p)
                max_scores(0)
                max_transposed(0)
                for p in range(PAIRS):
                    work_moved(pe, f"mT{p}", b)
                    main_unit(p, 0)
                    main_unit(p, 1)
                    rest_unit(p)
                    if p + 2 < PAIRS:
                        project(f"q{p + 2}", 0, p + 2)
                        project(f"k{p + 2}", 1, p + 2)
                    if p + 1 < PAIRS:
                        max_scores(p + 1)
                    if p >= 1:
                        values1(p - 1)
                    if p + 1 < PAIRS:
                        max_transposed(p + 1)
                values1(PAIRS - 1)
                pe.wait_ge(out_free[0], b * OUT_PER + OUT_A1 + PAIRS + 1)
                w = work_open(pe, "proj", b)
                for t in range(TILES):
                    cols = slice(t * P, (t + 1) * P)
                    for p in range(PAIRS):
                        last = mm(w[:, cols], yT[:, p, cols], wo_sb[:, p, :], start=(p == 0),
                                  stop=(p == PAIRS - 1))
                last.then_inc(full_of("proj"), 1)

                pe.wait_ge(rows_ready, b * 5 + 5)
                transposes("xnT", norm_a)
                work_moved(pe, "xnT", b)
                w = work_open(pe, "lg1", b)
                for t in range(TILES):
                    last = mm(w[:, t * EXPERTS:(t + 1) * EXPERTS], xT[:, t * P:(t + 1) * P],
                              wg1_sb[:], start=True, stop=True)
                last.then_inc(full_of("lg1"), 1)

                def hidden1(e):
                    for h in range(CH1 // 2):
                        u = UNIT_F1 + e * (CH1 // 2) + h
                        pe.wait_ge(score_done, b * UNITS + u + 1)
                        for c in range(2):
                            at = e * HID1 + (2 * h + c) * P
                            last = mm3(unit_slot(u)[:, c * SEQ:(c + 1) * SEQ],
                                       w1_hi[:, at:at + P], w1_lo[:, at:at + P], xT_hi[:],
                                       xT_lo[:])
                        last.then_inc(score_full, 1)

                def experts_out(e):
                    pe.wait_ge(out_free[e % 2], b * OUT_PER + OUT_F1 + e // 2 + 1)
                    pe.wait_ge(score_done,
                               b * UNITS + UNIT_F1 + (e + 1) * (CH1 // 2) + 2)
                    for t in range(TILES):
                        cols = slice(t * P, (t + 1) * P)
                        for c in range(CH1):
                            last = mm(outs[:, e % 2, cols], hid1T(e, c)[:, cols],
                                      w2_1_sb[:, e * CH1 + c, :], start=(c == 0),
                                      stop=(c == CH1 - 1))
                    last.then_inc(out_full[e % 2], 1)

                hidden1(0)
                pe.wait_ge(comb_ready, b + 1)
                w = work_open(pe, "cT", b)
                for t in range(TILES):
                    last = mm(w[0:EXPERTS, t * P:(t + 1) * P], comb[:, t, :], ident[:], start=True,
                              stop=True)
                last.then_inc(full_of("cT"), 1)
                work_moved(pe, "cT", b)
                w = work_open(pe, "b2", b)
                for t in range(TILES):
                    cols = slice(t * P, (t + 1) * P)
                    last = mm(w[:, cols], selT[:, cols], b2_1_sb[:], start=True, stop=True)
                last.then_inc(full_of("b2"), 1)
                for e in range(EXPERTS):
                    if e + 1 < EXPERTS:
                        hidden1(e + 1)
                    experts_out(e)
                if WORK[-1] == "pad":
                    w = work_open(pe, "pad", b)
                    mm(w[0:EXPERTS, 0:EXPERTS], ident_b[:, 0:EXPERTS], ident_b[:, 0:EXPERTS],
                       start=True, stop=True).then_inc(full_of("pad"), 1)


def kernel(L0_attn_x, L0_attn_Wq, L0_attn_Wk, L0_attn_Wv, L0_attn_g_scale, L0_ffn_Wg,
           L0_ffn_ln_scale, L0_ffn_ln_bias, L0_ffn_W1, L0_ffn_b1, L0_ffn_W2, L0_ffn_b2,
           L1_attn_w_q, L1_attn_w_k, L1_attn_w_v, L1_attn_w_o, L1_ffn_Wg, L1_ffn_bg, L1_ffn_W1,
           L1_ffn_b1, L1_ffn_W2, L1_ffn_b2, L1_ffn_gamma, L1_ffn_beta):
    import concourse.bacc as bacc
    from concourse.bass_utils import run_bass_kernel_spmd

    def rows(a):
        return np.asarray(a).reshape(-1, P, a.shape[-1]).transpose(1, 0, 2)

    def flat(a):
        return np.asarray(a).reshape(-1, DIM).T

    ins = {
        "x": np.asarray(L0_attn_x).reshape(BATCH, TILES, P, DIM).transpose(0, 2, 1, 3),
        "wqkv0": np.concatenate([np.asarray(w).T for w in (L0_attn_Wq, L0_attn_Wk, L0_attn_Wv)], 1),
        "g_scale": np.asarray(L0_attn_g_scale).reshape(1, 1),
        "wg0": np.asarray(L0_ffn_Wg).T,
        "s0": np.asarray(L0_ffn_ln_scale).T,
        "bias_ln0": np.asarray(L0_ffn_ln_bias).T,
        "w1_0": np.asarray(L0_ffn_W1).transpose(1, 0, 2).reshape(DIM, EXPERTS * HID0),
        "b1_0": np.asarray(L0_ffn_b1).reshape(CH0, P).T,
        "w2_0": rows(np.asarray(L0_ffn_W2).reshape(EXPERTS * HID0, DIM)),
        "b2_0": np.asarray(L0_ffn_b2),
        "wq1": flat(L1_attn_w_q),
        "wk1": flat(L1_attn_w_k),
        "wv1": flat(L1_attn_w_v),
        "wo1": rows(np.asarray(L1_attn_w_o)),
        "wg1": np.asarray(L1_ffn_Wg),
        "bg1": np.asarray(L1_ffn_bg).reshape(1, EXPERTS),
        "w1_1": np.asarray(L1_ffn_W1).transpose(1, 0, 2).reshape(DIM, EXPERTS * HID1),
        "b1_1": np.asarray(L1_ffn_b1).reshape(EXPERTS * CH1, P).T,
        "w2_1": rows(np.asarray(L1_ffn_W2).reshape(EXPERTS * HID1, DIM)),
        "b2_1": np.asarray(L1_ffn_b2),
        "gamma": np.asarray(L1_ffn_gamma).reshape(1, DIM),
        "beta": np.asarray(L1_ffn_beta).reshape(1, DIM),
    }
    ins = {name: np.ascontiguousarray(a) for name, a in ins.items()}
    nc = bacc.Bacc("TRN2", target_bir_lowering=False, num_devices=1)
    drams = [nc.dram_tensor(f"in_{name}", a.shape, mybir.dt.from_np(a.dtype),
                            kind="ExternalInput").ap() for name, a in ins.items()]
    out = nc.dram_tensor("out", (BATCH, P, TILES, DIM), F32, kind="ExternalOutput").ap()
    layers_kernel(nc, *drams, out)
    got = run_bass_kernel_spmd(nc, [{f"in_{name}": a for name, a in ins.items()}], core_ids=[0])
    y = got.results[0]["out"]
    return y.transpose(0, 2, 1, 3).reshape(BATCH, SEQ, DIM)
```

```python
import numpy as np
from contextlib import ExitStack

import concourse.bass as bass
from concourse import mybir

F32 = mybir.dt.float32
F32R = mybir.dt.float32r
BF16 = mybir.dt.bfloat16
ALU = mybir.AluOpType
ACT = mybir.ActivationFunctionType
AX = mybir.AxisListType

P = 128
BATCH, SEQ, DIM = 8, 512, 128
TILES = SEQ // P
EXPERTS = 8
LN_EPS = 1e-5
L2_EPS = 1e-12
MASKED = -1e30

H0 = 16
D0 = DIM // H0
HG = 4
GROUPS0 = H0 // HG
STRIP = 32
TERMS = 4
STEPS0 = GROUPS0 * TILES
HID0 = 32
CH0 = EXPERTS * HID0 // P
H1 = 16
D1 = 64
PAIRS = H1 // 2
SCALE1 = 1.0 / D1 ** 0.5
HID1 = 512
CH1 = HID1 // P

SKEW = 2


def work_order(l1, f0, a0):
    names = []
    if l1:
        names += ["x2T"] + [f"v{t}_{n}" for t in range(TILES) for n in range(2)]
        names += ["q0", "k0", "q1", "k1"] + [f"mx0_{i}" for i in range(5)] + ["mT0"]
    for p in range(PAIRS):
        if l1 and p + 1 < PAIRS:
            names += [f"mx{p + 1}_{i}" for i in range(5)]
        if l1 and p + 2 < PAIRS:
            names += [f"q{p + 2}"]
        if l1 and p + 1 < PAIRS:
            names += [f"mT{p + 1}"]
        if l1 and p + 2 < PAIRS:
            names += [f"k{p + 2}"]
        if a0:
            names += {2: ["xT0_0", "xT0_1"], 3: [f"qkv0_{t}" for t in range(TILES)]}.get(p, [])
        if f0:
            names += {3: ["xtT"], 4: ["lg0", "xh2T"], 6: ["ohT"]}.get(p, [])
    names += ["qT0", "kT0"] if a0 else []
    names += ["hid0_0", "hid0_1"] if f0 else []
    names += ["proj"] if l1 else []
    names += ["mask0", "mask1"] if f0 else []
    names += ["xnT", "lg1"] if l1 else []
    names += ["y0_0", "y0_1"] if f0 else []
    for k in range(GROUPS0):
        names += ["cT", "b2"] if l1 and k == 0 else []
        names += [f"oT{k - 1}"] if a0 and k else []
        names += [f"qT{k + 1}", f"kT{k + 1}"] if a0 and k + 1 < GROUPS0 else []
    names += [f"oT{GROUPS0 - 1}"] if a0 else []
    assert len(names) % 2 == 0
    return names


def unit_order(l1, a0):
    units = [("pair", p, i) for p in range(PAIRS) for i in range(3)] if l1 else []
    for k in range(GROUPS0):
        units += [("hidden", e, h) for e in (2 * k, 2 * k + 1) for h in range(CH1 // 2)] if l1 else []
        units += [("cosine", n, i) for n in range(TILES * k, TILES * (k + 1))
                  for i in range(2)] if a0 else []
    assert len(units) % 2 == 0
    return units


class Pass:

    def __init__(self, l1, f0, a0, work, units, sums):
        self.l1, self.f0, self.a0 = l1, f0, a0
        here = [x is not None for x in (l1, f0, a0)]
        self.work_no = {n: i for i, n in enumerate(work_order(*here))}
        self.unit_no = {u: i for i, u in enumerate(unit_order(here[0], here[2]))}
        self.work, self.units, self.sums = work, units, sums
        self.next = (work + len(self.work_no) // 2, units + len(self.unit_no),
                     sums + (PAIRS if here[0] else 0) + (GROUPS0 if here[2] else 0))


def passes(eng):
    def at(i, before):
        batch = [i + n if 0 <= i + n < BATCH else None for n in range(SKEW + 1)]
        return Pass(*batch, *before)

    before = (0, 0, 0)
    for i in range(-SKEW, 0):
        one = at(i, before)
        yield one
        before = one.next
    step = [b - a for a, b in zip(before, at(0, before).next)]
    with eng.Fori(0, BATCH - SKEW) as i:
        yield Pass(i, i + 1, i + 2, *(a + i * d for a, d in zip(before, step)))
    before = tuple(a + (BATCH - SKEW) * d for a, d in zip(before, step))
    for i in range(BATCH - SKEW, BATCH):
        one = at(i, before)
        yield one
        before = one.next


OUT0 = PAIRS + EXPERTS

PROB0 = 0
PROB0_SLOTS = 3
HIDT = PROB0_SLOTS * HG * SEQ
V1 = 0
PROB1 = V1 + TILES * H1 * D1
PROB1_PAIR = 2 * 1024 + 512
TSUM = PROB1 + 2 * PROB1_PAIR
BIG = max(TSUM + 2 * 384, HIDT + 2 * CH1 * SEQ)

LOOP_LINKS = 72


def layers_kernel(nc, x, wqkv0, g_scale, wg0, s0, bias_ln0, w1_0, b1_0, w2_0, b2_0,
                  wq1, wk1, wv1, wo1, wg1, bg1, w1_1, b1_1, w2_1, b2_1, gamma, beta, out):
    ctx = ExitStack()
    with ctx:
        def sb(name, shape, dt=F32):
            return ctx.enter_context(nc.sbuf_tensor(name, shape, dt))

        def sem(name):
            return ctx.enter_context(nc.semaphore(name))

        ident_r = sb("ident_r", [P, P], F32R)
        ident = ident_r[:].bitcast(F32)
        ident_b = sb("ident_b", [P, P], BF16)
        mask_qk = sb("mask_qk", [P, P], BF16)
        mask_kq = sb("mask_kq", [P, P], BF16)
        ones = sb("ones", [P, D1])
        rank = sb("rank", [P, EXPERTS])
        head_sel = sb("head_sel", [P, 2, 1])
        wqkv0_sb = sb("wqkv0_sb", [P, 3 * DIM])
        g_sb = sb("g_sb", [P, 1])
        wg0_sb = sb("wg0_sb", [P, EXPERTS])
        s0_sb = sb("s0_sb", [P, EXPERTS])
        bias_ln0_sb = sb("bias_ln0_sb", [P, EXPERTS])
        w1s0 = sb("w1s0", [P, EXPERTS * HID0])
        b1_0_sb = sb("b1_0_sb", [P, CH0])
        bias0 = sb("bias0", [P, CH0])
        w2_0_sb = sb("w2_0_sb", [P, CH0, DIM])
        b2_0_sb = sb("b2_0_sb", [EXPERTS, DIM])
        wqkv1_hi = sb("wqkv1_hi", [P, 3, H1 * D1], F32R)
        wqkv1_lo = sb("wqkv1_lo", [P, 3, H1 * D1], F32R)
        wo_sb = sb("wo_sb", [P, PAIRS, DIM])
        wg1_sb = sb("wg1_sb", [P, EXPERTS])
        bg1_sb = sb("bg1_sb", [P, EXPERTS])
        w1_hi = sb("w1_hi", [P, EXPERTS * HID1], F32R)
        w1_lo = sb("w1_lo", [P, EXPERTS * HID1], F32R)
        b1_1_sb = sb("b1_1_sb", [P, EXPERTS * CH1])
        w2_1_sb = sb("w2_1_sb", [P, EXPERTS * CH1, DIM])
        b2_1_sb = sb("b2_1_sb", [EXPERTS, DIM])
        gamma_sb = sb("gamma_sb", [P, DIM])
        beta_sb = sb("beta_sb", [P, DIM])

        x_in = sb("x_in", [P, TILES, DIM])
        res0 = sb("res0", [P, TILES, DIM])
        res1 = sb("res1", [P, TILES, DIM])
        rows_a = sb("rows_a", [P, TILES, DIM])
        rows_b = sb("rows_b", [P, TILES, DIM])
        xT_a = sb("xT_a", [P, SEQ])
        xT_b = sb("xT_b", [P, SEQ])
        xT1 = sb("xT1", [P, SEQ])
        xT_hi = sb("xT_hi", [P, SEQ], F32R)
        xT_lo = sb("xT_lo", [P, SEQ], F32R)
        stats = sb("stats", [P, TILES, 6])
        mean = sb("mean", [P, TILES])
        halves = sb("halves", [P, TILES])
        var_eps = sb("var_eps", [P, TILES])
        minus_half = sb("minus_half", [P, TILES])
        rstd = sb("rstd", [P, TILES])
        inv_norm = sb("inv_norm", [P, 2 * TILES * H0])
        qk_sb = sb("qk_sb", [P, 2 * TILES * DIM])
        vstat = sb("vstat", [P, TILES, H0, STRIP])
        oT_sb = sb("oT_sb", [P, SEQ])
        rsum0 = sb("rsum0", [P, TILES * HG])
        lg = sb("lg", [P, TILES, EXPERTS])
        lg2 = sb("lg2", [P, TILES, EXPERTS])
        eq = sb("eq", [P, TILES, EXPERTS])
        oh1 = sb("oh1", [P, TILES, EXPERTS])
        oh2 = sb("oh2", [P, TILES, EXPERTS])
        comb = sb("comb", [P, TILES, EXPERTS])
        top1 = sb("top1", [P, TILES])
        top2 = sb("top2", [P, TILES])
        best = sb("best", [P, TILES])
        gap = sb("gap", [P, TILES])
        eg = sb("eg", [P, TILES])
        sc1 = sb("sc1", [P, TILES])
        sc2 = sb("sc2", [P, TILES])
        neg_max = sb("neg_max", [P, TILES, 2])
        neg_max_hl = sb("neg_max_hl", [P, TILES, 4], BF16)
        ra = sb("ra", [P, 8 * SEQ], F32R)
        rb = sb("rb", [P, 8 * SEQ], F32R)
        big = sb("big", [P, BIG])
        g_buf = sb("g_buf", [P, PAIRS, SEQ])
        yT = g_buf
        x3, xn, acc, result, attn0 = (g_buf[:, n, :].rearrange("p (t d) -> p t d", t=TILES)
                                      for n in range(5))
        norms = rows_a[:, :, :].rearrange("p t d -> p (t d)")
        N_LEN = 2 * TILES * H0
        sq_tile = norms[:, 0:2 * DIM]
        sum_sq = norms[:, 2 * DIM:2 * DIM + N_LEN]
        newton = norms[:, 2 * DIM + N_LEN:2 * DIM + 2 * N_LEN]
        mask_f = rows_a[:, 0:2, :]
        ident_f = rows_a[:, 2, :]
        ohx = rows_b[:, :, :].bitcast(BF16).rearrange("p t (e h) -> p t e h", e=EXPERTS)
        w1raw0 = xT_a[:, 0:EXPERTS * HID0]
        selT0 = xT_b[0:EXPERTS, :]
        selT1 = xT1[0:EXPERTS, :]
        lnsum = xT1
        rsum1 = oT_sb
        parts = ra[:, :].rearrange("p (w t h r d) -> p w t h r d", w=2, t=TILES, h=H0, r=TERMS)
        qkT0 = rb[:, :].rearrange("p (w g n) -> p w g n", w=2, g=GROUPS0)
        qa1 = ra[:, 0:4 * SEQ].rearrange("p (s n) -> p s n", s=4)
        ka1 = ra[:, 4 * SEQ:8 * SEQ].rearrange("p (s n) -> p s n", s=4)
        qb1 = rb[:, 0:4 * SEQ].rearrange("p (s n) -> p s n", s=4)
        kb1 = rb[:, 4 * SEQ:8 * SEQ].rearrange("p (s n) -> p s n", s=4)
        v1 = big[:, V1:PROB1].rearrange("p (t n) -> p t n", t=TILES)
        hid0T = big[:, 0:CH0 * SEQ].rearrange("p (c n) -> p c n", c=CH0)
        stage_qkv1 = big[:, 0:3 * H1 * D1]
        stage_w1 = big[:, 3 * H1 * D1:3 * H1 * D1 + EXPERTS * HID1]

        def prob0(n):
            at = PROB0 + (n % PROB0_SLOTS) * HG * SEQ
            return big[:, at:at + HG * SEQ]

        def prob1_main(p, j):
            at = PROB1 + (p % 2) * PROB1_PAIR + j * 1024
            return big[:, at:at + 1024]

        def prob1_rest(p):
            at = PROB1 + (p % 2) * PROB1_PAIR + 2048
            return big[:, at:at + 512]

        def tsum(j):
            at = TSUM + j * 384
            return big[:, at:at + 384]

        def hid1T(e, c):
            at = HIDT + ((e % 2) * CH1 + c) * SEQ
            return big[:, at:at + SEQ]

        scores = ctx.enter_context(nc.psum_tensor("scores", [P, 2, 1024], F32))
        outs = ctx.enter_context(nc.psum_tensor("outs", [P, 2, SEQ], F32))
        work = ctx.enter_context(nc.psum_tensor("work", [P, 2, SEQ], F32))

        weights_in = sem("weights_in")
        consts = sem("consts")
        const_step = sem("const_step")
        weights_hi = sem("weights_hi")
        weights_ready = sem("weights_ready")
        fold_ready = sem("fold_ready")
        x_loaded = sem("x_loaded")
        x_taken = sem("x_taken")
        out_sent = sem("out_sent")
        out_ready = sem("out_ready")
        streams = ("a0", "f0", "l1")
        var_ready = {n: sem(f"var_ready_{n}") for n in streams}
        rstd_ready = {n: sem(f"rstd_ready_{n}") for n in streams}
        rows_ready = {n: sem(f"rows_ready_{n}") for n in streams}
        sumsq_ready = sem("sumsq_ready")
        ln_done = sem("ln_done")
        invn_ready = sem("invn_ready")
        qkn_ready = sem("qkn_ready")
        parts_hi = sem("parts_hi")
        parts_ready = sem("parts_ready")
        pv0_done = sem("pv0_done")
        onehot_ready = sem("onehot_ready")
        hid0m_ready = sem("hid0m_ready")
        x_hi = sem("x_hi")
        qk1_hi = sem("qk1_hi")
        negmax_ready = sem("negmax_ready")
        tsum_ready = sem("tsum_ready")
        tsum_step = sem("tsum_step")
        rsum1_ready = sem("rsum1_ready")
        gap_ready = sem("gap_ready")
        eg_ready = sem("eg_ready")
        comb_ready = sem("comb_ready")
        dve_step = sem("dve_step")
        score_full = sem("score_full")
        score_done = sem("score_done")
        out_full = [sem(f"out_full{i}") for i in range(2)]
        out_free = [sem(f"out_free{i}") for i in range(2)]
        work_full = [sem(f"work_full{i}") for i in range(2)]
        work_free = [sem(f"work_free{i}") for i in range(2)]

        block = ctx.enter_context(nc.Block())

        def bank_no(o, name):
            return o.work_no[name] % 2

        def work_bank(o, name):
            return work[:, bank_no(o, name), :]

        def work_fills(o, name):
            return o.work + (o.work_no[name] // 2 + 1)

        def work_open(pe, o, name):
            pe.wait_ge(work_free[bank_no(o, name)], work_fills(o, name))
            return work_bank(o, name)

        def work_wait(eng, o, name):
            eng.wait_ge(work_full[bank_no(o, name)], work_fills(o, name))
            return work_bank(o, name)

        def work_moved(eng, o, name):
            eng.wait_ge(work_free[bank_no(o, name)], work_fills(o, name) + 1)

        def full_of(o, name):
            return work_full[bank_no(o, name)]

        def free_of(o, name):
            return work_free[bank_no(o, name)]

        def unit_slot(o, *unit):
            return scores[:, o.unit_no[unit] % 2, :]

        def unit_open(pe, o, *unit):
            pe.wait_ge(score_done, o.units + (o.unit_no[unit] + 1))
            return unit_slot(o, *unit)

        def unit_wait(act, o, *unit):
            act.wait_ge(score_full, o.units + (o.unit_no[unit] + 1))
            return unit_slot(o, *unit)

        def unit_done(eng, o, *unit):
            eng.wait_ge(score_done, o.units + (o.unit_no[unit] + 3))

        def out0(o, n):
            return o.l1 * OUT0 + (n + 1)

        def sums_no(o, p):
            return o.sums + (p + 1)

        def group_no(o, g):
            return o.sums + ((PAIRS if o.l1 is not None else 0) + g + 1)

        N_WEIGHTS = 20

        @block.sync
        def _(sp):
            for dst, src in ((wqkv0_sb[:], wqkv0), (g_sb[:], g_scale.to_broadcast([P, 1])),
                             (wg0_sb[:], wg0), (s0_sb[:], s0), (bias_ln0_sb[:], bias_ln0),
                             (w1raw0[:], w1_0), (b1_0_sb[:], b1_0),
                             (stage_qkv1[:, 0:H1 * D1], wq1),
                             (stage_qkv1[:, H1 * D1:2 * H1 * D1], wk1),
                             (stage_qkv1[:, 2 * H1 * D1:], wv1), (stage_w1, w1_1),
                             (w2_0_sb[:], w2_0), (b2_0_sb[:], b2_0), (wo_sb[:], wo1),
                             (wg1_sb[:], wg1), (bg1_sb[:], bg1.to_broadcast([P, EXPERTS])),
                             (b1_1_sb[:], b1_1), (w2_1_sb[:], w2_1), (b2_1_sb[:], b2_1),
                             (gamma_sb[:], gamma.to_broadcast([P, DIM]))):
                sp.dma_start(dst, src).then_inc(weights_in, 16)
            sp.dma_start(x_in[:], x[0]).then_inc(x_loaded, 16)
            sp.dma_start(beta_sb[:], beta.to_broadcast([P, DIM])).then_inc(out_sent, 16)
            for a in range(1, SKEW + 1):
                sp.wait_ge(x_taken, a)
                sp.dma_start(x_in[:], x[a]).then_inc(x_loaded, 16)
            with sp.Fori(0, BATCH - SKEW - 1) as b:
                sp.wait_ge(x_taken, b + SKEW + 1)
                sp.dma_start(x_in[:], x[bass.ds(b + SKEW + 1, 1)]).then_inc(x_loaded, 16)
                sp.wait_ge(out_ready, b + 1)
                sp.dma_start(out[bass.ds(b, 1)], result).then_inc(out_sent, 16)
            for b in range(BATCH - SKEW - 1, BATCH):
                sp.wait_ge(out_ready, b + 1)
                sp.dma_start(out[b], result).then_inc(out_sent, 16)
            sp.wait_ge(out_sent, 16 * (BATCH + 1))

        @block.gpsimd
        def _(pool):
            nc.gpsimd.memset(ident_f, 0.0).then_inc(const_step, 1)
            nc.gpsimd.memset(mask_f, 0.0).then_inc(const_step, 1)
            nc.gpsimd.memset(head_sel[:], 0.0).then_inc(const_step, 1)
            nc.gpsimd.memset(ones[:], 1.0)
            nc.gpsimd.memset(minus_half[:], -0.5)
            nc.gpsimd.iota(rank[:], pattern=[[-1, EXPERTS]], base=EXPERTS, channel_multiplier=0,
                           allow_small_or_imprecise_dtypes=True)
            pool.wait_ge(const_step, 3)
            nc.gpsimd.affine_select(out=ident_f, in_=ident_f, compare_op=ALU.not_equal, fill=1.0,
                                    base=0, pattern=[[-1, P]], channel_multiplier=1)
            nc.gpsimd.affine_select(out=mask_f[:, 0, :], in_=mask_f[:, 0, :], compare_op=ALU.is_ge,
                                    fill=MASKED, base=0, pattern=[[-1, P]], channel_multiplier=1)
            nc.gpsimd.affine_select(out=mask_f[:, 1, :], in_=mask_f[:, 1, :], compare_op=ALU.is_ge,
                                    fill=MASKED, base=0, pattern=[[1, P]],
                                    channel_multiplier=-1).then_inc(const_step, 1)
            pool.wait_ge(const_step, 4)
            sel = head_sel[D1:D1 + 4, :, 0]
            nc.gpsimd.affine_select(out=sel, in_=sel, compare_op=ALU.not_equal, fill=1.0, base=0,
                                    pattern=[[-1, 2]], channel_multiplier=1).then_inc(const_step, 1)
            pool.wait_ge(const_step, 5)
            nc.gpsimd.affine_select(out=sel, in_=sel, compare_op=ALU.not_equal, fill=1.0, base=-2,
                                    pattern=[[-1, 2]], channel_multiplier=1).then_inc(consts, 1)

            def inverse_deviations(stream, n):
                pool.wait_ge(var_ready[stream], n + 1)
                nc.gpsimd.tensor_tensor(rstd[:], var_eps[:], minus_half[:],
                                        ALU.pow).then_inc(rstd_ready[stream], 1)

            def sum_blocks(o, p):
                unit_done(pool, o, "pair", p, 2)
                for j in range(2):
                    m, r = prob1_main(p, j), prob1_rest(p)
                    t = tsum(j)
                    first = o.l1 * (4 * PAIRS) + (4 * p + 2 * j + 1)
                    if j == 0 and p:
                        pool.wait_ge(out_full[1], sums_no(o, p - 1))
                    nc.gpsimd.tensor_tensor(t, m[:, P:SEQ], m[:, SEQ:SEQ + 3 * P],
                                            ALU.add).then_inc(tsum_step, 1)
                    pool.wait_ge(tsum_step, first)
                    nc.gpsimd.tensor_tensor(t[:, P:3 * P], t[:, P:3 * P],
                                            r[:, 2 * P * j:2 * P * (j + 1)],
                                            ALU.add).then_inc(tsum_step, 1)
                    pool.wait_ge(tsum_step, first + 1)
                    nc.gpsimd.tensor_tensor(t[:, 2 * P:3 * P], t[:, 2 * P:3 * P],
                                            m[:, 7 * P:8 * P], ALU.add).then_inc(tsum_ready, 1)

            for o in passes(pool):
                for p in range(PAIRS):
                    if o.l1 is not None:
                        sum_blocks(o, p)
                    if p == 0 and o.a0 is not None:
                        inverse_deviations("a0", o.a0)
                    if p in (1, 2) and o.f0 is not None:
                        inverse_deviations("f0", o.f0 * 3 + (p - 1))
                if o.l1 is not None:
                    inverse_deviations("l1", o.l1 * 2)
                if o.f0 is not None:
                    inverse_deviations("f0", o.f0 * 3 + 2)
                if o.l1 is not None:
                    inverse_deviations("l1", o.l1 * 2 + 1)

        @block.scalar
        def _(act):
            copy, activation = nc.scalar.copy, nc.scalar.activation
            act.wait_ge(consts, 1)
            copy(eg[:], minus_half[:]).then_inc(score_done, 2)
            act.wait_ge(weights_in, 16 * N_WEIGHTS)
            copy(wqkv1_hi[:].rearrange("p a n -> p (a n)"), stage_qkv1).then_inc(weights_hi, 1)
            copy(w1_hi[:], stage_w1).then_inc(weights_hi, 1)

            def exp_tables():
                nc.scalar.preload_act_table_set("natural_log_exp_and_others")

            def hi_q(o, p):
                w = work_wait(act, o, f"q{p}")
                for j in range(2):
                    slot = 2 * (p % 2) + j
                    copy(qb1[0:D1, slot, :], w[j * D1:(j + 1) * D1, :])
                    last = copy(qa1[0:D1, slot, :], w[j * D1:(j + 1) * D1, :])
                last.then_inc(qk1_hi, 1)

            def hi_k(o, p):
                w = work_wait(act, o, f"k{p}")
                for j in range(2):
                    last = copy(ka1[0:D1, 2 * (p % 2) + j, :], w[j * D1:(j + 1) * D1, :])
                last.then_inc(qk1_hi, 1)

            def max_rows(o, p):
                w = work_wait(act, o, f"mT{p}")
                for j in range(2):
                    last = copy(qb1[D1:D1 + 4, 2 * (p % 2) + j, :], w[D1:D1 + 4, :])
                last.then_inc(free_of(o, f"mT{p}"), 1)

            def inverse_sums(o, p):
                act.wait_ge(out_full[1], sums_no(o, p))
                activation(lnsum[:], outs[:, 1, :], ACT.Ln).then_inc(out_free[1], 1)
                act.wait_ge(out_free[1], sums_no(o, p) + 1)
                act.wait_ge(out_free[0], out0(o, p))
                activation(rsum1[:], lnsum[:], ACT.Exp, scale=-1.0).then_inc(rsum1_ready, 1)

            def attention1_head(o):
                w = work_wait(act, o, "x2T")
                copy(xT_hi[:], w).then_inc(x_hi, 1)
                for t in range(TILES):
                    w = work_wait(act, o, f"v{t}_0")
                    copy(v1[:, t, 0:SEQ], w).then_inc(free_of(o, f"v{t}_0"), 1)
                for p in range(2):
                    hi_q(o, p)
                    hi_k(o, p)
                max_rows(o, 0)

            def pair_step(o, p):
                for j in range(2):
                    activation(prob1_main(p, j), unit_wait(act, o, "pair", p, j), ACT.Exp,
                               scale=SCALE1).then_inc(score_done, 1)
                activation(prob1_rest(p), unit_wait(act, o, "pair", p, 2)[:, 0:512], ACT.Exp,
                           scale=SCALE1).then_inc(score_done, 1)
                if p + 2 < PAIRS:
                    hi_q(o, p + 2)
                if p + 1 < PAIRS:
                    max_rows(o, p + 1)
                if p + 2 < PAIRS:
                    hi_k(o, p + 2)
                if p >= 1:
                    inverse_sums(o, p - 1)

            def attention0_head(o, p):
                if p == 2:
                    for i in range(2):
                        w = work_wait(act, o, f"xT0_{i}")
                        half = slice(i * 2 * P, (i + 1) * 2 * P)
                        copy(xT_a[:, half], w[:, 0:2 * P]).then_inc(free_of(o, f"xT0_{i}"), 1)
                if p == 3:
                    for t in range(TILES):
                        w = work_wait(act, o, f"qkv0_{t}")
                        copy(qk_sb[:].rearrange("p (w t n) -> p w t n", w=2, t=TILES)[:, :, t, :],
                             w[:, 0:2 * DIM].rearrange("p (w n) -> p w n", w=2))
                        copy(vstat[:, t, :, 0:D0],
                             w[:, 2 * DIM:3 * DIM].rearrange("p (h d) -> p h d", d=D0)
                             ).then_inc(free_of(o, f"qkv0_{t}"), 1)
                if p == 5:
                    act.wait_ge(sumsq_ready, o.a0 + 1)
                    activation(newton, sum_sq, ACT.Ln).then_inc(ln_done, 1)
                    act.wait_ge(ln_done, o.a0 + 1)
                    activation(inv_norm[:], newton, ACT.Exp, scale=-0.5).then_inc(invn_ready, 1)

            def experts0(o, p):
                if p == 3:
                    w = work_wait(act, o, "xtT")
                    copy(xT_b[:], w).then_inc(free_of(o, "xtT"), 1)
                if p == 6:
                    w = work_wait(act, o, "ohT")
                    copy(selT0, w[0:EXPERTS, :]).then_inc(free_of(o, "ohT"), 1)

            def hi_parts(o):
                act.wait_ge(qkn_ready, o.a0 + 1)
                n4 = qk_sb[:].rearrange("p (w n d) -> p w n d", w=2, d=D0)
                for w_, sl in ((0, slice(0, 2)), (1, slice(0, 3, 2))):
                    dst = parts[:, w_].rearrange("p t h r d -> p (t h) r d")[:, :, sl, :]
                    last = copy(dst, n4[:, w_].unsqueeze(2).broadcast_to([P, TILES * H0, 2, D0]))
                last.then_inc(parts_hi, 1)

            def hidden_gelu(o, e):
                if e >= 2:
                    act.wait_ge(out_full[0], out0(o, PAIRS + e - 2))
                for h in range(CH1 // 2):
                    w = unit_wait(act, o, "hidden", e, h)
                    for c in range(2):
                        ch = e * CH1 + 2 * h + c
                        last = activation(hid1T(e, 2 * h + c), w[:, c * SEQ:(c + 1) * SEQ],
                                          ACT.Gelu, bias=b1_1_sb[:, ch:ch + 1])
                    last.then_inc(score_done, 1)

            def cosine_exp(o, n):
                if n >= PROB0_SLOTS:
                    g, kb = (n - PROB0_SLOTS) // TILES, (n - PROB0_SLOTS) % TILES
                    if kb == TILES - 1:
                        act.wait_ge(out_full[1], group_no(o, g))
                    else:
                        act.wait_ge(pv0_done, (o.a0 * GROUPS0 + g) * (TILES - 1) + (kb + 1))
                for i in range(2):
                    activation(prob0(n)[:, i * 1024:(i + 1) * 1024],
                               unit_wait(act, o, "cosine", n, i),
                               ACT.Exp).then_inc(score_done, 1)

            act.wait_ge(weights_ready, 1)
            for o in passes(act):
                exp_tables()
                if o.l1 is not None:
                    attention1_head(o)
                for p in range(PAIRS):
                    if o.l1 is not None:
                        pair_step(o, p)
                    if o.a0 is not None:
                        attention0_head(o, p)
                    if o.f0 is not None:
                        experts0(o, p)
                if o.a0 is not None:
                    hi_parts(o)
                if o.l1 is not None:
                    inverse_sums(o, PAIRS - 1)
                if o.f0 is not None:
                    if o.l1 is not None:
                        act.wait_ge(out_full[0], out0(o, PAIRS - 1))
                    for c in range(CH0):
                        w = work_wait(act, o, f"hid0_{c}")
                        activation(hid0T[:, c, :], w, ACT.Gelu,
                                   bias=bias0[:, c:c + 1]).then_inc(free_of(o, f"hid0_{c}"), 1)
                if o.l1 is not None:
                    w = work_wait(act, o, "xnT")
                    copy(xT1[:], w)
                    copy(xT_hi[:], w).then_inc(x_hi, 1)
                for k in range(GROUPS0):
                    if o.l1 is not None:
                        hidden_gelu(o, 2 * k)
                        hidden_gelu(o, 2 * k + 1)
                    if o.l1 is not None and k == 0:
                        exp_tables()
                        act.wait_ge(gap_ready, o.l1 + 1)
                        activation(eg[:], gap[:], ACT.Exp).then_inc(eg_ready, 1)
                    if o.a0 is not None:
                        exp_tables()
                        for m in range(TILES):
                            cosine_exp(o, TILES * k + m)

        @block.vector
        def _(dve):
            v = nc.vector
            dve.wait_ge(weights_in, 16 * N_WEIGHTS)
            dve.wait_ge(consts, 1)
            v.memset(vstat[:], 0.0).then_inc(dve_step, 1)
            v.tensor_copy(ident_b[:], ident_f).then_inc(work_free[0], 1)
            v.tensor_copy(ident_r[:], ident_f).then_inc(work_free[1], 1)
            v.tensor_copy(mask_qk[:], mask_f[:, 0, :]).then_inc(out_free[0], 1)
            v.tensor_copy(mask_kq[:], mask_f[:, 1, :]).then_inc(out_free[1], 1)
            v.tensor_tensor(w1s0[:].rearrange("p (e h) -> p e h", h=HID0),
                            w1raw0.rearrange("p (e h) -> p e h", h=HID0),
                            s0_sb[:].unsqueeze(2).broadcast_to([P, EXPERTS, HID0]), ALU.mult)
            dve.wait_ge(dve_step, 1)
            v.memset(vstat[:, :, :, D0:D0 + 1], 1.0)
            dve.wait_ge(fold_ready, 1)
            for c in range(CH0):
                for j in range(P // HID0):
                    e = c * (P // HID0) + j
                    rows = slice(j * HID0, (j + 1) * HID0)
                    v.tensor_tensor(bias0[rows, c:c + 1], outs[rows, 0, c * 8 + e:c * 8 + e + 1],
                                    b1_0_sb[rows, c:c + 1], ALU.add)
            dve.wait_ge(weights_hi, 2)
            v.tensor_tensor(wqkv1_lo[:].rearrange("p a n -> p (a n)"), stage_qkv1,
                            wqkv1_hi[:].bitcast(F32).rearrange("p a n -> p (a n)"), ALU.subtract)
            v.tensor_tensor(w1_lo[:], stage_w1, w1_hi[:].bitcast(F32),
                            ALU.subtract).then_inc(weights_ready, 1)
            dve.wait_ge(weights_ready, 1)

            links = [1, 0]

            def link(ins):
                links[1] += 1
                ins.then_inc(dve_step, 1)
                dve.wait_ge(dve_step, links[0] + links[1])

            def variances(stream, src):
                for t in range(TILES):
                    last = v.bn_stats(stats[:, t, :], src[:, t, :])
                link(last)
                v.tensor_tensor(mean[:], stats[:, :, 1], stats[:, :, 4], ALU.add)
                v.tensor_tensor(var_eps[:], stats[:, :, 2], stats[:, :, 5], ALU.add)
                link(v.tensor_tensor(halves[:], stats[:, :, 1], stats[:, :, 4], ALU.subtract))
                v.tensor_scalar(mean[:], mean[:], 0.5, None, ALU.mult)
                link(v.tensor_tensor(halves[:], halves[:], halves[:], ALU.mult))
                link(v.scalar_tensor_tensor(var_eps[:], halves[:], DIM / 4.0, var_eps[:],
                                            ALU.mult, ALU.add))
                v.tensor_scalar(var_eps[:], var_eps[:], 1.0 / DIM, LN_EPS, ALU.mult,
                                ALU.add).then_inc(var_ready[stream], 1)

            def standardize(stream, n, src, dst):
                dve.wait_ge(rstd_ready[stream], n + 1)
                for t in range(TILES):
                    last = v.tensor_scalar(dst[:, t, :], src[:, t, :], mean[:, t:t + 1],
                                           rstd[:, t:t + 1], ALU.subtract, ALU.mult)
                return last

            wide = [P, TILES, EXPERTS]

            def first_best(logits, onehot, value):
                link(v.tensor_reduce(value[:], logits[:], AX.X, ALU.max))
                link(v.tensor_tensor(eq[:], logits[:], value[:].unsqueeze(2).broadcast_to(wide),
                                     ALU.is_equal))
                link(v.tensor_tensor(eq[:], eq[:], rank[:].unsqueeze(1).broadcast_to(wide),
                                     ALU.mult))
                link(v.tensor_reduce(best[:], eq[:], AX.X, ALU.max))
                return v.tensor_tensor(onehot[:], rank[:].unsqueeze(1).broadcast_to(wide),
                                       best[:].unsqueeze(2).broadcast_to(wide), ALU.is_equal)

            def flat_rows(a):
                return a[:, :, :].rearrange("p t d -> p (t d)")

            def lo_rows(o, name, n):
                w = work_wait(dve, o, name)
                dve.wait_ge(x_hi, o.l1 * 2 + n)
                v.tensor_tensor(xT_lo[:], w, xT_hi[:].bitcast(F32),
                                ALU.subtract).then_inc(free_of(o, name), 1)

            def lo_q(o, p):
                w = work_bank(o, f"q{p}")
                dve.wait_ge(qk1_hi, o.l1 * 2 * PAIRS + (2 * p + 1))
                for j in range(2):
                    slot = 2 * (p % 2) + j
                    last = v.tensor_tensor(qa1[D1:2 * D1, slot, :], w[j * D1:(j + 1) * D1, :],
                                           qa1[0:D1, slot, :].bitcast(F32), ALU.subtract)
                last.then_inc(free_of(o, f"q{p}"), 1)

            def lo_k(o, p):
                w = work_bank(o, f"k{p}")
                dve.wait_ge(qk1_hi, o.l1 * 2 * PAIRS + (2 * p + 2))
                for j in range(2):
                    slot = 2 * (p % 2) + j
                    v.tensor_tensor(kb1[0:D1, slot, :], w[j * D1:(j + 1) * D1, :],
                                    ka1[0:D1, slot, :].bitcast(F32), ALU.subtract)
                    last = v.tensor_copy(ka1[D1:2 * D1, slot, :], ka1[0:D1, slot, :])
                last.then_inc(free_of(o, f"k{p}"), 1)

            def maxima(o, p, j):
                w = work_wait(dve, o, f"mx{p}_{2 * j}")
                v.tensor_reduce(neg_max[:, 0, j:j + 1], w[:, 0:P], AX.X, ALU.max, negate=True)
                v.tensor_reduce(neg_max[:, 2, j:j + 1], w[:, P:4 * P], AX.X, ALU.max,
                                negate=True).then_inc(free_of(o, f"mx{p}_{2 * j}"), 1)
                w = work_wait(dve, o, f"mx{p}_{2 * j + 1}")
                v.tensor_reduce(neg_max[:, 3, j:j + 1], w, AX.X, ALU.max,
                                negate=True).then_inc(free_of(o, f"mx{p}_{2 * j + 1}"), 1)

            def maxima_parts(o, p):
                w = work_wait(dve, o, f"mx{p}_4")
                v.tensor_reduce(neg_max[:, 1, :], w.rearrange("p (j n) -> p j n", j=2), AX.X,
                                ALU.max, negate=True).then_inc(free_of(o, f"mx{p}_4"), 1)
                for i in (3, 4):
                    work_moved(dve, o, f"mx{p}_{i}")
                link(v.tensor_copy(neg_max_hl[:, :, 0:2], neg_max[:]))
                v.tensor_tensor(neg_max_hl[:, :, 2:4], neg_max[:], neg_max_hl[:, :, 0:2],
                                ALU.subtract).then_inc(negmax_ready, 1)

            def normalize(o, p):
                dve.wait_ge(out_full[0], out0(o, p))
                dve.wait_ge(rsum1_ready, o.l1 * PAIRS + (p + 1))
                v.tensor_tensor(yT[:, p, :], outs[:, 0, :], rsum1[:],
                                ALU.mult).then_inc(out_free[0], 1)

            def attention1_head(o):
                work_wait(dve, o, "x2T")
                v.tensor_copy(kb1[D1:D1 + 4, :, :].rearrange("p (a j) n -> p a j n", j=2),
                              head_sel[D1:D1 + 4].unsqueeze(1).broadcast_to([4, 2, 2, SEQ]))
                lo_rows(o, "x2T", 1)
                for t in range(TILES):
                    w = work_wait(dve, o, f"v{t}_1")
                    v.tensor_copy(v1[:, t, SEQ:2 * SEQ], w).then_inc(free_of(o, f"v{t}_1"), 1)
                for p in range(2):
                    lo_q(o, p)
                    lo_k(o, p)
                maxima(o, 0, 0)
                maxima(o, 0, 1)
                maxima_parts(o, 0)

            def pair_step(o, p):
                if p + 1 < PAIRS:
                    maxima(o, p + 1, 0)
                if p == 2:
                    dve.wait_ge(out_sent, o.l1 * 16 + 16)
                if p >= 2:
                    normalize(o, p - 2)
                if p + 1 < PAIRS:
                    maxima(o, p + 1, 1)
                    maxima_parts(o, p + 1)
                if p + 2 < PAIRS:
                    lo_q(o, p + 2)
                    lo_k(o, p + 2)

            def attention0_head(o, p):
                if p == 0:
                    dve.wait_ge(x_loaded, o.a0 * 16 + 16)
                    variances("a0", x_in)
                if p == 1:
                    standardize("a0", o.a0, x_in, rows_b).then_inc(rows_ready["a0"], 1)
                if p == 4:
                    for t in range(TILES - 2, TILES):
                        work_moved(dve, o, f"qkv0_{t}")
                    if o.f0 is not None:
                        work_wait(dve, o, "xtT")
                        dve.wait_ge(rows_ready["f0"], o.f0 * 3 + 2)
                    q4 = qk_sb[:].rearrange("p (w t n) -> p w t n", w=2, t=TILES)
                    s4 = sum_sq.rearrange("p (w t h) -> p w t h", w=2, t=TILES)
                    for t in range(TILES):
                        link(v.tensor_tensor(sq_tile.rearrange("p (w n) -> p w n", w=2),
                                             q4[:, :, t, :], q4[:, :, t, :], ALU.mult))
                        link(v.tensor_reduce(
                            s4[:, :, t, :], sq_tile.rearrange("p (w h d) -> p w h d", w=2, d=D0),
                            AX.X, ALU.add))
                    v.tensor_scalar(sum_sq, sum_sq, L2_EPS ** 2, None,
                                    ALU.max).then_inc(sumsq_ready, 1)
                if p == 6:
                    dve.wait_ge(invn_ready, o.a0 + 1)
                    link(v.tensor_tensor(newton, inv_norm[:], inv_norm[:], ALU.mult))
                    link(v.tensor_tensor(newton, newton, sum_sq, ALU.mult))
                    link(v.tensor_scalar(newton, newton, -0.5, 1.5, ALU.mult, ALU.add))
                    link(v.tensor_tensor(inv_norm[:], inv_norm[:], newton, ALU.mult))
                    link(v.tensor_scalar(inv_norm[:, 0:TILES * H0], inv_norm[:, 0:TILES * H0],
                                         g_sb[:, 0:1], None, ALU.mult))
                    qk3 = qk_sb[:].rearrange("p (n d) -> p n d", d=D0)
                    v.tensor_tensor(qk3, qk3, inv_norm[:].unsqueeze(2).broadcast_to(
                        [P, N_LEN, D0]), ALU.mult).then_inc(qkn_ready, 1)

            def experts0(o, p):
                if p == 1:
                    variances("f0", res0)
                if p == 2:
                    standardize("f0", o.f0 * 3, res0, rows_a).then_inc(rows_ready["f0"], 1)
                    dve.wait_ge(rows_ready["f0"], o.f0 * 3 + 1)
                    variances("f0", rows_a)
                if p == 3:
                    if o.a0 is not None:
                        work_wait(dve, o, "xT0_1")
                    standardize("f0", o.f0 * 3 + 1, rows_a, rows_b).then_inc(rows_ready["f0"], 1)
                if p == 4:
                    w = work_wait(dve, o, "lg0")
                    v.tensor_copy(lg[:], w[:, 0:TILES * EXPERTS].rearrange(
                        "p (t e) -> p t e", e=EXPERTS)).then_inc(free_of(o, "lg0"), 1)
                    w = work_wait(dve, o, "xh2T")
                    v.tensor_copy(xT_a[:], w).then_inc(free_of(o, "xh2T"), 1)
                if p == 5:
                    work_moved(dve, o, "lg0")
                    link(first_best(lg, oh1, top1))
                    v.tensor_copy(ohx, oh1[:].unsqueeze(3).broadcast_to(
                        [P, TILES, EXPERTS, HID0])).then_inc(onehot_ready, 1)

            def lo_parts(o):
                dve.wait_ge(qkn_ready, o.a0 + 1)
                dve.wait_ge(parts_hi, o.a0 + 1)
                n4 = qk_sb[:].rearrange("p (w n d) -> p w n d", w=2, d=D0)
                for w_, sl in ((0, slice(2, 4)), (1, slice(1, 4, 2))):
                    hl = parts[:, w_].rearrange("p t h r d -> p (t h) r d")
                    four = [P, TILES * H0, 2, D0]
                    last = v.tensor_tensor(
                        hl[:, :, sl, :], n4[:, w_].unsqueeze(2).broadcast_to(four),
                        hl[:, :, 0, :].bitcast(F32).unsqueeze(2).broadcast_to(four), ALU.subtract)
                last.then_inc(parts_ready, 1)

            def group_operands(o, g):
                for w_, name in enumerate((f"qT{g}", f"kT{g}")):
                    w = work_wait(dve, o, name)
                    v.tensor_copy(qkT0[:, w_, g, :], w).then_inc(free_of(o, name), 1)

            def group_out(o, g):
                dve.wait_ge(out_full[1], group_no(o, g))
                v.tensor_copy(oT_sb[:], outs[:, 1, :]).then_inc(out_free[1], 1)

            def group_rows(o, g):
                w = work_wait(dve, o, f"oT{g}").rearrange("p (n s) -> p n s", s=STRIP)
                link(v.reciprocal(rsum0[:], w[:, :, D0]))
                v.tensor_tensor(
                    attn0[:, :, g * HG * D0:(g + 1) * HG * D0].rearrange(
                        "p t (h d) -> p t h d", d=D0),
                    w[:, :, 0:D0].rearrange("p (t h) d -> p t h d", h=HG),
                    rsum0[:].rearrange("p (t h) -> p t h", h=HG).unsqueeze(3).broadcast_to(
                        [P, TILES, HG, D0]), ALU.mult).then_inc(free_of(o, f"oT{g}"), 1)

            def routing1(o):
                w = work_wait(dve, o, "lg1")
                v.tensor_tensor(lg[:], w[:, 0:TILES * EXPERTS].rearrange("p (t e) -> p t e",
                                                                        e=EXPERTS),
                                bg1_sb[:].unsqueeze(1).broadcast_to(wide),
                                ALU.add).then_inc(free_of(o, "lg1"), 1)
                work_moved(dve, o, "lg1")
                link(first_best(lg, oh1, top1))
                link(v.scalar_tensor_tensor(lg2[:], oh1[:], -3e38, lg[:], ALU.mult, ALU.add))
                link(first_best(lg2, oh2, top2))
                v.tensor_tensor(gap[:], top2[:], top1[:], ALU.subtract).then_inc(gap_ready, 1)

            def combine1(o):
                dve.wait_ge(eg_ready, o.l1 + 1)
                link(v.tensor_scalar(sc2[:], eg[:], 1.0, None, ALU.add))
                link(v.reciprocal(sc1[:], sc2[:]))
                link(v.tensor_tensor(sc2[:], eg[:], sc1[:], ALU.mult))
                v.tensor_tensor(oh1[:], oh1[:], sc1[:].unsqueeze(2).broadcast_to(wide), ALU.mult)
                link(v.tensor_tensor(oh2[:], oh2[:], sc2[:].unsqueeze(2).broadcast_to(wide),
                                     ALU.mult))
                v.tensor_tensor(comb[:], oh1[:], oh2[:], ALU.add).then_inc(comb_ready, 1)
                w = work_wait(dve, o, "cT")
                v.tensor_copy(selT1, w[0:EXPERTS, :]).then_inc(free_of(o, "cT"), 1)
                w = work_wait(dve, o, "b2")
                v.tensor_tensor(flat_rows(acc), flat_rows(xn), w,
                                ALU.add).then_inc(free_of(o, "b2"), 1)
                work_moved(dve, o, "b2")

            def accumulate1(o, e):
                dve.wait_ge(out_full[0], out0(o, PAIRS + e))
                for t in range(TILES):
                    last = v.scalar_tensor_tensor(
                        acc[:, t, :], outs[:, 0, t * DIM:(t + 1) * DIM], comb[:, t, e:e + 1],
                        acc[:, t, :], ALU.mult, ALU.add)
                last.then_inc(out_free[0], 1)
                dve.wait_ge(out_free[0], out0(o, PAIRS + e) + 1)

            for o in passes(dve):
                in_loop = not isinstance(o.a0 if o.a0 is not None else o.l1, int)
                if in_loop:
                    before_loop = links[0]
                    links[0] = before_loop + o.l1 * LOOP_LINKS
                l1, f0, a0 = o.l1 is not None, o.f0 is not None, o.a0 is not None
                if l1:
                    attention1_head(o)
                for p in range(PAIRS):
                    if l1:
                        pair_step(o, p)
                    if a0:
                        attention0_head(o, p)
                    if f0:
                        experts0(o, p)
                if l1:
                    normalize(o, PAIRS - 2)
                if a0:
                    lo_parts(o)
                    group_operands(o, 0)
                if l1:
                    normalize(o, PAIRS - 1)
                    w = work_wait(dve, o, "proj")
                    v.tensor_tensor(flat_rows(x3), flat_rows(res1), w,
                                    ALU.add).then_inc(free_of(o, "proj"), 1)
                    work_moved(dve, o, "proj")
                    variances("l1", x3)
                if f0:
                    for c in range(CH0):
                        work_moved(dve, o, f"hid0_{c}")
                        w = work_wait(dve, o, f"mask{c}")
                        v.tensor_tensor(hid0T[:, c, :], hid0T[:, c, :], w,
                                        ALU.mult).then_inc(free_of(o, f"mask{c}"), 1)
                if l1:
                    standardize("l1", o.l1 * 2, x3, xn).then_inc(rows_ready["l1"], 1)
                    lo_rows(o, "xnT", 2)
                    routing1(o)
                if f0:
                    for i in range(2):
                        w = work_wait(dve, o, f"y0_{i}")
                        half = slice(2 * i * P, 2 * (i + 1) * P)
                        v.tensor_tensor(flat_rows(res1)[:, half], flat_rows(res0)[:, half],
                                        w[:, 0:2 * P], ALU.add).then_inc(free_of(o, f"y0_{i}"), 1)
                    for i in range(2):
                        work_moved(dve, o, f"y0_{i}")
                for k in range(GROUPS0):
                    if a0 and k:
                        group_out(o, k - 1)
                    if l1 and k == 0:
                        combine1(o)
                    if l1:
                        accumulate1(o, 2 * k)
                    if a0 and k:
                        group_rows(o, k - 1)
                    if a0 and k + 1 < GROUPS0:
                        group_operands(o, k + 1)
                    if f0 and k == 2:
                        variances("f0", res1)
                    if f0 and k == 3:
                        standardize("f0", o.f0 * 3 + 2, res1, rows_a).then_inc(
                            rows_ready["f0"], 1)
                    if l1:
                        accumulate1(o, 2 * k + 1)
                if l1:
                    variances("l1", acc)
                if a0:
                    group_out(o, GROUPS0 - 1)
                    group_rows(o, GROUPS0 - 1)
                    for g in range(GROUPS0 - 2, GROUPS0):
                        work_moved(dve, o, f"oT{g}")
                    v.tensor_tensor(res0[:], x_in[:], attn0, ALU.add).then_inc(x_taken, 1)
                    dve.wait_ge(x_taken, o.a0 + 1)
                if l1:
                    link(standardize("l1", o.l1 * 2 + 1, acc, acc))
                    link(v.tensor_tensor(acc, acc, gamma_sb[:].unsqueeze(1).broadcast_to(
                        [P, TILES, DIM]), ALU.mult))
                    link(v.tensor_tensor(acc, acc, beta_sb[:].unsqueeze(1).broadcast_to(
                        [P, TILES, DIM]), ALU.add))
                    v.tensor_tensor(result, x3, acc, ALU.add).then_inc(out_ready, 1)
                    dve.wait_ge(out_ready, o.l1 + 1)
                if in_loop:
                    assert links[1] == LOOP_LINKS, links[1]
                    links[0] = before_loop + (BATCH - SKEW) * LOOP_LINKS
                else:
                    links[0] += links[1]
                links[1] = 0

        @block.tensor
        def _(pe):
            mm = nc.tensor.matmul
            pe.wait_ge(weights_in, 16 * N_WEIGHTS)
            for c in range(CH0):
                last = mm(outs[:, 0, c * 8:(c + 1) * 8], w1raw0[:, c * P:(c + 1) * P],
                          bias_ln0_sb[:], start=True, stop=True)
            last.then_inc(fold_ready, 1)
            pe.wait_ge(weights_ready, 1)

            def mm3(dst, w_hi, w_lo, x_hi_, x_lo_, swap=False):
                for n, (a, c) in enumerate(((w_hi, x_hi_), (w_hi, x_lo_), (w_lo, x_hi_))):
                    last = mm(dst, a, c, start=(n == 0), stop=(n == 2))
                return last

            def transposes(o, name, rows, tiles=range(TILES)):
                w = work_open(pe, o, name)
                for i, t in enumerate(tiles):
                    last = nc.tensor.transpose(w[:, i * P:(i + 1) * P], rows[:, t, :], ident)
                last.then_inc(full_of(o, name), 1)

            def project(o, name, which, p):
                w = work_open(pe, o, name)
                cols = slice(p * P, (p + 1) * P)
                mm3(w, wqkv1_hi[:, which, cols], wqkv1_lo[:, which, cols], xT_hi[:],
                    xT_lo[:]).then_inc(full_of(o, name), 1)

            def query_tile(w, p, j, qt):
                slot = 2 * (p % 2) + j
                width = (qt + 1) * P
                mm(w[:, 0:width], qa1[:, slot, qt * P:(qt + 1) * P], ka1[:, slot, 0:width],
                   start=True, stop=False)
                return mm(w[:, width - P:width], ident_b[:], mask_qk[:], start=False, stop=True)

            def max_scores(o, p, j):
                if j == 0:
                    work_moved(pe, o, f"q{p}")
                    work_moved(pe, o, f"k{p}")
                w = work_open(pe, o, f"mx{p}_{2 * j}")
                query_tile(w, p, j, 0)
                query_tile(w[:, P:], p, j, 2).then_inc(full_of(o, f"mx{p}_{2 * j}"), 1)
                w = work_open(pe, o, f"mx{p}_{2 * j + 1}")
                query_tile(w, p, j, 3).then_inc(full_of(o, f"mx{p}_{2 * j + 1}"), 1)

            def max_scores_rest(o, p):
                w = work_open(pe, o, f"mx{p}_4")
                query_tile(w, p, 0, 1)
                query_tile(w[:, 2 * P:], p, 1, 1).then_inc(full_of(o, f"mx{p}_4"), 1)

            def max_transposed(o, p):
                pe.wait_ge(negmax_ready, o.l1 * PAIRS + (p + 1))
                w = work_open(pe, o, f"mT{p}")
                for qt in range(TILES):
                    last = mm(w[D1:D1 + 4, qt * P:(qt + 1) * P], neg_max_hl[:, qt, :],
                              ident_b[:], start=True, stop=True)
                last.then_inc(full_of(o, f"mT{p}"), 1)

            def key_block(dst, p, j, kb):
                slot = 2 * (p % 2) + j
                keys, queries = slice(kb * P, (kb + 1) * P), slice(kb * P, SEQ)
                mm(dst, ka1[:, slot, keys], qa1[:, slot, queries], start=True, stop=False)
                mm(dst, kb1[0:D1 + 4, slot, keys], qb1[0:D1 + 4, slot, queries], start=False,
                   stop=False)
                return mm(dst[:, 0:P], ident_b[:], mask_kq[:], start=False, stop=True)

            def main_unit(o, p, j):
                d = unit_open(pe, o, "pair", p, j)
                key_block(d[:, 0:4 * P], p, j, 0)
                key_block(d[:, 4 * P:7 * P], p, j, 1)
                key_block(d[:, 7 * P:8 * P], p, j, 3).then_inc(score_full, 1)

            def rest_unit(o, p):
                d = unit_open(pe, o, "pair", p, 2)
                key_block(d[:, 0:2 * P], p, 0, 2)
                key_block(d[:, 2 * P:4 * P], p, 1, 2).then_inc(score_full, 1)

            def values1(o, p, kbs):
                if 0 in kbs:
                    pe.wait_ge(out_free[0], out0(o, p))
                    unit_done(pe, o, "pair", p, 2)
                for kb in kbs:
                    for j in range(2):
                        h = 2 * p + j
                        probs = {0: prob1_main(p, j)[:, 0:4 * P],
                                 1: prob1_main(p, j)[:, 4 * P:7 * P],
                                 2: prob1_rest(p)[:, 2 * P * j:2 * P * (j + 1)],
                                 3: prob1_main(p, j)[:, 7 * P:8 * P]}[kb]
                        last = mm(outs[D1 * j:D1 * (j + 1), 0, kb * P:],
                                  v1[:, kb, h * D1:(h + 1) * D1], probs, start=(kb == 0),
                                  stop=(kb == TILES - 1))
                if TILES - 1 in kbs:
                    last.then_inc(out_full[0], 1)

            def sums1(o, p):
                pe.wait_ge(out_free[1], sums_no(o, p))
                pe.wait_ge(tsum_ready, o.l1 * (2 * PAIRS) + 2 * (p + 1))
                for j in range(2):
                    mm(outs[D1 * j:D1 * (j + 1), 1, 0:P], ones[:], prob1_main(p, j)[:, 0:P],
                       start=True, stop=True)
                for j in range(2):
                    last = mm(outs[D1 * j:D1 * (j + 1), 1, P:], ones[:], tsum(j), start=True,
                              stop=True)
                last.then_inc(out_full[1], 1)

            def attention1_head(o):
                transposes(o, "x2T", rows_a)
                work_moved(pe, o, "x2T")
                for t in range(TILES):
                    cols = slice(t * P, (t + 1) * P)
                    for n in range(2):
                        w = work_open(pe, o, f"v{t}_{n}")
                        half = slice(n * SEQ, (n + 1) * SEQ)
                        mm3(w, xT_hi[:, cols], xT_lo[:, cols], wqkv1_hi[:, 2, half],
                            wqkv1_lo[:, 2, half]).then_inc(full_of(o, f"v{t}_{n}"), 1)
                for p in range(2):
                    project(o, f"q{p}", 0, p)
                    project(o, f"k{p}", 1, p)
                for j in range(2):
                    max_scores(o, 0, j)
                max_scores_rest(o, 0)
                max_transposed(o, 0)

            def pair_step(o, p):
                work_moved(pe, o, f"mT{p}")
                main_unit(o, p, 0)
                if p + 1 < PAIRS:
                    max_scores(o, p + 1, 0)
                main_unit(o, p, 1)
                if p + 1 < PAIRS:
                    max_scores(o, p + 1, 1)
                    max_scores_rest(o, p + 1)
                if p >= 1:
                    values1(o, p - 1, (0, 1))
                rest_unit(o, p)
                if p + 2 < PAIRS:
                    project(o, f"q{p + 2}", 0, p + 2)
                if p >= 1:
                    values1(o, p - 1, (2, 3))
                if p + 1 < PAIRS:
                    max_transposed(o, p + 1)
                if p + 2 < PAIRS:
                    project(o, f"k{p + 2}", 1, p + 2)
                if p >= 1:
                    sums1(o, p - 1)

            def attention0_head(o, p):
                if p == 2:
                    pe.wait_ge(rows_ready["a0"], o.a0 + 1)
                    for i in range(2):
                        transposes(o, f"xT0_{i}", rows_b, (2 * i, 2 * i + 1))
                if p == 3:
                    for i in range(2):
                        work_moved(pe, o, f"xT0_{i}")
                    for t in range(TILES):
                        w = work_open(pe, o, f"qkv0_{t}")
                        mm(w[:, 0:3 * DIM], xT_a[:, t * P:(t + 1) * P], wqkv0_sb[:],
                           start=True, stop=True).then_inc(full_of(o, f"qkv0_{t}"), 1)

            def experts0(o, p):
                if p == 3:
                    pe.wait_ge(rows_ready["f0"], o.f0 * 3 + 1)
                    transposes(o, "xtT", rows_a)
                if p == 4:
                    work_moved(pe, o, "xtT")
                    w = work_open(pe, o, "lg0")
                    for t in range(TILES):
                        last = mm(w[:, t * EXPERTS:(t + 1) * EXPERTS], xT_b[:, t * P:(t + 1) * P],
                                  wg0_sb[:], start=True, stop=True)
                    last.then_inc(full_of(o, "lg0"), 1)
                    pe.wait_ge(rows_ready["f0"], o.f0 * 3 + 2)
                    transposes(o, "xh2T", rows_b)
                if p == 6:
                    pe.wait_ge(onehot_ready, o.f0 + 1)
                    w = work_open(pe, o, "ohT")
                    for t in range(TILES):
                        last = mm(w[0:EXPERTS, t * P:(t + 1) * P], oh1[:, t, :], ident,
                                  start=True, stop=True)
                    last.then_inc(full_of(o, "ohT"), 1)

            def hidden0(o):
                work_moved(pe, o, "xh2T")
                for c in range(CH0):
                    w = work_open(pe, o, f"hid0_{c}")
                    mm(w, w1s0[:, c * P:(c + 1) * P], xT_a[:], start=True,
                       stop=True).then_inc(full_of(o, f"hid0_{c}"), 1)

            def masks0(o):
                for c in range(CH0):
                    w = work_open(pe, o, f"mask{c}")
                    for t in range(TILES):
                        rows = ohx[:, t].rearrange("p e h -> p (e h)")[:, c * P:(c + 1) * P]
                        last = mm(w[:, t * P:(t + 1) * P], rows, ident_b[:], start=True, stop=True)
                    last.then_inc(full_of(o, f"mask{c}"), 1)

            def experts0_out(o):
                for c in range(CH0):
                    work_moved(pe, o, f"mask{c}")
                for i in range(2):
                    w = work_open(pe, o, f"y0_{i}")
                    for n in range(2):
                        cols = slice((2 * i + n) * P, (2 * i + n + 1) * P)
                        d = w[:, n * P:(n + 1) * P]
                        for c in range(CH0):
                            mm(d, hid0T[:, c, cols], w2_0_sb[:, c, :], start=(c == 0), stop=False)
                        last = mm(d, selT0[:, cols], b2_0_sb[:], start=False, stop=True)
                    last.then_inc(full_of(o, f"y0_{i}"), 1)

            def group_operands(o, g):
                pe.wait_ge(parts_ready, o.a0 + 1)
                for w_, name in enumerate((f"qT{g}", f"kT{g}")):
                    w = work_open(pe, o, name).bitcast(F32R)
                    for t in range(TILES):
                        rows = parts[:, w_, t, g * HG:(g + 1) * HG].rearrange("p h r d -> p (h r d)")
                        last = nc.tensor.transpose(w[:, t * P:(t + 1) * P], rows, ident_r[:])
                    last.then_inc(full_of(o, name), 1)

            def cosines(o, n):
                g, kb = n // TILES, n % TILES
                if kb == 0:
                    work_moved(pe, o, f"qT{g}")
                    work_moved(pe, o, f"kT{g}")
                for pair in range(2):
                    d = unit_open(pe, o, "cosine", n, pair)
                    for i in range(2):
                        j = 2 * pair + i
                        rows = slice(STRIP * j, STRIP * (j + 1))
                        last = mm(d[:, i * SEQ:(i + 1) * SEQ],
                                  qkT0[rows, 1, g, kb * P:(kb + 1) * P], qkT0[rows, 0, g, :],
                                  start=True, stop=True)
                    last.then_inc(score_full, 1)

            def values0(o, n):
                g, kb = n // TILES, n % TILES
                if kb == 0:
                    pe.wait_ge(out_free[1], group_no(o, g))
                unit_done(pe, o, "cosine", n, 1)
                for j in range(HG):
                    last = mm(outs[STRIP * j:STRIP * (j + 1), 1, :],
                              vstat[:, kb, g * HG + j, :], prob0(n)[:, j * SEQ:(j + 1) * SEQ],
                              start=(kb == 0), stop=(kb == TILES - 1))
                last.then_inc(out_full[1] if kb == TILES - 1 else pv0_done, 1)

            def group_rows(o, g):
                pe.wait_ge(out_free[1], group_no(o, g) + 1)
                w = work_open(pe, o, f"oT{g}")
                for t in range(TILES):
                    last = nc.tensor.transpose(w[:, t * P:(t + 1) * P],
                                               oT_sb[:, t * P:(t + 1) * P], ident)
                last.then_inc(full_of(o, f"oT{g}"), 1)

            def hidden1(o, e):
                for h in range(CH1 // 2):
                    d = unit_open(pe, o, "hidden", e, h)
                    for c in range(2):
                        at = e * HID1 + (2 * h + c) * P
                        last = mm3(d[:, c * SEQ:(c + 1) * SEQ], w1_hi[:, at:at + P],
                                   w1_lo[:, at:at + P], xT_hi[:], xT_lo[:])
                    last.then_inc(score_full, 1)

            def experts1_out(o, e, tiles):
                if 0 in tiles:
                    pe.wait_ge(out_free[0], out0(o, PAIRS + e))
                    unit_done(pe, o, "hidden", e, CH1 // 2 - 1)
                for t in tiles:
                    cols = slice(t * P, (t + 1) * P)
                    for c in range(CH1):
                        last = mm(outs[:, 0, cols], hid1T(e, c)[:, cols],
                                  w2_1_sb[:, e * CH1 + c, :], start=(c == 0), stop=(c == CH1 - 1))
                if TILES - 1 in tiles:
                    last.then_inc(out_full[0], 1)

            def combine_transposed(o):
                pe.wait_ge(comb_ready, o.l1 + 1)
                w = work_open(pe, o, "cT")
                for t in range(TILES):
                    last = mm(w[0:EXPERTS, t * P:(t + 1) * P], comb[:, t, :], ident, start=True,
                              stop=True)
                last.then_inc(full_of(o, "cT"), 1)

            def combine_bias(o):
                work_moved(pe, o, "cT")
                w = work_open(pe, o, "b2")
                for t in range(TILES):
                    cols = slice(t * P, (t + 1) * P)
                    last = mm(w[:, cols], selT1[:, cols], b2_1_sb[:], start=True, stop=True)
                last.then_inc(full_of(o, "b2"), 1)

            for o in passes(pe):
                l1, f0, a0 = o.l1 is not None, o.f0 is not None, o.a0 is not None
                if l1:
                    pe.wait_ge(rows_ready["f0"], o.l1 * 3 + 3)
                    attention1_head(o)
                for p in range(PAIRS):
                    if l1:
                        pair_step(o, p)
                    if a0:
                        attention0_head(o, p)
                    if f0:
                        experts0(o, p)
                if l1:
                    values1(o, PAIRS - 1, range(TILES))
                    sums1(o, PAIRS - 1)
                if a0:
                    group_operands(o, 0)
                if f0:
                    hidden0(o)
                if l1:
                    pe.wait_ge(out_free[0], out0(o, PAIRS))
                    w = work_open(pe, o, "proj")
                    for t in range(TILES):
                        cols = slice(t * P, (t + 1) * P)
                        for p in range(PAIRS):
                            last = mm(w[:, cols], yT[:, p, cols], wo_sb[:, p, :], start=(p == 0),
                                      stop=(p == PAIRS - 1))
                    last.then_inc(full_of(o, "proj"), 1)
                if f0:
                    masks0(o)
                if l1:
                    pe.wait_ge(rows_ready["l1"], o.l1 + 1)
                    transposes(o, "xnT", xn)
                    work_moved(pe, o, "xnT")
                    w = work_open(pe, o, "lg1")
                    for t in range(TILES):
                        last = mm(w[:, t * EXPERTS:(t + 1) * EXPERTS], xT1[:, t * P:(t + 1) * P],
                                  wg1_sb[:], start=True, stop=True)
                    last.then_inc(full_of(o, "lg1"), 1)
                if f0:
                    experts0_out(o)
                for k in range(GROUPS0):
                    if l1:
                        hidden1(o, 2 * k)
                        hidden1(o, 2 * k + 1)
                    for m in range(TILES):
                        n = TILES * k + m
                        if a0:
                            cosines(o, n)
                        if l1 and k == 0 and m == 0:
                            combine_transposed(o)
                        if l1 and k == 0 and m == 1:
                            combine_bias(o)
                        if l1:
                            experts1_out(o, 2 * k + m // 2, (2 * (m % 2), 2 * (m % 2) + 1))
                        if a0 and n:
                            values0(o, n - 1)
                        if a0 and m == 1 and k:
                            group_rows(o, k - 1)
                        if a0 and m == 2 and k + 1 < GROUPS0:
                            group_operands(o, k + 1)
                if a0:
                    values0(o, STEPS0 - 1)
                    group_rows(o, GROUPS0 - 1)


def kernel(L0_attn_x, L0_attn_Wq, L0_attn_Wk, L0_attn_Wv, L0_attn_g_scale, L0_ffn_Wg,
           L0_ffn_ln_scale, L0_ffn_ln_bias, L0_ffn_W1, L0_ffn_b1, L0_ffn_W2, L0_ffn_b2,
           L1_attn_w_q, L1_attn_w_k, L1_attn_w_v, L1_attn_w_o, L1_ffn_Wg, L1_ffn_bg, L1_ffn_W1,
           L1_ffn_b1, L1_ffn_W2, L1_ffn_b2, L1_ffn_gamma, L1_ffn_beta):
    import concourse.bacc as bacc
    from concourse.bass_utils import run_bass_kernel_spmd

    def rows(a):
        return np.asarray(a).reshape(-1, P, a.shape[-1]).transpose(1, 0, 2)

    def flat(a):
        return np.asarray(a).reshape(-1, DIM).T

    ins = {
        "x": np.asarray(L0_attn_x).reshape(BATCH, TILES, P, DIM).transpose(0, 2, 1, 3),
        "wqkv0": np.concatenate([np.asarray(w).T for w in (L0_attn_Wq, L0_attn_Wk, L0_attn_Wv)], 1),
        "g_scale": np.asarray(L0_attn_g_scale).reshape(1, 1),
        "wg0": np.asarray(L0_ffn_Wg).T,
        "s0": np.asarray(L0_ffn_ln_scale).T,
        "bias_ln0": np.asarray(L0_ffn_ln_bias).T,
        "w1_0": np.asarray(L0_ffn_W1).transpose(1, 0, 2).reshape(DIM, EXPERTS * HID0),
        "b1_0": np.asarray(L0_ffn_b1).reshape(CH0, P).T,
        "w2_0": rows(np.asarray(L0_ffn_W2).reshape(EXPERTS * HID0, DIM)),
        "b2_0": np.asarray(L0_ffn_b2),
        "wq1": flat(L1_attn_w_q),
        "wk1": flat(L1_attn_w_k),
        "wv1": flat(L1_attn_w_v),
        "wo1": rows(np.asarray(L1_attn_w_o)),
        "wg1": np.asarray(L1_ffn_Wg),
        "bg1": np.asarray(L1_ffn_bg).reshape(1, EXPERTS),
        "w1_1": np.asarray(L1_ffn_W1).transpose(1, 0, 2).reshape(DIM, EXPERTS * HID1),
        "b1_1": np.asarray(L1_ffn_b1).reshape(EXPERTS * CH1, P).T,
        "w2_1": rows(np.asarray(L1_ffn_W2).reshape(EXPERTS * HID1, DIM)),
        "b2_1": np.asarray(L1_ffn_b2),
        "gamma": np.asarray(L1_ffn_gamma).reshape(1, DIM),
        "beta": np.asarray(L1_ffn_beta).reshape(1, DIM),
    }
    ins = {name: np.ascontiguousarray(a) for name, a in ins.items()}
    nc = bacc.Bacc("TRN2", target_bir_lowering=False, num_devices=1)
    drams = [nc.dram_tensor(f"in_{name}", a.shape, mybir.dt.from_np(a.dtype),
                            kind="ExternalInput").ap() for name, a in ins.items()]
    out = nc.dram_tensor("out", (BATCH, P, TILES, DIM), F32, kind="ExternalOutput").ap()
    layers_kernel(nc, *drams, out)
    got = run_bass_kernel_spmd(nc, [{f"in_{name}": a for name, a in ins.items()}], core_ids=[0])
    y = got.results[0]["out"]
    return y.transpose(0, 2, 1, 3).reshape(BATCH, SEQ, DIM)
```

```python
import numpy as np
from contextlib import ExitStack

import concourse.bass as bass
from concourse import mybir

F32 = mybir.dt.float32
F32R = mybir.dt.float32r
BF16 = mybir.dt.bfloat16
ALU = mybir.AluOpType
ACT = mybir.ActivationFunctionType
AX = mybir.AxisListType

P = 128
BATCH, SEQ, DIM = 8, 512, 128
TILES = SEQ // P
EXPERTS = 8
LN_EPS = 1e-5
L2_EPS = 1e-12
MASKED = -1e30

H0 = 16
D0 = DIM // H0
HG = 4
GROUPS0 = H0 // HG
STRIP = 32
TERMS = 4
STEPS0 = GROUPS0 * TILES
HID0 = 32
CH0 = EXPERTS * HID0 // P
H1 = 16
D1 = 64
PAIRS = H1 // 2
SCALE1 = 1.0 / D1 ** 0.5
HID1 = 512
CH1 = HID1 // P

SKEW = 2


def work_order(l1, f0, a0):
    names = []
    for p in range(PAIRS):
        if l1 and p + 1 < PAIRS:
            names += [f"mx{p + 1}_{i}" for i in range(5)] + [f"mT{p + 1}"]
        if l1 and p + 2 < PAIRS:
            names += [f"q{p + 2}", f"k{p + 2}"]
        if a0:
            names += {2: ["xT0_0", "xT0_1"], 3: ["qkv0_0", "qkv0_1"],
                      4: ["qkv0_2", "qkv0_3"]}.get(p, [])
        if f0:
            names += {3: ["xtT"], 4: ["lg0", "xh2T"]}.get(p, [])
    names += ["hid0_0", "hid0_1", "ohT"] if f0 else []
    names += ["qT0", "kT0"] if a0 else []
    names += ["proj"] if l1 else []
    names += ["mask0", "mask1", "y0_0", "y0_1"] if f0 else []
    names += ["xnT"] if l1 else []
    names += ["qT1", "kT1"] if a0 else []
    names += ["lg1", "cT", "b2"] if l1 else []
    for k in range(GROUPS0):
        names += [f"oT{k}"] if a0 else []
        names += [f"qT{k + 2}", f"kT{k + 2}"] if a0 and k + 2 < GROUPS0 else []
    names += ["x2T", "q0", "k0", "v0_0", "v0_1", "mx0_0", "mx0_1", "v1_0", "v1_1", "mx0_2",
              "mx0_3", "q1", "v2_0", "mx0_4", "k1", "v2_1", "mT0", "v3_0", "v3_1"] if f0 else []
    return names


def unit_order(l1, a0):
    units = [("pair", p, i) for p in range(PAIRS) for i in range(3)] if l1 else []
    for k in range(-1, GROUPS0):
        units += [("hidden", e, h) for e in (2 * k, 2 * k + 1)
                  for h in range(CH1 // 2)] if l1 and k >= 0 else []
        units += [("cosine", n, i) for n in range(TILES * (k + 1), TILES * (k + 2))
                  for i in range(2)] if a0 and k + 1 < GROUPS0 else []
    assert len(units) % 2 == 0
    return units


class Pass:

    def __init__(self, l1, f0, a0, work, phase, units, sums):
        self.l1, self.f0, self.a0 = l1, f0, a0
        self.first = l1 is None and f0 is None
        self.looped = False
        here = [x is not None for x in (l1, f0, a0)]
        self.work_no = {n: phase + i for i, n in enumerate(work_order(*here))}
        self.unit_no = {u: i for i, u in enumerate(unit_order(here[0], here[2]))}
        self.work, self.units, self.sums = work, units, sums
        fills = phase + len(self.work_no)
        self.next = (work + fills // 2, fills % 2, units + len(self.unit_no),
                     sums + (PAIRS if here[0] else 0) + (GROUPS0 if here[2] else 0))


def passes(eng):
    def at(i, before):
        batch = [i + n if 0 <= i + n < BATCH else None for n in range(SKEW + 1)]
        return Pass(*batch, *before)

    before = (0, 0, 0, 0)
    for i in range(-SKEW, 0):
        one = at(i, before)
        yield one
        before = one.next
    step = [b - a for a, b in zip(before, at(0, before).next)]
    assert step[1] == 0
    with eng.Fori(0, BATCH - SKEW) as i:
        one = Pass(i, i + 1, i + 2, *(a + i * d if d else a for a, d in zip(before, step)))
        one.looped = True
        yield one
    before = tuple(a + (BATCH - SKEW) * d for a, d in zip(before, step))
    for i in range(BATCH - SKEW, BATCH):
        one = at(i, before)
        yield one
        before = one.next


OUT0 = PAIRS + EXPERTS

PROB0 = 0
PROB0_SLOTS = 3
HIDT = PROB0_SLOTS * HG * SEQ
V1 = 0
PROB1 = V1 + TILES * H1 * D1
PROB1_PAIR = 2 * 1024 + 512
TSUM = PROB1 + 2 * PROB1_PAIR
BIG = max(TSUM + 2 * 384, HIDT + 2 * CH1 * SEQ)

LOOP_LINKS = 69


def layers_kernel(nc, x, wqkv0, g_scale, wg0, s0, bias_ln0, w1_0, b1_0, w2_0, b2_0,
                  wq1, wk1, wv1, wo1, wg1, bg1, w1_1, b1_1, w2_1, b2_1, gamma, beta, out):
    ctx = ExitStack()
    with ctx:
        def sb(name, shape, dt=F32):
            return ctx.enter_context(nc.sbuf_tensor(name, shape, dt))

        def sem(name):
            return ctx.enter_context(nc.semaphore(name))

        ident_r = sb("ident_r", [P, P], F32R)
        ident = ident_r[:].bitcast(F32)
        ident_b = sb("ident_b", [P, P], BF16)
        mask_qk = sb("mask_qk", [P, P], BF16)
        mask_kq = sb("mask_kq", [P, P], BF16)
        ones = sb("ones", [P, D1])
        rank = sb("rank", [P, EXPERTS])
        head_sel = sb("head_sel", [P, 2, 1])
        wqkv0_sb = sb("wqkv0_sb", [P, 3 * DIM])
        g_sb = sb("g_sb", [P, 1])
        wg0_sb = sb("wg0_sb", [P, EXPERTS])
        s0_sb = sb("s0_sb", [P, EXPERTS])
        bias_ln0_sb = sb("bias_ln0_sb", [P, EXPERTS])
        w1s0 = sb("w1s0", [P, EXPERTS * HID0])
        b1_0_sb = sb("b1_0_sb", [P, CH0])
        bias0 = sb("bias0", [P, CH0])
        w2_0_sb = sb("w2_0_sb", [P, CH0, DIM])
        b2_0_sb = sb("b2_0_sb", [EXPERTS, DIM])
        wqkv1_hi = sb("wqkv1_hi", [P, 3, H1 * D1], F32R)
        wqkv1_lo = sb("wqkv1_lo", [P, 3, H1 * D1], F32R)
        wo_sb = sb("wo_sb", [P, PAIRS, DIM])
        wg1_sb = sb("wg1_sb", [P, EXPERTS])
        wg1_hi = sb("wg1_hi", [P, EXPERTS], F32R)
        wg1_lo = sb("wg1_lo", [P, EXPERTS], F32R)
        bg1_sb = sb("bg1_sb", [P, EXPERTS])
        w1_hi = sb("w1_hi", [P, EXPERTS * HID1], F32R)
        w1_lo = sb("w1_lo", [P, EXPERTS * HID1], F32R)
        b1_1_sb = sb("b1_1_sb", [P, EXPERTS * CH1])
        w2_1_sb = sb("w2_1_sb", [P, EXPERTS * CH1, DIM])
        b2_1_sb = sb("b2_1_sb", [EXPERTS, DIM])
        gamma_sb = sb("gamma_sb", [P, DIM])
        beta_sb = sb("beta_sb", [P, DIM])

        x_in = sb("x_in", [P, TILES, DIM])
        res0 = sb("res0", [P, TILES, DIM])
        res1 = sb("res1", [P, TILES, DIM])
        rows_a = sb("rows_a", [P, TILES, DIM])
        rows_b = sb("rows_b", [P, TILES, DIM])
        xT_a = sb("xT_a", [P, SEQ])
        x2_hi = sb("x2_hi", [P, SEQ], F32R)
        x2_lo = sb("x2_lo", [P, SEQ], F32R)
        xn_hi = sb("xn_hi", [P, SEQ], F32R)
        xn_lo = sb("xn_lo", [P, SEQ], F32R)
        stats = sb("stats", [P, TILES, 6])
        mean = sb("mean", [P, TILES])
        halves = sb("halves", [P, TILES])
        var_eps = sb("var_eps", [P, TILES])
        minus_half = sb("minus_half", [P, TILES])
        rstd = sb("rstd", [P, TILES])
        inv_norm = sb("inv_norm", [P, 2 * TILES * H0])
        qk_sb = sb("qk_sb", [P, 2 * TILES * DIM])
        vstat = sb("vstat", [P, TILES, H0, STRIP])
        oT_sb = sb("oT_sb", [P, SEQ])
        rsum0 = sb("rsum0", [P, TILES * HG])
        lg = sb("lg", [P, TILES, EXPERTS])
        lg2 = sb("lg2", [P, TILES, EXPERTS])
        eq = sb("eq", [P, TILES, EXPERTS])
        oh1 = sb("oh1", [P, TILES, EXPERTS])
        oh2 = sb("oh2", [P, TILES, EXPERTS])
        comb = sb("comb", [P, TILES, EXPERTS])
        top1 = sb("top1", [P, TILES])
        top2 = sb("top2", [P, TILES])
        best = sb("best", [P, TILES])
        gap = sb("gap", [P, TILES])
        eg = sb("eg", [P, TILES])
        sc1 = sb("sc1", [P, TILES])
        sc2 = sb("sc2", [P, TILES])
        neg_max = sb("neg_max", [P, TILES, 2])
        neg_max_hl = sb("neg_max_hl", [P, TILES, 4], BF16)
        ra = sb("ra", [P, 8 * SEQ], F32R)
        rb = sb("rb", [P, 8 * SEQ], F32R)
        big = sb("big", [P, BIG])
        g_buf = sb("g_buf", [P, PAIRS, SEQ])
        yT = g_buf
        xT_b = g_buf[:, PAIRS - 1, :]
        x3, xn, acc, result, attn0 = (g_buf[:, n, :].rearrange("p (t d) -> p t d", t=TILES)
                                      for n in range(5))
        norms = rows_a[:, :, :].rearrange("p t d -> p (t d)")
        N_LEN = 2 * TILES * H0
        sq_tile = norms[:, 0:2 * DIM]
        sum_sq = norms[:, 2 * DIM:2 * DIM + N_LEN]
        newton = norms[:, 2 * DIM + N_LEN:2 * DIM + 2 * N_LEN]
        mask_f = rows_a[:, 0:2, :]
        ident_f = rows_a[:, 2, :]
        ohx = rows_b[:, :, :].bitcast(BF16).rearrange("p t (e h) -> p t e h", e=EXPERTS)
        w1raw0 = res1[:, 0:2, :].rearrange("p t d -> p (t d)")
        selT0 = rows_a[0:EXPERTS, :, :].rearrange("p t d -> p (t d)")
        selT1 = xT_a[0:EXPERTS, :]
        rsum1 = oT_sb
        parts = ra[:, :].rearrange("p (w t h r d) -> p w t h r d", w=2, t=TILES, h=H0, r=TERMS)
        qkT0 = rb[:, :].rearrange("p (w g n) -> p w g n", w=2, g=GROUPS0)
        qa1 = ra[:, 0:4 * SEQ].rearrange("p (s n) -> p s n", s=4)
        ka1 = ra[:, 4 * SEQ:8 * SEQ].rearrange("p (s n) -> p s n", s=4)
        qb1 = rb[:, 0:4 * SEQ].rearrange("p (s n) -> p s n", s=4)
        kb1 = rb[:, 4 * SEQ:8 * SEQ].rearrange("p (s n) -> p s n", s=4)
        v1 = big[:, V1:PROB1].rearrange("p (t n) -> p t n", t=TILES)
        hid0T = big[:, PROB1:PROB1 + CH0 * SEQ].rearrange("p (c n) -> p c n", c=CH0)
        stage_qk1 = g_buf[:, 0:4, :].rearrange("p a n -> p (a n)")
        stage_v1 = g_buf[:, 5:7, :].rearrange("p a n -> p (a n)")
        stage_w1 = big[:, HIDT:HIDT + EXPERTS * HID1]

        def prob0(n):
            at = PROB0 + (n % PROB0_SLOTS) * HG * SEQ
            return big[:, at:at + HG * SEQ]

        def prob1_main(p, j):
            at = PROB1 + (p % 2) * PROB1_PAIR + j * 1024
            return big[:, at:at + 1024]

        def prob1_rest(p):
            at = PROB1 + (p % 2) * PROB1_PAIR + 2048
            return big[:, at:at + 512]

        def tsum(j):
            at = TSUM + j * 384
            return big[:, at:at + 384]

        def hid1T(e, c):
            at = HIDT + ((e % 2) * CH1 + c) * SEQ
            return big[:, at:at + SEQ]

        scores = ctx.enter_context(nc.psum_tensor("scores", [P, 2, 1024], F32))
        outs = ctx.enter_context(nc.psum_tensor("outs", [P, 2, SEQ], F32))
        work = ctx.enter_context(nc.psum_tensor("work", [P, 2, SEQ], F32))

        first_in = sem("first_in")
        weights_in = sem("weights_in")
        consts = sem("consts")
        const_step = sem("const_step")
        weights_hi = sem("weights_hi")
        vstat_ready = sem("vstat_ready")
        wg1_ready = sem("wg1_ready")
        weights_ready = sem("weights_ready")
        fold_ready = sem("fold_ready")
        x_loaded = sem("x_loaded")
        x_taken = sem("x_taken")
        out_sent = sem("out_sent")
        out_ready = sem("out_ready")
        result_step = sem("result_step")
        k_twice = sem("k_twice")
        sel_ready = sem("sel_ready")
        streams = ("a0", "f0", "l1")
        var_ready = {n: sem(f"var_ready_{n}") for n in streams}
        rstd_ready = {n: sem(f"rstd_ready_{n}") for n in streams}
        rows_ready = {n: sem(f"rows_ready_{n}") for n in streams}
        sumsq_ready = sem("sumsq_ready")
        ln_done = sem("ln_done")
        invn_ready = sem("invn_ready")
        qkn_ready = sem("qkn_ready")
        parts_hi = sem("parts_hi")
        parts_ready = sem("parts_ready")
        pv0_done = sem("pv0_done")
        onehot_ready = sem("onehot_ready")
        hid0m_ready = sem("hid0m_ready")
        x_hi = sem("x_hi")
        qk1_hi = sem("qk1_hi")
        negmax_ready = sem("negmax_ready")
        tsum_ready = sem("tsum_ready")
        tsum_step = sem("tsum_step")
        rsum1_ready = sem("rsum1_ready")
        gap_ready = sem("gap_ready")
        eg_ready = sem("eg_ready")
        comb_ready = sem("comb_ready")
        dve_step = sem("dve_step")
        score_full = sem("score_full")
        score_done = sem("score_done")
        out_full = [sem(f"out_full{i}") for i in range(2)]
        out_free = [sem(f"out_free{i}") for i in range(2)]
        work_full = [sem(f"work_full{i}") for i in range(2)]
        work_free = [sem(f"work_free{i}") for i in range(2)]

        block = ctx.enter_context(nc.Block())

        def bank_no(o, name):
            return o.work_no[name] % 2

        def work_bank(o, name):
            return work[:, bank_no(o, name), :]

        def work_fills(o, name):
            return o.work + (o.work_no[name] // 2 + 1)

        def work_open(pe, o, name):
            pe.wait_ge(work_free[bank_no(o, name)], work_fills(o, name))
            return work_bank(o, name)

        def work_wait(eng, o, name):
            eng.wait_ge(work_full[bank_no(o, name)], work_fills(o, name))
            return work_bank(o, name)

        def work_moved(eng, o, name):
            eng.wait_ge(work_free[bank_no(o, name)], work_fills(o, name) + 1)

        def full_of(o, name):
            return work_full[bank_no(o, name)]

        def free_of(o, name):
            return work_free[bank_no(o, name)]

        def unit_slot(o, *unit):
            return scores[:, o.unit_no[unit] % 2, :]

        def unit_open(pe, o, *unit):
            pe.wait_ge(score_done, o.units + (o.unit_no[unit] + 1))
            return unit_slot(o, *unit)

        def unit_wait(act, o, *unit):
            act.wait_ge(score_full, o.units + (o.unit_no[unit] + 1))
            return unit_slot(o, *unit)

        def unit_done(eng, o, *unit):
            eng.wait_ge(score_done, o.units + (o.unit_no[unit] + 3))

        def out0(o, n):
            return o.l1 * OUT0 + (n + 1)

        def sums_no(o, p):
            return o.sums + (p + 1)

        def group_no(o, g):
            return o.sums + ((PAIRS if o.l1 is not None else 0) + g + 1)

        N_WEIGHTS = 18

        @block.sync
        def _(sp):
            sp.dma_start(x_in[:], x[0]).then_inc(x_loaded, 16)
            for dst, src in ((wqkv0_sb[:], wqkv0), (g_sb[:], g_scale.to_broadcast([P, 1]))):
                sp.dma_start(dst, src).then_inc(first_in, 16)
            for dst, src in ((wg0_sb[:], wg0), (s0_sb[:], s0), (bias_ln0_sb[:], bias_ln0),
                             (w1raw0[:], w1_0), (b1_0_sb[:], b1_0),
                             (stage_qk1[:, 0:H1 * D1], wq1), (stage_qk1[:, H1 * D1:], wk1),
                             (stage_v1, wv1), (stage_w1, w1_1),
                             (w2_0_sb[:], w2_0), (b2_0_sb[:], b2_0), (wo_sb[:], wo1),
                             (wg1_sb[:], wg1), (bg1_sb[:], bg1.to_broadcast([P, EXPERTS])),
                             (b1_1_sb[:], b1_1), (w2_1_sb[:], w2_1), (b2_1_sb[:], b2_1),
                             (gamma_sb[:], gamma.to_broadcast([P, DIM]))):
                sp.dma_start(dst, src).then_inc(weights_in, 16)
            sp.dma_start(beta_sb[:], beta.to_broadcast([P, DIM])).then_inc(out_sent, 16)
            for a in range(1, SKEW + 1):
                sp.wait_ge(x_taken, a)
                sp.dma_start(x_in[:], x[a]).then_inc(x_loaded, 16)
            with sp.Fori(0, BATCH - SKEW - 1) as b:
                sp.wait_ge(x_taken, b + SKEW + 1)
                sp.dma_start(x_in[:], x[bass.ds(b + SKEW + 1, 1)]).then_inc(x_loaded, 16)
                sp.wait_ge(out_ready, b + 1)
                sp.dma_start(out[bass.ds(b, 1)], result).then_inc(out_sent, 16)
            for b in range(BATCH - SKEW - 1, BATCH):
                sp.wait_ge(out_ready, b + 1)
                sp.dma_start(out[b], result).then_inc(out_sent, 16)
            sp.wait_ge(out_sent, 16 * (BATCH + 1))

        @block.gpsimd
        def _(pool):
            nc.gpsimd.memset(ident_f, 0.0).then_inc(const_step, 1)
            nc.gpsimd.memset(mask_f, 0.0).then_inc(const_step, 1)
            nc.gpsimd.memset(head_sel[:], 0.0).then_inc(const_step, 1)
            nc.gpsimd.memset(ones[:], 1.0)
            nc.gpsimd.memset(minus_half[:], -0.5)
            nc.gpsimd.iota(rank[:], pattern=[[-1, EXPERTS]], base=EXPERTS, channel_multiplier=0,
                           allow_small_or_imprecise_dtypes=True)
            pool.wait_ge(const_step, 3)
            nc.gpsimd.affine_select(out=ident_f, in_=ident_f, compare_op=ALU.not_equal, fill=1.0,
                                    base=0, pattern=[[-1, P]], channel_multiplier=1)
            nc.gpsimd.affine_select(out=mask_f[:, 0, :], in_=mask_f[:, 0, :], compare_op=ALU.is_ge,
                                    fill=MASKED, base=0, pattern=[[-1, P]], channel_multiplier=1)
            nc.gpsimd.affine_select(out=mask_f[:, 1, :], in_=mask_f[:, 1, :], compare_op=ALU.is_ge,
                                    fill=MASKED, base=0, pattern=[[1, P]],
                                    channel_multiplier=-1).then_inc(const_step, 1)
            pool.wait_ge(const_step, 4)
            sel = head_sel[D1:D1 + 4, :, 0]
            nc.gpsimd.affine_select(out=sel, in_=sel, compare_op=ALU.not_equal, fill=1.0, base=0,
                                    pattern=[[-1, 2]], channel_multiplier=1).then_inc(const_step, 1)
            pool.wait_ge(const_step, 5)
            nc.gpsimd.affine_select(out=sel, in_=sel, compare_op=ALU.not_equal, fill=1.0, base=-2,
                                    pattern=[[-1, 2]], channel_multiplier=1).then_inc(consts, 1)

            def inverse_deviations(stream, n):
                pool.wait_ge(var_ready[stream], n + 1)
                nc.gpsimd.tensor_tensor(rstd[:], var_eps[:], minus_half[:],
                                        ALU.pow).then_inc(rstd_ready[stream], 1)

            def sum_blocks(o, p):
                unit_done(pool, o, "pair", p, 2)
                for j in range(2):
                    m, r = prob1_main(p, j), prob1_rest(p)
                    t = tsum(j)
                    first = o.l1 * (4 * PAIRS) + (4 * p + 2 * j + 1)
                    if j == 0 and p:
                        pool.wait_ge(out_full[1], sums_no(o, p - 1))
                    nc.gpsimd.tensor_tensor(t, m[:, P:SEQ], m[:, SEQ:SEQ + 3 * P],
                                            ALU.add).then_inc(tsum_step, 1)
                    pool.wait_ge(tsum_step, first)
                    nc.gpsimd.tensor_tensor(t[:, P:3 * P], t[:, P:3 * P],
                                            r[:, 2 * P * j:2 * P * (j + 1)],
                                            ALU.add).then_inc(tsum_step, 1)
                    pool.wait_ge(tsum_step, first + 1)
                    nc.gpsimd.tensor_tensor(t[:, 2 * P:3 * P], t[:, 2 * P:3 * P],
                                            m[:, 7 * P:8 * P], ALU.add).then_inc(tsum_ready, 1)

            def hi_k_again(s, p):
                pool.wait_ge(qk1_hi, s * 2 * PAIRS + (2 * p + 2))
                slots = slice(2 * (p % 2), 2 * (p % 2) + 2)
                one = ones[0:D1, 0:1].unsqueeze(1).broadcast_to([D1, 2, SEQ])
                nc.gpsimd.tensor_tensor(ka1[D1:2 * D1, slots, :],
                                        ka1[0:D1, slots, :].bitcast(F32), one,
                                        ALU.mult).then_inc(k_twice, 1)
                pool.wait_ge(k_twice, s * PAIRS + (p + 1))

            for o in passes(pool):
                for p in range(PAIRS):
                    if o.l1 is not None:
                        sum_blocks(o, p)
                    if o.l1 is not None and p + 2 < PAIRS:
                        pool.wait_ge(tsum_ready, o.l1 * (2 * PAIRS) + 2 * (p + 1))
                        hi_k_again(o.l1, p + 2)
                    if p == 0 and o.a0 is not None:
                        inverse_deviations("a0", o.a0)
                    if p in (1, 2) and o.f0 is not None:
                        inverse_deviations("f0", o.f0 * 3 + (p - 1))
                if o.l1 is not None:
                    inverse_deviations("l1", o.l1 * 2)
                if o.f0 is not None:
                    inverse_deviations("f0", o.f0 * 3 + 2)
                    pool.wait_ge(rstd_ready["f0"], o.f0 * 3 + 3)
                    work_wait(pool, o, "x2T")
                    sel = head_sel[D1:D1 + 4].unsqueeze(1).broadcast_to([4, 2, 2, SEQ])
                    nc.gpsimd.tensor_tensor(
                        kb1[D1:D1 + 4, :, :].rearrange("p (a j) n -> p a j n", j=2), sel, sel,
                        ALU.mult).then_inc(sel_ready, 1)
                    pool.wait_ge(sel_ready, o.f0 + 1)
                    for p in range(2):
                        hi_k_again(o.f0, p)
                if o.l1 is not None:
                    inverse_deviations("l1", o.l1 * 2 + 1)
                    wide = [P, TILES, DIM]
                    pool.wait_ge(rows_ready["l1"], o.l1 * 2 + 2)
                    nc.gpsimd.tensor_tensor(
                        acc, acc, gamma_sb[:].unsqueeze(1).broadcast_to(wide),
                        ALU.mult).then_inc(result_step, 1)
                    pool.wait_ge(result_step, o.l1 * 2 + 1)
                    nc.gpsimd.tensor_tensor(
                        acc, acc, beta_sb[:].unsqueeze(1).broadcast_to(wide),
                        ALU.add).then_inc(result_step, 1)
                    pool.wait_ge(result_step, o.l1 * 2 + 2)
                    nc.gpsimd.tensor_tensor(result, x3, acc, ALU.add).then_inc(out_ready, 1)

        @block.scalar
        def _(act):
            copy, activation = nc.scalar.copy, nc.scalar.activation
            act.wait_ge(consts, 1)
            copy(eg[:], minus_half[:]).then_inc(score_done, 2)

            def weights_hi_parts():
                act.wait_ge(weights_in, 16 * N_WEIGHTS)
                copy(wqkv1_hi[:, 0:2, :].rearrange("p a n -> p (a n)"),
                     stage_qk1).then_inc(weights_hi, 1)
                copy(wqkv1_hi[:, 2, :], stage_v1).then_inc(weights_hi, 1)
                copy(w1_hi[:], stage_w1).then_inc(weights_hi, 1)

            def exp_tables():
                nc.scalar.preload_act_table_set("natural_log_exp_and_others")

            def hi_part(o, which, p):
                w = work_wait(act, o, f"{which}{p}")
                dst = {"q": qa1, "k": ka1}[which]
                for j in range(2):
                    last = copy(dst[0:D1, 2 * (p % 2) + j, :], w[j * D1:(j + 1) * D1, :])
                last.then_inc(qk1_hi, 1)

            def hi_q_again(s, p):
                act.wait_ge(qk1_hi, s * 2 * PAIRS + (2 * p + 2))
                for j in range(2):
                    slot = 2 * (p % 2) + j
                    copy(qb1[0:D1, slot, :], qa1[0:D1, slot, :])

            def max_rows(o, p):
                w = work_wait(act, o, f"mT{p}")
                for j in range(2):
                    last = copy(qb1[D1:D1 + 4, 2 * (p % 2) + j, :], w[D1:D1 + 4, :])
                last.then_inc(free_of(o, f"mT{p}"), 1)

            def inverse_sums(o, p):
                act.wait_ge(out_full[1], sums_no(o, p))
                act.wait_ge(out_free[0], out0(o, p))
                activation(rsum1[:], outs[:, 1, :], ACT.Ln).then_inc(out_free[1], 1)
                act.wait_ge(out_free[1], sums_no(o, p) + 1)
                activation(rsum1[:], rsum1[:], ACT.Exp, scale=-1.0).then_inc(rsum1_ready, 1)

            def attention1_head(o):
                w = work_wait(act, o, "x2T")
                copy(x2_hi[:], w).then_inc(x_hi, 1)
                hi_part(o, "q", 0)
                hi_part(o, "k", 0)
                hi_q_again(o.f0, 0)
                for t in range(TILES):
                    for n in range(2):
                        w = work_wait(act, o, f"v{t}_{n}")
                        copy(v1[:, t, n * SEQ:(n + 1) * SEQ],
                             w).then_inc(free_of(o, f"v{t}_{n}"), 1)
                        if (t, n) == (1, 1):
                            hi_part(o, "q", 1)
                        if (t, n) == (2, 0):
                            hi_part(o, "k", 1)
                        if (t, n) == (2, 1):
                            max_rows(o, 0)
                        if (t, n) == (3, 0):
                            hi_q_again(o.f0, 1)

            def pair_step(o, p):
                for j in range(2):
                    activation(prob1_main(p, j), unit_wait(act, o, "pair", p, j), ACT.Exp,
                               scale=SCALE1).then_inc(score_done, 1)
                activation(prob1_rest(p), unit_wait(act, o, "pair", p, 2)[:, 0:512], ACT.Exp,
                           scale=SCALE1).then_inc(score_done, 1)
                if p + 1 < PAIRS:
                    max_rows(o, p + 1)
                if p + 2 < PAIRS:
                    hi_part(o, "q", p + 2)
                    hi_part(o, "k", p + 2)
                if p >= 1:
                    inverse_sums(o, p - 1)
                if p + 2 < PAIRS:
                    hi_q_again(o.l1, p + 2)

            def attention0_head(o, p):
                if p == 2:
                    for i in range(2):
                        w = work_wait(act, o, f"xT0_{i}")
                        half = slice(i * 2 * P, (i + 1) * 2 * P)
                        copy(xT_a[:, half], w[:, 0:2 * P]).then_inc(free_of(o, f"xT0_{i}"), 1)
                if p in (3, 4):
                    for t in (2 * p - 6, 2 * p - 5):
                        w = work_wait(act, o, f"qkv0_{t}")
                        copy(qk_sb[:].rearrange("p (w t n) -> p w t n", w=2, t=TILES)[:, :, t, :],
                             w[:, 0:2 * DIM].rearrange("p (w n) -> p w n", w=2))
                        copy(vstat[:, t, :, 0:D0],
                             w[:, 2 * DIM:3 * DIM].rearrange("p (h d) -> p h d", d=D0)
                             ).then_inc(free_of(o, f"qkv0_{t}"), 1)
                if p == 6:
                    act.wait_ge(sumsq_ready, o.a0 + 1)
                    activation(newton, sum_sq, ACT.Ln).then_inc(ln_done, 1)
                    act.wait_ge(ln_done, o.a0 + 1)
                    activation(inv_norm[:], newton, ACT.Exp, scale=-0.5).then_inc(invn_ready, 1)

            def experts0(o, p):
                if p == 3:
                    w = work_wait(act, o, "xtT")
                    copy(xT_b, w).then_inc(free_of(o, "xtT"), 1)

            def hi_parts(o):
                act.wait_ge(qkn_ready, o.a0 + 1)
                n4 = qk_sb[:].rearrange("p (w n d) -> p w n d", w=2, d=D0)
                for w_, sl in ((0, slice(0, 2)), (1, slice(0, 3, 2))):
                    dst = parts[:, w_].rearrange("p t h r d -> p (t h) r d")[:, :, sl, :]
                    last = copy(dst, n4[:, w_].unsqueeze(2).broadcast_to([P, TILES * H0, 2, D0]))
                last.then_inc(parts_hi, 1)

            def hidden_gelu(o, e):
                if e >= 2:
                    act.wait_ge(out_full[0], out0(o, PAIRS + e - 2))
                for h in range(CH1 // 2):
                    w = unit_wait(act, o, "hidden", e, h)
                    for c in range(2):
                        ch = e * CH1 + 2 * h + c
                        last = activation(hid1T(e, 2 * h + c), w[:, c * SEQ:(c + 1) * SEQ],
                                          ACT.Gelu, bias=b1_1_sb[:, ch:ch + 1])
                    last.then_inc(score_done, 1)

            def cosine_exp(o, n):
                if n >= PROB0_SLOTS:
                    g, kb = (n - PROB0_SLOTS) // TILES, (n - PROB0_SLOTS) % TILES
                    if kb == TILES - 1:
                        act.wait_ge(out_full[1], group_no(o, g))
                    else:
                        act.wait_ge(pv0_done, (o.a0 * GROUPS0 + g) * (TILES - 1) + (kb + 1))
                for i in range(2):
                    activation(prob0(n)[:, i * 1024:(i + 1) * 1024],
                               unit_wait(act, o, "cosine", n, i),
                               ACT.Exp).then_inc(score_done, 1)

            act.wait_ge(vstat_ready, 1)
            for o in passes(act):
                exp_tables()
                for p in range(PAIRS):
                    if o.l1 is not None:
                        pair_step(o, p)
                    if o.a0 is not None:
                        attention0_head(o, p)
                    if o.f0 is not None:
                        experts0(o, p)
                    if o.first and p == 6:
                        weights_hi_parts()
                if o.a0 is not None:
                    hi_parts(o)
                if o.f0 is not None:
                    for c in range(CH0):
                        w = work_wait(act, o, f"hid0_{c}")
                        activation(hid0T[:, c, :], w, ACT.Gelu,
                                   bias=bias0[:, c:c + 1]).then_inc(free_of(o, f"hid0_{c}"), 1)
                    exp_tables()
                if o.l1 is not None:
                    inverse_sums(o, PAIRS - 1)
                if o.a0 is not None:
                    for n in range(2):
                        cosine_exp(o, n)
                if o.l1 is not None:
                    w = work_wait(act, o, "xnT")
                    copy(xn_hi[:], w).then_inc(x_hi, 1)
                if o.a0 is not None:
                    for n in range(2, TILES):
                        cosine_exp(o, n)
                if o.l1 is not None:
                    act.wait_ge(gap_ready, o.l1 + 1)
                    activation(eg[:], gap[:], ACT.Exp).then_inc(eg_ready, 1)
                for k in range(GROUPS0):
                    if o.l1 is not None:
                        hidden_gelu(o, 2 * k)
                        hidden_gelu(o, 2 * k + 1)
                    if o.a0 is not None and k + 1 < GROUPS0:
                        if o.l1 is not None:
                            exp_tables()
                        for m in range(TILES):
                            cosine_exp(o, TILES * (k + 1) + m)
                if o.f0 is not None:
                    attention1_head(o)
                if o.first:
                    act.wait_ge(weights_ready, 1)

        @block.vector
        def _(dve):
            v = nc.vector
            v.memset(vstat[:], 0.0).then_inc(dve_step, 1)
            dve.wait_ge(dve_step, 1)
            v.memset(vstat[:, :, :, D0:D0 + 1], 1.0).then_inc(vstat_ready, 1)
            dve.wait_ge(consts, 1)
            v.tensor_copy(ident_b[:], ident_f).then_inc(work_free[0], 1)
            v.tensor_copy(ident_r[:], ident_f).then_inc(work_free[1], 1)
            v.tensor_copy(mask_qk[:], mask_f[:, 0, :]).then_inc(out_free[0], 1)
            v.tensor_copy(mask_kq[:], mask_f[:, 1, :]).then_inc(out_free[1], 1)
            dve.wait_ge(first_in, 16 * 2)

            def weights_folded():
                dve.wait_ge(weights_in, 16 * N_WEIGHTS)
                v.tensor_tensor(w1s0[:].rearrange("p (e h) -> p e h", h=HID0),
                                w1raw0.rearrange("p (e h) -> p e h", h=HID0),
                                s0_sb[:].unsqueeze(2).broadcast_to([P, EXPERTS, HID0]), ALU.mult)
                v.tensor_copy(wg1_hi[:], wg1_sb[:]).then_inc(wg1_ready, 1)
                dve.wait_ge(wg1_ready, 1)
                v.tensor_tensor(wg1_lo[:], wg1_sb[:], wg1_hi[:].bitcast(F32), ALU.subtract)
                dve.wait_ge(fold_ready, 1)
                for c in range(CH0):
                    for j in range(P // HID0):
                        e = c * (P // HID0) + j
                        rows = slice(j * HID0, (j + 1) * HID0)
                        v.tensor_tensor(bias0[rows, c:c + 1],
                                        outs[rows, 0, c * 8 + e:c * 8 + e + 1],
                                        b1_0_sb[rows, c:c + 1], ALU.add)
                dve.wait_ge(weights_hi, 2)
                hi = wqkv1_hi[:].bitcast(F32)
                v.tensor_tensor(wqkv1_lo[:, 0:2, :].rearrange("p a n -> p (a n)"), stage_qk1,
                                hi[:, 0:2, :].rearrange("p a n -> p (a n)"), ALU.subtract)
                v.tensor_tensor(wqkv1_lo[:, 2, :], stage_v1, hi[:, 2, :], ALU.subtract)

            def weights_lo_parts():
                dve.wait_ge(weights_hi, 3)
                v.tensor_tensor(w1_lo[:], stage_w1, w1_hi[:].bitcast(F32),
                                ALU.subtract).then_inc(weights_ready, 1)
                dve.wait_ge(weights_ready, 1)

            links = [1, 0]

            def link(ins):
                links[1] += 1
                ins.then_inc(dve_step, 1)
                dve.wait_ge(dve_step, links[0] + links[1])

            def variances(stream, src):
                for t in range(TILES):
                    last = v.bn_stats(stats[:, t, :], src[:, t, :])
                link(last)
                v.tensor_tensor(mean[:], stats[:, :, 1], stats[:, :, 4], ALU.add)
                v.tensor_tensor(var_eps[:], stats[:, :, 2], stats[:, :, 5], ALU.add)
                link(v.tensor_tensor(halves[:], stats[:, :, 1], stats[:, :, 4], ALU.subtract))
                v.tensor_scalar(mean[:], mean[:], 0.5, None, ALU.mult)
                link(v.tensor_tensor(halves[:], halves[:], halves[:], ALU.mult))
                link(v.scalar_tensor_tensor(var_eps[:], halves[:], DIM / 4.0, var_eps[:],
                                            ALU.mult, ALU.add))
                v.tensor_scalar(var_eps[:], var_eps[:], 1.0 / DIM, LN_EPS, ALU.mult,
                                ALU.add).then_inc(var_ready[stream], 1)

            def standardize(stream, n, src, dst):
                dve.wait_ge(rstd_ready[stream], n + 1)
                for t in range(TILES):
                    last = v.tensor_scalar(dst[:, t, :], src[:, t, :], mean[:, t:t + 1],
                                           rstd[:, t:t + 1], ALU.subtract, ALU.mult)
                return last

            wide = [P, TILES, EXPERTS]

            def first_best(logits, onehot, value):
                link(v.tensor_reduce(value[:], logits[:], AX.X, ALU.max))
                link(v.tensor_tensor(eq[:], logits[:], value[:].unsqueeze(2).broadcast_to(wide),
                                     ALU.is_equal))
                link(v.tensor_tensor(eq[:], eq[:], rank[:].unsqueeze(1).broadcast_to(wide),
                                     ALU.mult))
                link(v.tensor_reduce(best[:], eq[:], AX.X, ALU.max))
                return v.tensor_tensor(onehot[:], rank[:].unsqueeze(1).broadcast_to(wide),
                                       best[:].unsqueeze(2).broadcast_to(wide), ALU.is_equal)

            def flat_rows(a):
                return a[:, :, :].rearrange("p t d -> p (t d)")

            def lo_rows(o, name, n, hi, lo):
                w = work_wait(dve, o, name)
                dve.wait_ge(x_hi, n)
                v.tensor_tensor(lo[:], w, hi[:].bitcast(F32),
                                ALU.subtract).then_inc(free_of(o, name), 1)

            def lo_q(o, s, p):
                w = work_bank(o, f"q{p}")
                dve.wait_ge(qk1_hi, s * 2 * PAIRS + (2 * p + 1))
                for j in range(2):
                    slot = 2 * (p % 2) + j
                    last = v.tensor_tensor(qa1[D1:2 * D1, slot, :], w[j * D1:(j + 1) * D1, :],
                                           qa1[0:D1, slot, :].bitcast(F32), ALU.subtract)
                last.then_inc(free_of(o, f"q{p}"), 1)

            def lo_k(o, s, p):
                w = work_bank(o, f"k{p}")
                dve.wait_ge(qk1_hi, s * 2 * PAIRS + (2 * p + 2))
                for j in range(2):
                    slot = 2 * (p % 2) + j
                    last = v.tensor_tensor(kb1[0:D1, slot, :], w[j * D1:(j + 1) * D1, :],
                                           ka1[0:D1, slot, :].bitcast(F32), ALU.subtract)
                last.then_inc(free_of(o, f"k{p}"), 1)

            def maxima(o, p, j):
                w = work_wait(dve, o, f"mx{p}_{2 * j}")
                v.tensor_reduce(neg_max[:, 0, j:j + 1], w[:, 0:P], AX.X, ALU.max, negate=True)
                v.tensor_reduce(neg_max[:, 2, j:j + 1], w[:, P:4 * P], AX.X, ALU.max,
                                negate=True).then_inc(free_of(o, f"mx{p}_{2 * j}"), 1)
                w = work_wait(dve, o, f"mx{p}_{2 * j + 1}")
                v.tensor_reduce(neg_max[:, 3, j:j + 1], w, AX.X, ALU.max,
                                negate=True).then_inc(free_of(o, f"mx{p}_{2 * j + 1}"), 1)

            def maxima_parts(o, p):
                w = work_wait(dve, o, f"mx{p}_4")
                v.tensor_reduce(neg_max[:, 1, :], w.rearrange("p (j n) -> p j n", j=2), AX.X,
                                ALU.max, negate=True).then_inc(free_of(o, f"mx{p}_4"), 1)
                for i in (3, 4):
                    work_moved(dve, o, f"mx{p}_{i}")
                link(v.tensor_copy(neg_max_hl[:, :, 0:2], neg_max[:]))
                v.tensor_tensor(neg_max_hl[:, :, 2:4], neg_max[:], neg_max_hl[:, :, 0:2],
                                ALU.subtract).then_inc(negmax_ready, 1)

            def normalize(o, p):
                dve.wait_ge(out_full[0], out0(o, p))
                dve.wait_ge(rsum1_ready, o.l1 * PAIRS + (p + 1))
                v.tensor_tensor(yT[:, p, :], outs[:, 0, :], rsum1[:],
                                ALU.mult).then_inc(out_free[0], 1)

            def attention1_head(o):
                lo_rows(o, "x2T", o.f0 * 2 + 1, x2_hi, x2_lo)

            def pair_step(o, p):
                if p == 2:
                    dve.wait_ge(out_sent, o.l1 * 16 + 16)
                if p >= 2:
                    normalize(o, p - 2)
                if p + 1 < PAIRS:
                    maxima(o, p + 1, 0)
                    maxima(o, p + 1, 1)
                    maxima_parts(o, p + 1)

            def next_operands(o, p):
                if p + 2 < PAIRS:
                    lo_q(o, o.l1, p + 2)
                    lo_k(o, o.l1, p + 2)

            def attention0_head(o, p):
                if p == 0:
                    dve.wait_ge(x_loaded, o.a0 * 16 + 16)
                    variances("a0", x_in)
                if p == 1:
                    standardize("a0", o.a0, x_in, rows_b).then_inc(rows_ready["a0"], 1)
                if p == 4:
                    if o.f0 is not None:
                        work_wait(dve, o, "xtT")
                        dve.wait_ge(rows_ready["f0"], o.f0 * 3 + 2)
                if p in (4, 5):
                    q4 = qk_sb[:].rearrange("p (w t n) -> p w t n", w=2, t=TILES)
                    s4 = sum_sq.rearrange("p (w t h) -> p w t h", w=2, t=TILES)
                    for t in (2 * p - 8, 2 * p - 7):
                        work_moved(dve, o, f"qkv0_{t}")
                    for t in (2 * p - 8, 2 * p - 7):
                        link(v.tensor_tensor(sq_tile.rearrange("p (w n) -> p w n", w=2),
                                             q4[:, :, t, :], q4[:, :, t, :], ALU.mult))
                        link(v.tensor_reduce(
                            s4[:, :, t, :], sq_tile.rearrange("p (w h d) -> p w h d", w=2, d=D0),
                            AX.X, ALU.add))
                if p == 5:
                    v.tensor_scalar(sum_sq, sum_sq, L2_EPS ** 2, None,
                                    ALU.max).then_inc(sumsq_ready, 1)
                if p == 6:
                    dve.wait_ge(invn_ready, o.a0 + 1)
                    link(v.tensor_tensor(newton, inv_norm[:], inv_norm[:], ALU.mult))
                    link(v.tensor_tensor(newton, newton, sum_sq, ALU.mult))
                    link(v.tensor_scalar(newton, newton, -0.5, 1.5, ALU.mult, ALU.add))
                    link(v.tensor_tensor(inv_norm[:], inv_norm[:], newton, ALU.mult))
                    link(v.tensor_scalar(inv_norm[:, 0:TILES * H0], inv_norm[:, 0:TILES * H0],
                                         g_sb[:, 0:1], None, ALU.mult))
                    qk3 = qk_sb[:].rearrange("p (n d) -> p n d", d=D0)
                    v.tensor_tensor(qk3, qk3, inv_norm[:].unsqueeze(2).broadcast_to(
                        [P, N_LEN, D0]), ALU.mult).then_inc(qkn_ready, 1)

            def experts0(o, p):
                if p == 1:
                    variances("f0", res0)
                if p == 2:
                    standardize("f0", o.f0 * 3, res0, rows_a).then_inc(rows_ready["f0"], 1)
                    dve.wait_ge(rows_ready["f0"], o.f0 * 3 + 1)
                    variances("f0", rows_a)
                if p == 3:
                    if o.a0 is not None:
                        work_wait(dve, o, "xT0_1")
                    standardize("f0", o.f0 * 3 + 1, rows_a, rows_b).then_inc(rows_ready["f0"], 1)
                if p == 5:
                    work_moved(dve, o, "lg0")
                    link(first_best(lg, oh1, top1))
                    v.tensor_copy(ohx, oh1[:].unsqueeze(3).broadcast_to(
                        [P, TILES, EXPERTS, HID0])).then_inc(onehot_ready, 1)

            def experts0_moved(o):
                w = work_wait(dve, o, "lg0")
                v.tensor_copy(lg[:], w[:, 0:TILES * EXPERTS].rearrange(
                    "p (t e) -> p t e", e=EXPERTS)).then_inc(free_of(o, "lg0"), 1)
                w = work_wait(dve, o, "xh2T")
                v.tensor_copy(xT_a[:], w).then_inc(free_of(o, "xh2T"), 1)

            def lo_parts(o):
                dve.wait_ge(qkn_ready, o.a0 + 1)
                dve.wait_ge(parts_hi, o.a0 + 1)
                n4 = qk_sb[:].rearrange("p (w n d) -> p w n d", w=2, d=D0)
                for w_, sl in ((0, slice(2, 4)), (1, slice(1, 4, 2))):
                    hl = parts[:, w_].rearrange("p t h r d -> p (t h) r d")
                    four = [P, TILES * H0, 2, D0]
                    last = v.tensor_tensor(
                        hl[:, :, sl, :], n4[:, w_].unsqueeze(2).broadcast_to(four),
                        hl[:, :, 0, :].bitcast(F32).unsqueeze(2).broadcast_to(four), ALU.subtract)
                last.then_inc(parts_ready, 1)

            def group_operands(o, g):
                for w_, name in enumerate((f"qT{g}", f"kT{g}")):
                    w = work_wait(dve, o, name)
                    v.tensor_copy(qkT0[:, w_, g, :], w).then_inc(free_of(o, name), 1)

            def group_out(o, g):
                dve.wait_ge(out_full[1], group_no(o, g))
                v.tensor_copy(oT_sb[:], outs[:, 1, :]).then_inc(out_free[1], 1)

            def group_rows(o, g):
                w = work_wait(dve, o, f"oT{g}").rearrange("p (n s) -> p n s", s=STRIP)
                link(v.reciprocal(rsum0[:], w[:, :, D0]))
                v.tensor_tensor(
                    attn0[:, :, g * HG * D0:(g + 1) * HG * D0].rearrange(
                        "p t (h d) -> p t h d", d=D0),
                    w[:, :, 0:D0].rearrange("p (t h) d -> p t h d", h=HG),
                    rsum0[:].rearrange("p (t h) -> p t h", h=HG).unsqueeze(3).broadcast_to(
                        [P, TILES, HG, D0]), ALU.mult).then_inc(free_of(o, f"oT{g}"), 1)

            def routing1(o):
                w = work_wait(dve, o, "lg1")
                v.tensor_tensor(lg[:], w[:, 0:TILES * EXPERTS].rearrange("p (t e) -> p t e",
                                                                        e=EXPERTS),
                                bg1_sb[:].unsqueeze(1).broadcast_to(wide),
                                ALU.add).then_inc(free_of(o, "lg1"), 1)
                work_moved(dve, o, "lg1")
                link(first_best(lg, oh1, top1))
                link(v.scalar_tensor_tensor(lg2[:], oh1[:], -3e38, lg[:], ALU.mult, ALU.add))
                link(first_best(lg2, oh2, top2))
                v.tensor_tensor(gap[:], top2[:], top1[:], ALU.subtract).then_inc(gap_ready, 1)

            def combine1(o):
                dve.wait_ge(eg_ready, o.l1 + 1)
                link(v.tensor_scalar(sc2[:], eg[:], 1.0, None, ALU.add))
                link(v.reciprocal(sc1[:], sc2[:]))
                link(v.tensor_tensor(sc2[:], eg[:], sc1[:], ALU.mult))
                v.tensor_tensor(oh1[:], oh1[:], sc1[:].unsqueeze(2).broadcast_to(wide), ALU.mult)
                link(v.tensor_tensor(oh2[:], oh2[:], sc2[:].unsqueeze(2).broadcast_to(wide),
                                     ALU.mult))
                v.tensor_tensor(comb[:], oh1[:], oh2[:], ALU.add).then_inc(comb_ready, 1)
                w = work_wait(dve, o, "cT")
                v.tensor_copy(selT1, w[0:EXPERTS, :]).then_inc(free_of(o, "cT"), 1)
                w = work_wait(dve, o, "b2")
                v.tensor_tensor(flat_rows(acc), flat_rows(xn), w,
                                ALU.add).then_inc(free_of(o, "b2"), 1)
                work_moved(dve, o, "b2")

            def accumulate1(o, e):
                dve.wait_ge(out_full[0], out0(o, PAIRS + e))
                for t in range(TILES):
                    last = v.scalar_tensor_tensor(
                        acc[:, t, :], outs[:, 0, t * DIM:(t + 1) * DIM], comb[:, t, e:e + 1],
                        acc[:, t, :], ALU.mult, ALU.add)
                last.then_inc(out_free[0], 1)
                dve.wait_ge(out_free[0], out0(o, PAIRS + e) + 1)

            for o in passes(dve):
                if o.looped:
                    before_loop = links[0]
                    links[0] = before_loop + o.l1 * LOOP_LINKS
                l1, f0, a0 = o.l1 is not None, o.f0 is not None, o.a0 is not None
                for p in range(PAIRS):
                    if l1:
                        pair_step(o, p)
                    if a0:
                        attention0_head(o, p - 1)
                    if f0:
                        experts0(o, p - 1)
                    if l1:
                        next_operands(o, p)
                    if f0 and p == 4:
                        experts0_moved(o)
                if l1:
                    normalize(o, PAIRS - 2)
                if a0:
                    lo_parts(o)
                if f0:
                    w = work_wait(dve, o, "ohT")
                    v.tensor_copy(selT0, w[0:EXPERTS, :]).then_inc(free_of(o, "ohT"), 1)
                if a0:
                    group_operands(o, 0)
                if l1:
                    normalize(o, PAIRS - 1)
                    w = work_wait(dve, o, "proj")
                    v.tensor_tensor(flat_rows(x3), flat_rows(res1), w,
                                    ALU.add).then_inc(free_of(o, "proj"), 1)
                    work_moved(dve, o, "proj")
                    variances("l1", x3)
                if f0:
                    for c in range(CH0):
                        work_moved(dve, o, f"hid0_{c}")
                        w = work_wait(dve, o, f"mask{c}")
                        v.tensor_tensor(hid0T[:, c, :], hid0T[:, c, :], w,
                                        ALU.mult).then_inc(free_of(o, f"mask{c}"), 1)
                if l1:
                    standardize("l1", o.l1 * 2, x3, xn).then_inc(rows_ready["l1"], 1)
                if f0:
                    for i in range(2):
                        w = work_wait(dve, o, f"y0_{i}")
                        half = slice(2 * i * P, 2 * (i + 1) * P)
                        v.tensor_tensor(flat_rows(res1)[:, half], flat_rows(res0)[:, half],
                                        w[:, 0:2 * P], ALU.add).then_inc(free_of(o, f"y0_{i}"), 1)
                if l1:
                    lo_rows(o, "xnT", o.l1 * 2 + 2, xn_hi, xn_lo)
                if o.first:
                    weights_folded()
                if a0:
                    group_operands(o, 1)
                if o.first:
                    weights_lo_parts()
                if l1:
                    routing1(o)
                    combine1(o)
                for k in range(GROUPS0):
                    if a0:
                        group_out(o, k)
                    if l1 and k + 1 < GROUPS0:
                        accumulate1(o, 2 * k)
                    if a0:
                        group_rows(o, k)
                    if a0 and k + 2 < GROUPS0:
                        group_operands(o, k + 2)
                    if f0 and k == 1:
                        for i in range(2):
                            work_moved(dve, o, f"y0_{i}")
                        variances("f0", res1)
                    if f0 and k == 2:
                        standardize("f0", o.f0 * 3 + 2, res1, rows_a).then_inc(
                            rows_ready["f0"], 1)
                    if l1 and k + 1 < GROUPS0:
                        accumulate1(o, 2 * k + 1)
                if a0:
                    for g in range(GROUPS0 - 2, GROUPS0):
                        work_moved(dve, o, f"oT{g}")
                    v.tensor_tensor(res0[:], x_in[:], attn0, ALU.add).then_inc(x_taken, 1)
                    dve.wait_ge(x_taken, o.a0 + 1)
                if f0:
                    attention1_head(o)
                if l1:
                    accumulate1(o, EXPERTS - 2)
                if f0:
                    lo_q(o, o.f0, 0)
                    lo_k(o, o.f0, 0)
                if l1:
                    accumulate1(o, EXPERTS - 1)
                if f0:
                    maxima(o, 0, 0)
                    maxima(o, 0, 1)
                    lo_q(o, o.f0, 1)
                    maxima_parts(o, 0)
                    lo_k(o, o.f0, 1)
                if l1:
                    variances("l1", acc)
                    standardize("l1", o.l1 * 2 + 1, acc, acc).then_inc(rows_ready["l1"], 1)
                if o.looped:
                    assert links[1] == LOOP_LINKS, links[1]
                    links[0] = before_loop + (BATCH - SKEW) * LOOP_LINKS
                else:
                    links[0] += links[1]
                links[1] = 0

        @block.tensor
        def _(pe):
            mm = nc.tensor.matmul
            pe.wait_ge(first_in, 16 * 2)

            def fold_bias():
                pe.wait_ge(weights_in, 16 * N_WEIGHTS)
                for c in range(CH0):
                    last = mm(outs[:, 0, c * 8:(c + 1) * 8], w1raw0[:, c * P:(c + 1) * P],
                              bias_ln0_sb[:], start=True, stop=True)
                last.then_inc(fold_ready, 1)

            def mm3(dst, w_hi, w_lo, x_hi_, x_lo_):
                for n, (a, c) in enumerate(((w_hi, x_hi_), (w_hi, x_lo_), (w_lo, x_hi_))):
                    last = mm(dst, a, c, start=(n == 0), stop=(n == 2))
                return last

            def transposes(o, name, rows, tiles=range(TILES)):
                w = work_open(pe, o, name)
                for i, t in enumerate(tiles):
                    last = nc.tensor.transpose(w[:, i * P:(i + 1) * P], rows[:, t, :], ident)
                last.then_inc(full_of(o, name), 1)

            def project(o, name, which, p):
                w = work_open(pe, o, name)
                cols = slice(p * P, (p + 1) * P)
                mm3(w, wqkv1_hi[:, which, cols], wqkv1_lo[:, which, cols], x2_hi[:],
                    x2_lo[:]).then_inc(full_of(o, name), 1)

            def query_tile(w, p, j, qt, start):
                slot = 2 * (p % 2) + j
                width = (qt + 1) * P
                mm(w[:, 0:width], qa1[0:D1, slot, qt * P:(qt + 1) * P], ka1[0:D1, slot, 0:width],
                   start=start, stop=False)

            def masked(w, mask, blocks):
                first, step = blocks[0], (blocks[-1] - blocks[0]) or 1
                dst = w.rearrange("p (b n) -> p b n", n=P)[:, first:blocks[-1] + 1:step, :]
                return mm(dst, ident_b[:], mask[:].unsqueeze(1).broadcast_to([P, len(blocks), P]),
                          start=False, stop=True)

            def max_scores(o, s, p, j):
                if j == 0:
                    pe.wait_ge(qk1_hi, s * 2 * PAIRS + (2 * p + 2))
                w = work_open(pe, o, f"mx{p}_{2 * j}")
                query_tile(w, p, j, 0, True)
                query_tile(w[:, P:], p, j, 2, False)
                masked(w, mask_qk, (0, 3)).then_inc(full_of(o, f"mx{p}_{2 * j}"), 1)
                w = work_open(pe, o, f"mx{p}_{2 * j + 1}")
                query_tile(w, p, j, 3, True)
                masked(w, mask_qk, (3,)).then_inc(full_of(o, f"mx{p}_{2 * j + 1}"), 1)

            def max_scores_rest(o, p):
                w = work_open(pe, o, f"mx{p}_4")
                query_tile(w, p, 0, 1, True)
                query_tile(w[:, 2 * P:], p, 1, 1, False)
                masked(w, mask_qk, (1, 3)).then_inc(full_of(o, f"mx{p}_4"), 1)

            def max_transposed(o, s, p):
                pe.wait_ge(negmax_ready, s * PAIRS + (p + 1))
                w = work_open(pe, o, f"mT{p}")
                for qt in range(TILES):
                    last = mm(w[D1:D1 + 4, qt * P:(qt + 1) * P], neg_max_hl[:, qt, :],
                              ident_b[:], start=True, stop=True)
                last.then_inc(full_of(o, f"mT{p}"), 1)

            def key_block(dst, p, j, kb, start):
                slot = 2 * (p % 2) + j
                keys, queries = slice(kb * P, (kb + 1) * P), slice(kb * P, SEQ)
                mm(dst, ka1[:, slot, keys], qa1[:, slot, queries], start=start, stop=False)
                mm(dst, kb1[0:D1 + 4, slot, keys], qb1[0:D1 + 4, slot, queries], start=False,
                   stop=False)

            def main_unit(o, p, j):
                d = unit_open(pe, o, "pair", p, j)
                key_block(d[:, 0:4 * P], p, j, 0, True)
                masked(d[:, 0:4 * P], mask_kq, (0,))
                key_block(d[:, 4 * P:7 * P], p, j, 1, True)
                key_block(d[:, 7 * P:8 * P], p, j, 3, False)
                masked(d[:, 4 * P:8 * P], mask_kq, (0, 3)).then_inc(score_full, 1)

            def rest_unit(o, p):
                d = unit_open(pe, o, "pair", p, 2)
                key_block(d[:, 0:2 * P], p, 0, 2, True)
                key_block(d[:, 2 * P:4 * P], p, 1, 2, False)
                masked(d[:, 0:4 * P], mask_kq, (0, 2)).then_inc(score_full, 1)

            def values1(o, p, kbs):
                if 0 in kbs:
                    pe.wait_ge(out_free[0], out0(o, p))
                    unit_done(pe, o, "pair", p, 2)
                for kb in kbs:
                    for j in range(2):
                        h = 2 * p + j
                        probs = {0: prob1_main(p, j)[:, 0:4 * P],
                                 1: prob1_main(p, j)[:, 4 * P:7 * P],
                                 2: prob1_rest(p)[:, 2 * P * j:2 * P * (j + 1)],
                                 3: prob1_main(p, j)[:, 7 * P:8 * P]}[kb]
                        last = mm(outs[D1 * j:D1 * (j + 1), 0, kb * P:],
                                  v1[:, kb, h * D1:(h + 1) * D1], probs, start=(kb == 0),
                                  stop=(kb == TILES - 1))
                if TILES - 1 in kbs:
                    last.then_inc(out_full[0], 1)

            def sums1(o, p):
                pe.wait_ge(out_free[1], sums_no(o, p))
                pe.wait_ge(tsum_ready, o.l1 * (2 * PAIRS) + 2 * (p + 1))
                for j in range(2):
                    mm(outs[D1 * j:D1 * (j + 1), 1, 0:P], ones[:], prob1_main(p, j)[:, 0:P],
                       start=True, stop=True)
                for j in range(2):
                    last = mm(outs[D1 * j:D1 * (j + 1), 1, P:], ones[:], tsum(j), start=True,
                              stop=True)
                last.then_inc(out_full[1], 1)

            def values1_rows(o, *parts_):
                for t, n in parts_:
                    cols = slice(t * P, (t + 1) * P)
                    w = work_open(pe, o, f"v{t}_{n}")
                    half = slice(n * SEQ, (n + 1) * SEQ)
                    mm3(w, x2_hi[:, cols], x2_lo[:, cols], wqkv1_hi[:, 2, half],
                        wqkv1_lo[:, 2, half]).then_inc(full_of(o, f"v{t}_{n}"), 1)

            def first_maxima(o):
                values1_rows(o, (0, 0), (0, 1))
                max_scores(o, o.f0, 0, 0)
                values1_rows(o, (1, 0), (1, 1))
                max_scores(o, o.f0, 0, 1)
                project(o, "q1", 0, 1)
                values1_rows(o, (2, 0))
                max_scores_rest(o, 0)
                project(o, "k1", 1, 1)
                values1_rows(o, (2, 1))
                max_transposed(o, o.f0, 0)
                values1_rows(o, (3, 0), (3, 1))

            def pair_step(o, p):
                pe.wait_ge(k_twice, o.l1 * PAIRS + (p + 1))
                if p == 0:
                    pe.wait_ge(sel_ready, o.l1 + 1)
                else:
                    work_moved(pe, o, f"mT{p}")
                if p >= 2 and bank_no(o, f"k{p}") != bank_no(o, f"mT{p}"):
                    work_moved(pe, o, f"k{p}")
                main_unit(o, p, 0)
                if p + 1 < PAIRS:
                    max_scores(o, o.l1, p + 1, 0)
                main_unit(o, p, 1)
                if p + 1 < PAIRS:
                    max_scores(o, o.l1, p + 1, 1)
                if p >= 1:
                    values1(o, p - 1, (0,))
                if p + 1 < PAIRS:
                    max_scores_rest(o, p + 1)
                if p >= 1:
                    values1(o, p - 1, (1,))
                rest_unit(o, p)
                if p + 1 < PAIRS:
                    max_transposed(o, o.l1, p + 1)
                if p + 2 < PAIRS:
                    project(o, f"q{p + 2}", 0, p + 2)
                if p >= 1:
                    values1(o, p - 1, (2, 3))
                if p + 2 < PAIRS:
                    project(o, f"k{p + 2}", 1, p + 2)
                if p >= 1:
                    sums1(o, p - 1)

            def attention0_head(o, p):
                if p == 2:
                    pe.wait_ge(rows_ready["a0"], o.a0 + 1)
                    for i in range(2):
                        transposes(o, f"xT0_{i}", rows_b, (2 * i, 2 * i + 1))
                if p == 3:
                    for i in range(2):
                        work_moved(pe, o, f"xT0_{i}")
                if p in (3, 4):
                    for t in (2 * p - 6, 2 * p - 5):
                        w = work_open(pe, o, f"qkv0_{t}")
                        mm(w[:, 0:3 * DIM], xT_a[:, t * P:(t + 1) * P], wqkv0_sb[:],
                           start=True, stop=True).then_inc(full_of(o, f"qkv0_{t}"), 1)

            def experts0(o, p):
                if p == 3:
                    pe.wait_ge(rows_ready["f0"], o.f0 * 3 + 1)
                    transposes(o, "xtT", rows_a)
                if p == 4:
                    work_moved(pe, o, "xtT")
                    w = work_open(pe, o, "lg0")
                    for t in range(TILES):
                        last = mm(w[:, t * EXPERTS:(t + 1) * EXPERTS], xT_b[:, t * P:(t + 1) * P],
                                  wg0_sb[:], start=True, stop=True)
                    last.then_inc(full_of(o, "lg0"), 1)
                    pe.wait_ge(rows_ready["f0"], o.f0 * 3 + 2)
                    transposes(o, "xh2T", rows_b)

            def hidden0(o):
                work_moved(pe, o, "xh2T")
                for c in range(CH0):
                    w = work_open(pe, o, f"hid0_{c}")
                    mm(w, w1s0[:, c * P:(c + 1) * P], xT_a[:], start=True,
                       stop=True).then_inc(full_of(o, f"hid0_{c}"), 1)

            def onehot_transposed(o):
                pe.wait_ge(onehot_ready, o.f0 + 1)
                w = work_open(pe, o, "ohT")
                for t in range(TILES):
                    last = mm(w[0:EXPERTS, t * P:(t + 1) * P], ohx[:, t, :, 0], ident_b[:],
                              start=True, stop=True)
                last.then_inc(full_of(o, "ohT"), 1)

            def masks0(o, c):
                w = work_open(pe, o, f"mask{c}")
                for t in range(TILES):
                    rows = ohx[:, t].rearrange("p e h -> p (e h)")[:, c * P:(c + 1) * P]
                    last = mm(w[:, t * P:(t + 1) * P], rows, ident_b[:], start=True, stop=True)
                last.then_inc(full_of(o, f"mask{c}"), 1)

            def experts0_out(o):
                for c in range(CH0):
                    work_moved(pe, o, f"mask{c}")
                for i in range(2):
                    w = work_open(pe, o, f"y0_{i}")
                    for n in range(2):
                        cols = slice((2 * i + n) * P, (2 * i + n + 1) * P)
                        d = w[:, n * P:(n + 1) * P]
                        for c in range(CH0):
                            mm(d, hid0T[:, c, cols], w2_0_sb[:, c, :], start=(c == 0), stop=False)
                        last = mm(d, selT0[:, cols], b2_0_sb[:], start=False, stop=True)
                    last.then_inc(full_of(o, f"y0_{i}"), 1)

            def group_operands(o, g):
                pe.wait_ge(parts_ready, o.a0 + 1)
                for w_, name in enumerate((f"qT{g}", f"kT{g}")):
                    w = work_open(pe, o, name).bitcast(F32R)
                    for t in range(TILES):
                        rows = parts[:, w_, t, g * HG:(g + 1) * HG].rearrange("p h r d -> p (h r d)")
                        last = nc.tensor.transpose(w[:, t * P:(t + 1) * P], rows, ident_r[:])
                    last.then_inc(full_of(o, name), 1)

            def cosines(o, n):
                g, kb = n // TILES, n % TILES
                if kb == 0:
                    work_moved(pe, o, f"qT{g}")
                    work_moved(pe, o, f"kT{g}")
                for pair in range(2):
                    d = unit_open(pe, o, "cosine", n, pair)
                    for i in range(2):
                        j = 2 * pair + i
                        rows = slice(STRIP * j, STRIP * (j + 1))
                        last = mm(d[:, i * SEQ:(i + 1) * SEQ],
                                  qkT0[rows, 1, g, kb * P:(kb + 1) * P], qkT0[rows, 0, g, :],
                                  start=True, stop=True)
                    last.then_inc(score_full, 1)

            def values0(o, n):
                g, kb = n // TILES, n % TILES
                if kb == 0:
                    pe.wait_ge(out_free[1], group_no(o, g))
                unit_done(pe, o, "cosine", n, 1)
                for j in range(HG):
                    last = mm(outs[STRIP * j:STRIP * (j + 1), 1, :],
                              vstat[:, kb, g * HG + j, :], prob0(n)[:, j * SEQ:(j + 1) * SEQ],
                              start=(kb == 0), stop=(kb == TILES - 1))
                last.then_inc(out_full[1] if kb == TILES - 1 else pv0_done, 1)

            def group_rows(o, g):
                pe.wait_ge(out_free[1], group_no(o, g) + 1)
                w = work_open(pe, o, f"oT{g}")
                for t in range(TILES):
                    last = nc.tensor.transpose(w[:, t * P:(t + 1) * P],
                                               oT_sb[:, t * P:(t + 1) * P], ident)
                last.then_inc(full_of(o, f"oT{g}"), 1)

            def hidden1(o, e):
                for h in range(CH1 // 2):
                    d = unit_open(pe, o, "hidden", e, h)
                    for c in range(2):
                        at = e * HID1 + (2 * h + c) * P
                        last = mm3(d[:, c * SEQ:(c + 1) * SEQ], w1_hi[:, at:at + P],
                                   w1_lo[:, at:at + P], xn_hi[:], xn_lo[:])
                    last.then_inc(score_full, 1)

            def experts1_out(o, e, tiles):
                if 0 in tiles:
                    pe.wait_ge(out_free[0], out0(o, PAIRS + e))
                    unit_done(pe, o, "hidden", e, CH1 // 2 - 1)
                for t in tiles:
                    cols = slice(t * P, (t + 1) * P)
                    for c in range(CH1):
                        last = mm(outs[:, 0, cols], hid1T(e, c)[:, cols],
                                  w2_1_sb[:, e * CH1 + c, :], start=(c == 0), stop=(c == CH1 - 1))
                if TILES - 1 in tiles:
                    last.then_inc(out_full[0], 1)

            def combine_transposed(o):
                pe.wait_ge(comb_ready, o.l1 + 1)
                w = work_open(pe, o, "cT")
                for t in range(TILES):
                    last = mm(w[0:EXPERTS, t * P:(t + 1) * P], comb[:, t, :], ident, start=True,
                              stop=True)
                last.then_inc(full_of(o, "cT"), 1)

            def combine_bias(o):
                work_moved(pe, o, "cT")
                w = work_open(pe, o, "b2")
                for t in range(TILES):
                    cols = slice(t * P, (t + 1) * P)
                    last = mm(w[:, cols], selT1[:, cols], b2_1_sb[:], start=True, stop=True)
                last.then_inc(full_of(o, "b2"), 1)

            for o in passes(pe):
                l1, f0, a0 = o.l1 is not None, o.f0 is not None, o.a0 is not None
                for p in range(PAIRS):
                    if l1:
                        pair_step(o, p)
                    if a0:
                        attention0_head(o, p)
                    if f0:
                        experts0(o, p)
                if f0:
                    hidden0(o)
                if l1:
                    values1(o, PAIRS - 1, range(TILES))
                    sums1(o, PAIRS - 1)
                if f0:
                    onehot_transposed(o)
                if a0:
                    group_operands(o, 0)
                if l1:
                    w = work_open(pe, o, "proj")
                    for p in range(PAIRS):
                        if p >= PAIRS - 2:
                            pe.wait_ge(out_free[0], out0(o, p + 1))
                        for t in range(TILES):
                            cols = slice(t * P, (t + 1) * P)
                            last = mm(w[:, cols], yT[:, p, cols], wo_sb[:, p, :],
                                      start=(p == 0 and t == 0),
                                      stop=(p == PAIRS - 1 and t == TILES - 1))
                    last.then_inc(full_of(o, "proj"), 1)
                if f0:
                    masks0(o, 0)
                if o.first:
                    fold_bias()
                if a0:
                    cosines(o, 0)
                if f0:
                    masks0(o, 1)
                if a0:
                    cosines(o, 1)
                    values0(o, 0)
                if f0:
                    experts0_out(o)
                if l1:
                    pe.wait_ge(rows_ready["l1"], o.l1 * 2 + 1)
                    transposes(o, "xnT", xn)
                if a0:
                    cosines(o, 2)
                    group_operands(o, 1)
                    values0(o, 1)
                if l1:
                    work_moved(pe, o, "xnT")
                    w = work_open(pe, o, "lg1")
                    for t in range(TILES):
                        d = w[:, t * EXPERTS:(t + 1) * EXPERTS]
                        cols = slice(t * P, (t + 1) * P)
                        last = mm3(d, xn_hi[:, cols], xn_lo[:, cols], wg1_hi[:], wg1_lo[:])
                    last.then_inc(full_of(o, "lg1"), 1)
                if a0:
                    cosines(o, 3)
                    values0(o, 2)
                if l1 and not a0:
                    hidden1(o, 0)
                    combine_transposed(o)
                    hidden1(o, 1)
                    combine_bias(o)
                    for e in range(2, EXPERTS):
                        experts1_out(o, e - 2, range(TILES))
                        hidden1(o, e)
                for k in range(GROUPS0 - 1) if a0 else ():
                    if l1:
                        hidden1(o, 2 * k)
                        if k == 0:
                            combine_transposed(o)
                    values0(o, TILES * (k + 1) - 1)
                    if l1:
                        hidden1(o, 2 * k + 1)
                        if k == 0:
                            combine_bias(o)
                    for m in range(TILES):
                        n = TILES * (k + 1) + m
                        if l1:
                            experts1_out(o, 2 * k + m // 2, (2 * (m % 2), 2 * (m % 2) + 1))
                        cosines(o, n)
                        if m:
                            values0(o, n - 1)
                        if m == 1:
                            group_rows(o, k)
                        if m == 2 and k + 2 < GROUPS0:
                            group_operands(o, k + 2)
                if l1 and a0:
                    hidden1(o, EXPERTS - 2)
                if a0:
                    values0(o, STEPS0 - 1)
                if l1 and a0:
                    hidden1(o, EXPERTS - 1)
                if a0:
                    group_rows(o, GROUPS0 - 1)
                if f0:
                    pe.wait_ge(rows_ready["f0"], o.f0 * 3 + 3)
                    transposes(o, "x2T", rows_a)
                if l1:
                    experts1_out(o, EXPERTS - 2, range(TILES))
                if f0:
                    work_moved(pe, o, "x2T")
                    project(o, "q0", 0, 0)
                if l1:
                    experts1_out(o, EXPERTS - 1, (0, 1))
                if f0:
                    project(o, "k0", 1, 0)
                if l1:
                    experts1_out(o, EXPERTS - 1, (2, 3))
                if f0:
                    first_maxima(o)
                if o.first:
                    pe.wait_ge(weights_ready, 1)


def kernel(L0_attn_x, L0_attn_Wq, L0_attn_Wk, L0_attn_Wv, L0_attn_g_scale, L0_ffn_Wg,
           L0_ffn_ln_scale, L0_ffn_ln_bias, L0_ffn_W1, L0_ffn_b1, L0_ffn_W2, L0_ffn_b2,
           L1_attn_w_q, L1_attn_w_k, L1_attn_w_v, L1_attn_w_o, L1_ffn_Wg, L1_ffn_bg, L1_ffn_W1,
           L1_ffn_b1, L1_ffn_W2, L1_ffn_b2, L1_ffn_gamma, L1_ffn_beta):
    import concourse.bacc as bacc
    from concourse.bass_utils import run_bass_kernel_spmd

    def rows(a):
        return np.asarray(a).reshape(-1, P, a.shape[-1]).transpose(1, 0, 2)

    def flat(a):
        return np.asarray(a).reshape(-1, DIM).T

    ins = {
        "x": np.asarray(L0_attn_x).reshape(BATCH, TILES, P, DIM).transpose(0, 2, 1, 3),
        "wqkv0": np.concatenate([np.asarray(w).T for w in (L0_attn_Wq, L0_attn_Wk, L0_attn_Wv)], 1),
        "g_scale": np.asarray(L0_attn_g_scale).reshape(1, 1),
        "wg0": np.asarray(L0_ffn_Wg).T,
        "s0": np.asarray(L0_ffn_ln_scale).T,
        "bias_ln0": np.asarray(L0_ffn_ln_bias).T,
        "w1_0": np.asarray(L0_ffn_W1).transpose(1, 0, 2).reshape(DIM, EXPERTS * HID0),
        "b1_0": np.asarray(L0_ffn_b1).reshape(CH0, P).T,
        "w2_0": rows(np.asarray(L0_ffn_W2).reshape(EXPERTS * HID0, DIM)),
        "b2_0": np.asarray(L0_ffn_b2),
        "wq1": flat(L1_attn_w_q),
        "wk1": flat(L1_attn_w_k),
        "wv1": flat(L1_attn_w_v),
        "wo1": rows(np.asarray(L1_attn_w_o)),
        "wg1": np.asarray(L1_ffn_Wg),
        "bg1": np.asarray(L1_ffn_bg).reshape(1, EXPERTS),
        "w1_1": np.asarray(L1_ffn_W1).transpose(1, 0, 2).reshape(DIM, EXPERTS * HID1),
        "b1_1": np.asarray(L1_ffn_b1).reshape(EXPERTS * CH1, P).T,
        "w2_1": rows(np.asarray(L1_ffn_W2).reshape(EXPERTS * HID1, DIM)),
        "b2_1": np.asarray(L1_ffn_b2),
        "gamma": np.asarray(L1_ffn_gamma).reshape(1, DIM),
        "beta": np.asarray(L1_ffn_beta).reshape(1, DIM),
    }
    ins = {name: np.ascontiguousarray(a) for name, a in ins.items()}
    nc = bacc.Bacc("TRN2", target_bir_lowering=False, num_devices=1)
    drams = [nc.dram_tensor(f"in_{name}", a.shape, mybir.dt.from_np(a.dtype),
                            kind="ExternalInput").ap() for name, a in ins.items()]
    out = nc.dram_tensor("out", (BATCH, P, TILES, DIM), F32, kind="ExternalOutput").ap()
    layers_kernel(nc, *drams, out)
    got = run_bass_kernel_spmd(nc, [{f"in_{name}": a for name, a in ins.items()}], core_ids=[0])
    y = got.results[0]["out"]
    return y.transpose(0, 2, 1, 3).reshape(BATCH, SEQ, DIM)
```
